# Optimizing a Trainium2 kernel written in Bass

```python
import numpy as np
import jax
import jax.numpy as jnp

def _softmax(x, axis=-1):
    return jax.nn.softmax(x, axis=axis)

def _gelu(x):
    return jax.nn.gelu(x, approximate=True)

def _silu(x):
    return jax.nn.silu(x)

def _sigmoid(x):
    return jax.nn.sigmoid(x)

def _layernorm(x, axis=-1, eps=1e-05):
    m = jnp.mean(x, axis=axis, keepdims=True)
    v = jnp.var(x, axis=axis, keepdims=True)
    return (x - m) / jnp.sqrt(v + eps)

def _scatter_add(tgt, idx, src, axis=0):
    return tgt.at[idx].add(src)

def _segment_sum(src, seg, n):
    return jax.ops.segment_sum(src, seg, n)
kernel_name = 'mk_audio_tower_d1_tok_audfeat768_r4_3706cc'

def setup_inputs(seed: int=0):
    np.random.seed(seed)
    _w = jnp.asarray

    def _rec_inputs():
        import jax
        import jax.numpy as jnp
        _rk = jax.random.key(seed)
        x = -0.00040386 + 0.999972 * jax.random.normal(jax.random.fold_in(_rk, 1), (4, 750, 192), jnp.float32)
        return x
    x = _rec_inputs()

    def _L0_tok_setup():
        import jax, jax.numpy as jnp
        import numpy as np
        B, L, D = (4, 1024, 192)
        DI = 2 * D
        K = 4
        PAD = (K - 1) // 2
        EPS = 1e-06

        def silu(x):
            return x * jax.nn.sigmoid(x)
        key = jax.random.key(seed)
        ks = jax.random.split(key, 9)
        s_in = 1.0 / np.sqrt(D)
        s_di = 1.0 / np.sqrt(DI)
        return {'x': jax.random.normal(ks[0], (B, L, D), dtype=jnp.float32), 'W_in': jax.random.uniform(ks[1], (DI, D), jnp.float32, -s_in, s_in), 'conv_w': jax.random.uniform(ks[2], (DI, 1, K), jnp.float32, -0.5, 0.5), 'conv_b': jax.random.uniform(ks[3], (DI,), jnp.float32, -0.5, 0.5), 'W_x': jax.random.uniform(ks[4], (DI, DI), jnp.float32, -s_di, s_di), 'W_z': jax.random.uniform(ks[5], (DI, DI), jnp.float32, -s_di, s_di), 'W_out': jax.random.uniform(ks[6], (D, DI), jnp.float32, -s_di, s_di), 'gamma': jnp.ones((D,), jnp.float32), 'beta': jnp.zeros((D,), jnp.float32)}
    _L0_tok_all = _L0_tok_setup()
    _L0_tok_in = {k: v for k, v in _L0_tok_all.items() if k in ('W_in', 'conv_w', 'conv_b', 'W_x', 'W_z', 'W_out', 'gamma', 'beta')}
    del _L0_tok_all

    def _L0_attn_setup():
        import jax, jax.numpy as jnp
        import numpy as np
        import math
        N_HEAD = 12
        key = jax.random.key(seed)
        ks = jax.random.split(key, 5)
        B, T, C = (2, 512, 192)
        return {'x': jax.random.normal(ks[0], (B, T, C), jnp.float32), 'w_attn': jax.random.normal(ks[1], (3 * C, C), jnp.float32) * 0.02, 'b_attn': jax.random.normal(ks[2], (3 * C,), jnp.float32) * 0.02, 'w_proj': jax.random.normal(ks[3], (C, C), jnp.float32) * 0.02, 'b_proj': jax.random.normal(ks[4], (C,), jnp.float32) * 0.02}
    _L0_attn_all = _L0_attn_setup()
    _L0_attn_in = {k: v for k, v in _L0_attn_all.items() if k in ('w_attn', 'b_attn', 'w_proj', 'b_proj')}
    del _L0_attn_all

    def _L0_ffn_setup():
        import jax, jax.numpy as jnp
        import numpy as np
        import math
        B, T, C = (8, 512, 192)
        E = 3
        HD = C // E
        TOPK = 2
        NGLOB = 4

        def _masked_softmax(att, mask):
            att = jnp.where(mask, -jnp.inf, att)
            return jax.nn.softmax(att, axis=-1)
        key = jax.random.key(seed)
        ks = jax.random.split(key, 16)
        s = 0.02
        return {'x': jax.random.normal(ks[0], (B, T, C), jnp.float32), 'Wqk': jax.random.normal(ks[1], (C, 2 * C), jnp.float32) * s, 'bqk': jnp.zeros((2 * C,), jnp.float32), 'Wv': jax.random.normal(ks[2], (E, C, HD), jnp.float32) * s, 'bv': jnp.zeros((E, HD), jnp.float32), 'conv_w': jax.random.normal(ks[3], (HD, 1, 3), jnp.float32) * s, 'conv_b': jnp.zeros((HD,), jnp.float32), 'glob': jax.random.normal(ks[4], (NGLOB, HD), jnp.float32) * 0.02, 'pos_bias': jnp.zeros((64, 64), jnp.float32), 'Wg1': jax.random.normal(ks[5], (C, 32), jnp.float32) * s, 'bg1': jnp.zeros((32,), jnp.float32), 'Wg2': jax.random.normal(ks[6], (32, E), jnp.float32) * s, 'bg2': jnp.zeros((E,), jnp.float32), 'Wp': jax.random.normal(ks[7], (C, C), jnp.float32) * s, 'bp': jnp.zeros((C,), jnp.float32)}
    _L0_ffn_all = _L0_ffn_setup()
    _L0_ffn_in = {k: v for k, v in _L0_ffn_all.items() if k in ('Wqk', 'bqk', 'Wv', 'bv', 'conv_w', 'conv_b', 'glob', 'pos_bias', 'Wg1', 'bg1', 'Wg2', 'bg2', 'Wp', 'bp')}
    del _L0_ffn_all
    return {'x': x, 'L0_tok_W_in': _L0_tok_in['W_in'], 'L0_tok_conv_w': _L0_tok_in['conv_w'], 'L0_tok_conv_b': _L0_tok_in['conv_b'], 'L0_tok_W_x': _L0_tok_in['W_x'], 'L0_tok_W_z': _L0_tok_in['W_z'], 'L0_tok_W_out': _L0_tok_in['W_out'], 'L0_tok_gamma': _L0_tok_in['gamma'], 'L0_tok_beta': _L0_tok_in['beta'], 'L0_attn_w_attn': _L0_attn_in['w_attn'], 'L0_attn_b_attn': _L0_attn_in['b_attn'], 'L0_attn_w_proj': _L0_attn_in['w_proj'], 'L0_attn_b_proj': _L0_attn_in['b_proj'], 'L0_ffn_Wqk': _L0_ffn_in['Wqk'], 'L0_ffn_bqk': _L0_ffn_in['bqk'], 'L0_ffn_Wv': _L0_ffn_in['Wv'], 'L0_ffn_bv': _L0_ffn_in['bv'], 'L0_ffn_conv_w': _L0_ffn_in['conv_w'], 'L0_ffn_conv_b': _L0_ffn_in['conv_b'], 'L0_ffn_glob': _L0_ffn_in['glob'], 'L0_ffn_pos_bias': _L0_ffn_in['pos_bias'], 'L0_ffn_Wg1': _L0_ffn_in['Wg1'], 'L0_ffn_bg1': _L0_ffn_in['bg1'], 'L0_ffn_Wg2': _L0_ffn_in['Wg2'], 'L0_ffn_bg2': _L0_ffn_in['bg2'], 'L0_ffn_Wp': _L0_ffn_in['Wp'], 'L0_ffn_bp': _L0_ffn_in['bp']}

def reference(x, L0_tok_W_in, L0_tok_conv_w, L0_tok_conv_b, L0_tok_W_x, L0_tok_W_z, L0_tok_W_out, L0_tok_gamma, L0_tok_beta, L0_attn_w_attn, L0_attn_b_attn, L0_attn_w_proj, L0_attn_b_proj, L0_ffn_Wqk, L0_ffn_bqk, L0_ffn_Wv, L0_ffn_bv, L0_ffn_conv_w, L0_ffn_conv_b, L0_ffn_glob, L0_ffn_pos_bias, L0_ffn_Wg1, L0_ffn_bg1, L0_ffn_Wg2, L0_ffn_bg2, L0_ffn_Wp, L0_ffn_bp):
    import jax
    import jax.numpy as jnp

    def _L0_tok_ref(x, W_in, conv_w, conv_b, W_x, W_z, W_out, gamma, beta):
        import jax, jax.numpy as jnp
        import numpy as np
        B, L, D = (4, 1024, 192)
        DI = 2 * D
        K = 4
        PAD = (K - 1) // 2
        EPS = 1e-06

        def silu(x):
            return x * jax.nn.sigmoid(x)
        xe = jnp.einsum('bld,ed->ble', x, W_in)
        xc = jax.lax.conv_general_dilated(xe.transpose(0, 2, 1), conv_w, window_strides=(1,), padding=[(PAD, PAD)], feature_group_count=DI, dimension_numbers=('NCH', 'OIH', 'NCH')) + conv_b[None, :, None]
        h = silu(xc.transpose(0, 2, 1))
        xg = silu(jnp.einsum('ble,fe->blf', h, W_x))
        zg = silu(jnp.einsum('ble,fe->blf', h, W_z))
        y = jnp.einsum('blf,df->bld', xg * zg, W_out)
        mean = y.mean(-1, keepdims=True)
        var = jnp.sum((y - mean) ** 2, axis=-1, keepdims=True) / (D - 1)
        std = jnp.sqrt(var)
        return gamma * (y - mean) / (std + EPS) + beta

    def _L0_attn_ref(x, w_attn, b_attn, w_proj, b_proj):
        import jax, jax.numpy as jnp
        import numpy as np
        import math
        N_HEAD = 12
        B, T, C = x.shape
        H = N_HEAD
        D = C // H
        qkv = jnp.einsum('btc,oc->bto', x, w_attn) + b_attn
        q, k, v = jnp.split(qkv, 3, axis=-1)
        q = q.reshape(B, T, H, D).transpose(0, 2, 1, 3)
        k = k.reshape(B, T, H, D).transpose(0, 2, 1, 3)
        v = v.reshape(B, T, H, D).transpose(0, 2, 1, 3)
        att = jnp.einsum('bhqd,bhkd->bhqk', q, k) * (1.0 / math.sqrt(D))
        causal = jnp.tril(jnp.ones((T, T), dtype=bool))
        att = jnp.where(causal, att, jnp.float32(-jnp.inf))
        att = jax.nn.softmax(att, axis=-1)
        y = jnp.einsum('bhqk,bhkd->bhqd', att, v)
        y = y.transpose(0, 2, 1, 3).reshape(B, T, C)
        out = jnp.einsum('btc,oc->bto', y, w_proj) + b_proj
        return out

    def _L0_ffn_ref(x, Wqk, bqk, Wv, bv, conv_w, conv_b, glob, pos_bias, Wg1, bg1, Wg2, bg2, Wp, bp):
        import jax, jax.numpy as jnp
        import numpy as np
        import math
        B, T, C = (8, 512, 192)
        E = 3
        HD = C // E
        TOPK = 2
        NGLOB = 4

        def _masked_softmax(att, mask):
            att = jnp.where(mask, -jnp.inf, att)
            return jax.nn.softmax(att, axis=-1)
        Bx, Tx, Cx = x.shape
        scale = 1.0 / math.sqrt(HD)
        gate = jax.nn.softmax(jax.nn.relu(x @ Wg1 + bg1) @ Wg2 + bg2, axis=-1)
        top_w, top_i = jax.lax.top_k(gate, TOPK)
        top_w = jax.nn.softmax(top_w, axis=-1)
        qk = x @ Wqk + bqk
        q, k = (qk[..., :Cx], qk[..., Cx:])
        q = q.reshape(Bx, Tx, E, HD)
        k = k.reshape(Bx, Tx, E, HD)
        rows = jnp.arange(Tx)[:, None]
        ys = []
        for e in range(E):
            qe = q[:, :, e]
            ke = k[:, :, e]
            ve = x @ Wv[e] + bv[e]
            if e == 0:
                qc = jnp.transpose(qe, (0, 2, 1))
                qc = jax.lax.conv_general_dilated(qc, conv_w, window_strides=(1,), padding=((1, 1),), feature_group_count=HD, dimension_numbers=('NCH', 'OIH', 'NCH'))
                qe = jnp.transpose(qc + conv_b[None, :, None], (0, 2, 1))
            elif e == 1:
                gb = jnp.broadcast_to(glob[None], (Bx, NGLOB, HD))
                ke = jnp.concatenate([ke, gb], axis=1)
                ve = jnp.concatenate([ve, gb], axis=1)
            att = jnp.einsum('btd,bsd->bts', qe, ke) * scale
            if e == 2 and Tx <= 64:
                att = att + pos_bias[:Tx, :Tx][None]
            S = att.shape[-1]
            mask = jnp.arange(S)[None, :] > rows
            att = _masked_softmax(att, mask[None])
            ys.append(jnp.einsum('bts,bsd->btd', att, ve))
        ys = jnp.stack(ys, axis=2)
        w_e = jnp.sum(jax.nn.one_hot(top_i, E, dtype=x.dtype) * top_w[..., None], axis=-2)
        combined = (ys * w_e[..., None]).reshape(Bx, Tx, Cx)
        return combined @ Wp + bp
    h = _L0_tok_ref(x, L0_tok_W_in, L0_tok_conv_w, L0_tok_conv_b, L0_tok_W_x, L0_tok_W_z, L0_tok_W_out, L0_tok_gamma, L0_tok_beta)
    h = h + _L0_attn_ref(_layernorm(h, axis=-1), L0_attn_w_attn, L0_attn_b_attn, L0_attn_w_proj, L0_attn_b_proj)
    h = h + _L0_ffn_ref(_layernorm(h, axis=-1), L0_ffn_Wqk, L0_ffn_bqk, L0_ffn_Wv, L0_ffn_bv, L0_ffn_conv_w, L0_ffn_conv_b, L0_ffn_glob, L0_ffn_pos_bias, L0_ffn_Wg1, L0_ffn_bg1, L0_ffn_Wg2, L0_ffn_bg2, L0_ffn_Wp, L0_ffn_bp)
    return h

_drawn_inputs = setup_inputs


def setup_inputs(seed=0):
    import zlib

    import numpy as np

    out = dict(_drawn_inputs(seed))
    spreads = {'L0_tok_gamma': (1.0, 0.2),
     'L0_tok_beta': (0.0, 0.1),
     'L0_ffn_bqk': (0.0, 0.8),
     'L0_ffn_bv': (0.0, 0.717),
     'L0_ffn_conv_b': (0.0, 0.8),
     'L0_ffn_pos_bias': (0.0, 0.1),
     'L0_ffn_bg1': (0.0, 0.8),
     'L0_ffn_bg2': (0.0, 0.517),
     'L0_ffn_bp': (0.0, 0.1)}
    factors = {'L0_attn_b_attn': 8.0,
     'L0_attn_b_proj': 3.051,
     'L0_ffn_Wqk': 8.0,
     'L0_ffn_Wv': 4.342,
     'L0_ffn_conv_w': 8.0,
     'L0_ffn_Wg1': 8.0,
     'L0_ffn_Wg2': 8.0,
     'L0_ffn_Wp': 4.039}
    for name, (base, spread) in spreads.items():
        noise = np.random.default_rng([zlib.crc32(name.encode()), seed]).standard_normal(out[name].shape)
        drawn = base * np.exp(spread * noise) if base else spread * noise
        out[name] = jnp.asarray(drawn.astype(out[name].dtype))
    for name, factor in factors.items():
        out[name] = (out[name] * factor).astype(out[name].dtype)
    return out
```

```python
from contextlib import ExitStack

import concourse.bass as bass
from concourse import mybir

F32 = mybir.dt.float32
F32R = mybir.dt.float32r
BF16 = mybir.dt.bfloat16
ACT = mybir.ActivationFunctionType
ALU = mybir.AluOpType
AX = mybir.AxisListType

B, T, D = 4, 750, 192
DI = 2 * D
TAPS = 4
P, NT = 125, 6
KH, NK = 96, 2
MI = DI // 128
H, DH = 12, 16
HG, NG = 4, 3
E, HD, GH = 3, 64, 32
VS = 32
SPLIT = 500
C0 = 512 - SPLIT
RING = 3
NEG = -1.0e30
QPARTS = (0, 0, 0, 1, 1, 2)
KPARTS = (0, 1, 2, 0, 1, 0)
STACK = DH * len(QPARTS)
LEAD = 8


def cuts(a, z):
    return [(s, e) for s, e in ((a, min(z, SPLIT)), (max(a, SPLIT), z)) if s < e]


def softmax_order():
    def branch(kind, n_groups, heads):
        s1 = [("s1" + kind, g, i, h) for g in range(n_groups) for i in range(NT) for h in range(heads)]
        out, at = [], 0

        def upto(n):
            nonlocal at
            while at < min(n, len(s1)):
                out.append(s1[at])
                at += 1
                if at % (NT * heads) == 0:
                    out.append(("mt" + kind, at // (NT * heads) - 1, 0, 0))
        upto(NT * heads + (LEAD if n_groups > 1 else 0))
        for g in range(n_groups):
            for j in range(NT):
                out.extend(("s2" + kind, g, j, h) for h in range(heads))
                if j:
                    out.append(("pv" + kind, g, j - 1, 0))
                upto((g + 1) * NT * heads + LEAD * heads // HG + (j + 1) * heads)
            out.append(("pv" + kind, g, NT - 1, 0))
            out.append(("yt" + kind, g, 0, 0))
        return out
    return branch("a", NG, HG), branch("f", E, 1)


ATTN, FFN = softmax_order()
NOT_RING = ("pva", "pvf")


def units():
    u = [(("xt", k), "act") for k in range(NK)]
    u += [(("xe", m), "act") for m in range(MI)]
    u += [((n, m), "act") for m in range(MI) for n in ("xg", "zg")]
    u += [(("y", t), "act") for t in range(NT // 2)]
    u += [(("nt", k), "act") for k in range(NK)]
    u += [(("qk", n), "act") for n in range(2 * NK)]
    u += [(("v", t), "dve") for t in range(NT // 2)]
    eng = {"s1": "dve", "mt": "dve", "s2": "act", "yt": "dve"}
    u += [(s, eng[s[0][:2]]) for s in ATTN if s[0] not in NOT_RING]
    u += [(("ot", k), "act") for k in range(NK)]
    u += [(("p", t), "dve") for t in range(NT // 2)]
    u += [(("n2", k), "act") for k in range(NK)]
    u += [(("fq", n), "act") for n in range(2 * E)]
    u += [(("vg", t), "dve") for t in range(NT // 2)]
    u += [(s, eng[s[0][:2]]) for s in FFN if s[0] not in NOT_RING]
    u += [(("o2", k), "act") for k in range(NK)]
    u += [(("p2", t), "dve") for t in range(NT // 2)]
    return u


UNITS = units()
UNIT_AT = {key: n for n, (key, _) in enumerate(UNITS)}
EMPTIED = {"act": [k for k, e in UNITS if e == "act"], "dve": [k for k, e in UNITS if e == "dve"]}
EMPTY_AT = {k: n for ks in EMPTIED.values() for n, k in enumerate(ks)}
EMPTIER = dict(UNITS)

O_IN = 0
O_QK = O_IN + DI
O_V = O_QK + 2 * D
O_PROJ = O_V + D
O_FQK = O_PROJ + D
O_VG = O_FQK + 2 * E * 128
O_WP = O_VG + D + GH
W96 = O_WP + D
O_X = 0
O_Z = O_X + DI
O_OUT = O_Z + DI
W128 = O_OUT + D
C_CONV = 0
C_QK = C_CONV + MI * (TAPS + 1)
C_FQK = C_QK + 2 * NK
C_FB = C_FQK + 2 * E
C_FC = C_FB + E + 1
COLS = C_FC + 3
R_GAMMA = 0
R_BETA = R_GAMMA + D
R_BV = R_BETA + D
R_BPROJ = R_BV + D
R_BV2 = R_BPROJ + D
R_BG1 = R_BV2 + D
R_BP = R_BG1 + GH
R_WG2 = R_BP + D
R_BG2 = R_WG2 + E * GH
ROWS = R_BG2 + E
N_CONSTS = 4
CONSTS = (-0.5, 0.5, -1.0, D / (D - 1.0), 1e-6, 1e-5)
NSTAT = 2 * NT + 1


class Tally:

    def __init__(self, sem, per, start=0):
        self.sem, self.per, self.start = sem, per, start

    def at(self, b, k):
        return self.sem, b * self.per + (self.start + k)


def audio_tower(nc, x, w96, w128, cols, rows, out):
    with ExitStack() as ctx:
        def sb(name, shape, dt=F32):
            return ctx.enter_context(nc.sbuf_tensor(name, shape, dt))

        def sem(name):
            return ctx.enter_context(nc.semaphore(name))

        def tally(name, per, start=0):
            return Tally(sem(name), per, start)

        W = sb("W", [KH, NK, W96])
        W3 = sb("W3", [128, MI, W128])
        Cc = sb("Cc", [128, COLS])
        R = sb("R", [P, ROWS])
        idf = sb("idf", [128, 128])
        idb = sb("idb", [128, 128], BF16)
        mask_q = sb("mask_q", [P, P + 1], BF16)
        mask_k = sb("mask_k", [P, P + 1], BF16)
        expo = sb("expo", [P, len(CONSTS), NT])
        qb4 = sb("qb4", [KH, NK])
        fb8 = sb("fb8", [128, E + 1])
        xin = sb("xin", [P, NT, D])
        xe = sb("xe", [128, MI, T + TAPS - 1])
        stats = sb("stats", [P, 3, NT, 6])
        mv = sb("mv", [P, 3, NT, 2])
        begun = sb("begun", [P, 3])
        va = sb("va", [P, 3, NT])
        sd = sb("sd", [P, NT])
        sde = sb("sde", [P, NT])
        rs = sb("rs", [P, 3, NT])
        h0 = sb("h0", [P, NT, D])
        h1 = sb("h1", [P, NT, D])
        hn = sb("hn", [P, NT, D])
        nT = sb("nT", [KH, NK, T])
        ks = sb("ks", [STACK + 3, H, T], BF16)
        va_ = sb("vaug", [P, NT, H, VS])
        mx = sb("mx", [P, 2, NT, HG])
        mr = sb("mr", [P, 3, NT, HG])
        m3 = sb("m3", [P, NT, 3, HG])
        mb = sb("mb", [P, 2, NT, HG], BF16)
        mrow = sb("mrow", [3 * HG, T], BF16)
        pt = sb("pt", [P, 2, HG, T])
        ysb = sb("ysb", [128, 2, T])
        rl = sb("rl", [P, NT, HG])
        yn, yT = hn, nT
        f0 = sb("f0", [128, T + 2])
        kb = sb("kb", [KH, E, T], F32R)
        v2 = sb("v2", [P, NT, E, HD + 1])
        gt = sb("gt", [P, 2, NT, GH])
        gm = sb("gm", [P, E, NT, GH])
        z = sb("z", [P, 12, NT, E])
        zs = sb("zs", [P, 8, NT])
        mfx = sb("mfx", [P, 2, NT])
        mfr = sb("mfr", [P, 2, NT], F32R)
        mf = sb("mf", [P, NT, KH])
        wl = sb("wl", [P, 2, NT])
        with ExitStack() as stage:
            def sc(name, shape, dt=F32):
                return stage.enter_context(nc.sbuf_tensor(name, shape, dt))
            xT = sc("xT", [KH, NK, T])
            cv = sc("cv", [128, MI, T])
            hT = sc("hT", [128, MI, T])
            sg = sc("sg", [128, 2, T])
            gT = sc("gT", [128, MI, T])
            y = sc("y", [P, NT, D])
            t1 = sc("t1", [P, NT, D])
        with ExitStack() as stage:
            def sc(name, shape, dt=F32):
                return stage.enter_context(nc.sbuf_tensor(name, shape, dt))
            f = sc("f", [KH, 2 * NK, T])
            fr = sc("fr", [KH, 2, T])
            parts = sc("parts", [KH, 2 * NK, 3, T], BF16)
            qs = sc("qs", [STACK + 3, H, T], BF16)
        ff = sb("ff", [128, 2 * E, T])
        qc = sb("qc", [128, T])
        qa = sb("qa", [128, E, T], F32R)
        qb = sb("qb", [KH, E, T], F32R)
        ka = sb("ka", [128, E, T], F32R)
        rowsd = nc.dram_tensor("rowsd", [NG, 3 * HG, T], BF16, kind="Internal").ap()
        stackd = nc.dram_tensor("stackd", [2 * NK, KH, 3, T], BF16, kind="Internal").ap()

        ps = [ctx.enter_context(nc.psum_tensor(f"ps{n}", [128, 1024], F32)) for n in range(RING)]
        acc = ctx.enter_context(nc.psum_tensor("acc", [128, 1024], F32))

        filled = tally("filled", len(UNITS))
        emptied = {"act": tally("emptied_act", len(EMPTIED["act"]), RING),
                   "dve": tally("emptied_dve", len(EMPTIED["dve"]), RING)}
        w_in = sem("w_in")
        w_all = sem("w_all")
        consts = sem("consts")
        scaled = sem("scaled")
        x_in = tally("x_in", 16)
        tap = tally("tap", MI * TAPS)
        mixed = tally("mixed", MI)
        gated = tally("gated", MI)
        stat = tally("stat", 3 * NSTAT)
        var_c = tally("var_c", 7)
        normed = tally("normed", 3)
        norm_t = tally("norm_t", 1)
        h0_ok = tally("h0_ok", 1)
        h0b_ok = tally("h0b_ok", 2)
        split = tally("split", 3 * 2 * NK)
        split_s = tally("split_s", 2 * NK)
        var_s = tally("var_s", 1)
        made = sem("made")
        zeroed = sem("zeroed")
        stack_w = [tally(f"stack_w{n}", 16) for n in range(2 * NK)]
        stack_r = tally("stack_r", 16 * 2 * NK * len(QPARTS))
        msplit = tally("msplit", 6 * NG)
        mrow_w = [tally(f"mrow_w{g}", 16) for g in range(NG)]
        mrows = [tally(f"mrows{g}", 16) for g in range(NG)]
        pv_done = tally("pv_done", (NG + E) * NT)
        y_out = tally("y_out", NG + E)
        rl_ok = tally("rl_ok", NG + 2 * E)
        fsplit_a = tally("fsplit_a", 2 * E + 1)
        fconv = tally("fconv", 3)
        fsplit_v = tally("fsplit_v", 3 * E)
        mfsplit = tally("mfsplit", 4 * E)
        vg_ok = tally("vg_ok", NT // 2)
        gate_p = tally("gate_p", E)
        relu = tally("relu", 1)
        gate_v = tally("gate_v", 16)
        gate_a = tally("gate_a", 2)
        stored = tally("stored", 32, 32)

        block = ctx.enter_context(nc.Block())

        def ring(key):
            return ps[UNIT_AT[key] % RING]

        def free_at(b, key):
            n = UNIT_AT[key] - RING
            old = UNITS[n if n >= 0 else max(m for m in range(len(UNITS)) if (m - n) % RING == 0)][0]
            t = emptied[EMPTIER[old]]
            return t.at(b, EMPTY_AT[old] + 1 - (t.per if n < 0 else 0))

        def emptied_at(b, key):
            return emptied[EMPTIER[key]].at(b, EMPTY_AT[key] + 1)

        def filled_at(b, key):
            return filled.at(b, UNIT_AT[key] + 1)

        @block.sync
        def _(sp):
            sp.dma_start(W[:, :, 0:DI], w96[:, :, 0:DI]).then_inc(w_in, 16)
            sp.dma_start(Cc[:, :], cols).then_inc(w_in, 16)
            sp.dma_start(W3[:, :, :], w128).then_inc(w_all, 16)
            sp.dma_start(R[:, :], rows).then_inc(w_all, 16)
            sp.dma_start(W[:, :, DI:W96], w96[:, :, DI:W96]).then_inc(w_all, 16)
            with sp.Fori(0, B) as b:
                sp.wait_ge(*emptied["act"].at(b, 0))
                sp.dma_start(xin[:, :, :], x[bass.ds(b, 1), :, :].rearrange("o (n p) d -> p (o n) d", p=P)
                             ).then_inc(x_in.sem, 16)
                for n in range(2 * NK):
                    sp.wait_ge(*split.at(b, 3 * (n + 1)))
                    sp.dma_start(stackd[n], parts[:, n, :, :]).then_inc(stack_w[n].sem, 16)
                for n in range(2 * NK):
                    dst, order = (qs, QPARTS) if n < NK else (ks, KPARTS)
                    hh = H // NK
                    sp.wait_ge(*stack_w[n].at(b, 16))
                    for r, part in enumerate(order):
                        sp.dma_start(dst[r * DH:(r + 1) * DH, hh * (n % NK):hh * (n % NK + 1), :],
                                     stackd[n].rearrange("(h i) p t -> p i h t", i=DH)[part]
                                     ).then_inc(stack_r.sem, 16)
                for g in range(NG):
                    sp.wait_ge(*emptied_at(b, ("mta", g, 0, 0)))
                    sp.dma_start(rowsd[g], mrow[:, :]).then_inc(mrow_w[g].sem, 16)
                    sp.wait_ge(*mrow_w[g].at(b, 16))
                    sp.dma_start(qs[STACK:STACK + 3, HG * g:HG * (g + 1), :],
                                 rowsd[g].rearrange("(p h) t -> p h t", p=3)).then_inc(mrows[g].sem, 16)
                sp.wait_ge(*emptied_at(b, ("p2", NT // 2 - 1)))
                sp.dma_start(out[bass.ds(b, 1), 0:P * (NT - 1), :].rearrange("o (n p) d -> p (o n) d", p=P),
                             h1[:, 0:NT - 1, :]).then_inc(stored.sem, 16)
                sp.dma_start(out[bass.ds(b, 1), P * (NT - 1):T - 1, :].rearrange("o (n p) d -> p (o n) d", p=P - 1),
                             h1[0:P - 1, NT - 1:NT, :]).then_inc(stored.sem, 16)
            sp.wait_ge(stored.sem, 32 * (B + 1))

        @block.tensor
        def _(pe):
            def turn(b, key, src):
                pe.wait_ge(*free_at(b, key))
                d = ring(key)
                for i in range(NT):
                    c = C0 + P * i
                    mm = nc.tensor.transpose(d[0:KH, c:c + P], src[:, i, :], idf[0:P, 0:P])
                mm.then_inc(filled.sem, 1)

            def by_feature(b, key, w, src, m):
                pe.wait_ge(*free_at(b, key))
                d = ring(key)
                n = len(w)
                for s, e in cuts(0, T):
                    for k in range(n):
                        mm = nc.tensor.matmul(d[0:m, C0 + s:C0 + e], w[k], src[k][:, s:e],
                                              start=(k == 0), stop=(k == n - 1))
                mm.then_inc(filled.sem, 1)

            def by_token(b, key, src, w, width):
                pe.wait_ge(*free_at(b, key))
                d = ring(key)
                n = len(w)
                for o in range(2):
                    i = 2 * key[1] + o
                    for k in range(n):
                        mm = nc.tensor.matmul(d[0:P, 512 * o:512 * o + width], src[k][:, P * i:P * (i + 1)], w[k],
                                              start=(k == 0), stop=(k == n - 1))
                mm.then_inc(filled.sem, 1)

            def wk(o, n):
                return [W[:, k, o:o + n] for k in range(NK)]

            def softmax(b, steps):
                for kind, g, i, h in steps:
                    key, what, br = (kind, g, i, h), kind[:2], kind[2]
                    hd = HG * g + h
                    if what == "s1":
                        pe.wait_ge(*free_at(b, key))
                        d = ring(key)
                        z0 = P * (i + 1)
                        if br == "f":
                            z0 += z0 % 2
                        for s, e in cuts(0, z0):
                            diag = e == z0
                            if br == "a":
                                nc.tensor.matmul(d[0:P, C0 + s:C0 + e], qs[0:STACK, hd, P * i:P * (i + 1)],
                                                 ks[0:STACK, hd, s:e], start=True, stop=not diag)
                            else:
                                nc.tensor.matmul(d[0:P, C0 + s:C0 + e], qa[:, g, P * i:P * (i + 1)],
                                                 ka[:, g, s:e], start=True, stop=not diag)
                            if diag:
                                nc.tensor.matmul(d[0:P, C0 + P * i:C0 + z0], idb[0:P, 0:P],
                                                 mask_q[:, 0:z0 - P * i], start=False, stop=True
                                                 ).then_inc(filled.sem, 1)
                    elif what == "mt":
                        pe.wait_ge(*free_at(b, key))
                        d = ring(key)
                        if br == "a":
                            pe.wait_ge(*msplit.at(b, 6 * (g + 1)))
                        else:
                            pe.wait_ge(*mfsplit.at(b, 4 * (g + 1)))
                        for t in range(NT):
                            c = C0 + P * t
                            if br == "a":
                                mm = nc.tensor.transpose(d[0:3 * HG, c:c + P],
                                                         m3[:, t, :, :].rearrange("p a h -> p (a h)"), idf[0:P, 0:P])
                            else:
                                mm = nc.tensor.transpose(d[0:KH, c:c + P], mf[:, t, :], idf[0:P, 0:P])
                        mm.then_inc(filled.sem, 1)
                    elif what == "s2":
                        if br == "a" and h == 0 and i == 0:
                            pe.wait_ge(*mrows[g].at(b, 16))
                        if br == "f" and i == 0:
                            pe.wait_ge(*emptied_at(b, ("mtf", g, 0, 0)))
                        pe.wait_ge(*free_at(b, key))
                        d = ring(key)
                        a0 = P * i
                        if br == "f":
                            a0 -= a0 % 2
                        for s, e in cuts(a0, T):
                            diag = s == a0
                            dst = d[0:P, C0 + s:C0 + e]
                            last = e == T
                            if br == "a":
                                mm = nc.tensor.matmul(dst, ks[:, hd, P * i:P * (i + 1)], qs[:, hd, s:e],
                                                      start=True, stop=not diag)
                            else:
                                nc.tensor.matmul(dst, ka[:, g, P * i:P * (i + 1)], qa[:, g, s:e],
                                                 start=True, stop=False)
                                mm = nc.tensor.matmul(dst, kb[:, g, P * i:P * (i + 1)], qb[:, g, s:e],
                                                      start=False, stop=not diag)
                            if diag:
                                mm = nc.tensor.matmul(d[0:P, C0 + a0:C0 + P * (i + 1)], idb[0:P, 0:P],
                                                      mask_k[:, 1 - (P * i - a0):P + 1], start=False, stop=True)
                            if last:
                                mm.then_inc(filled.sem, 1)
                    elif what == "pv":
                        heads = HG if br == "a" else 1
                        if i == 0:
                            if g or br == "f":
                                pe.wait_ge(*y_out.at(b, g + (NG if br == "f" else 0)))
                        pe.wait_ge(*emptied_at(b, ("s2" + br, g, i, heads - 1)))
                        for s, e in cuts(P * i, T):
                            for hh in range(heads):
                                if br == "a":
                                    w, m0, m1 = va_[:, i, HG * g + hh, :], VS * hh, VS * (hh + 1)
                                else:
                                    w, m0, m1 = v2[:, i, g, :], 0, HD + 1
                                mm = nc.tensor.matmul(acc[m0:m1, C0 + s:C0 + e], w, pt[:, i % 2, hh, s:e],
                                                      start=(i == 0), stop=(P * (i + 1) == e))
                        mm.then_inc(pv_done.sem, 1)
                    else:
                        n = g + (NG if br == "f" else 0)
                        m = 128 if br == "a" else HD + 1
                        pe.wait_ge(*free_at(b, key))
                        d = ring(key)
                        pe.wait_ge(*y_out.at(b, n + 1))
                        for t in range(NT):
                            c = 512 * (t // 3) + 128 * (t % 3)
                            mm = nc.tensor.transpose(d[0:P, c:c + m], ysb[0:m, n % 2, P * t:P * (t + 1)],
                                                     idf[0:m, 0:m])
                        mm.then_inc(filled.sem, 1)

            pe.wait_ge(consts, N_CONSTS)
            pe.wait_ge(zeroed, 6)
            pe.wait_ge(w_in, 32)
            with pe.Fori(0, B) as b:
                pe.wait_ge(*x_in.at(b, 16))
                for k in range(NK):
                    turn(b, ("xt", k), xin[:, :, KH * k:KH * (k + 1)])
                pe.wait_ge(*emptied_at(b, ("xt", NK - 1)))
                for m in range(MI):
                    by_feature(b, ("xe", m), wk(O_IN + 128 * m, 128), [xT[:, k, :] for k in range(NK)], 128)
                pe.wait_ge(w_all, 48)
                pe.wait_ge(*mixed.at(b, MI))
                for m in range(MI):
                    for n, o in (("xg", O_X), ("zg", O_Z)):
                        by_feature(b, (n, m), [W3[:, k, o + 128 * m:o + 128 * (m + 1)] for k in range(MI)],
                                   [hT[:, k, :] for k in range(MI)], 128)
                pe.wait_ge(*gated.at(b, MI))
                for t in range(NT // 2):
                    by_token(b, ("y", t), [gT[:, k, :] for k in range(MI)],
                             [W3[:, k, O_OUT:O_OUT + D] for k in range(MI)], D)
                pe.wait_ge(*normed.at(b, 2))
                for k in range(NK):
                    turn(b, ("nt", k), hn[:, :, KH * k:KH * (k + 1)])
                pe.wait_ge(*emptied_at(b, ("nt", NK - 1)))
                nt = [nT[:, k, :] for k in range(NK)]
                for n in range(2 * NK):
                    by_feature(b, ("qk", n), wk(O_QK + KH * n, KH), nt, KH)
                for t in range(NT // 2):
                    by_token(b, ("v", t), nt, wk(O_V, D), D)
                pe.wait_ge(*emptied_at(b, ("v", NT // 2 - 1)))
                pe.wait_ge(*stack_r.at(b, stack_r.per))
                softmax(b, ATTN)
                pe.wait_ge(*emptied_at(b, ("yta", NG - 1, 0, 0)))
                for k in range(NK):
                    turn(b, ("ot", k), yn[:, :, KH * k:KH * (k + 1)])
                pe.wait_ge(*emptied_at(b, ("ot", NK - 1)))
                for t in range(NT // 2):
                    by_token(b, ("p", t), [yT[:, k, :] for k in range(NK)], wk(O_PROJ, D), D)
                pe.wait_ge(*normed.at(b, 3))
                for k in range(NK):
                    turn(b, ("n2", k), hn[:, :, KH * k:KH * (k + 1)])
                pe.wait_ge(*emptied_at(b, ("n2", NK - 1)))
                nt = [nT[:, k, :] for k in range(NK)]
                for n in range(2 * E):
                    by_feature(b, ("fq", n), wk(O_FQK + 128 * n, 128), nt, 128)
                for t in range(NT // 2):
                    by_token(b, ("vg", t), nt, wk(O_VG, D + GH), D + GH)
                pe.wait_ge(*emptied_at(b, ("vg", NT // 2 - 1)))
                pe.wait_ge(*fsplit_v.at(b, 3 * E))
                softmax(b, FFN)
                pe.wait_ge(*emptied_at(b, ("ytf", E - 1, 0, 0)))
                for k in range(NK):
                    turn(b, ("o2", k), yn[:, :, KH * k:KH * (k + 1)])
                pe.wait_ge(*emptied_at(b, ("o2", NK - 1)))
                for t in range(NT // 2):
                    by_token(b, ("p2", t), [yT[:, k, :] for k in range(NK)], wk(O_WP, D), D)

        @block.scalar
        def _(act):
            freed = emptied["act"].sem

            def row(key, m=128):
                return ring(key)[0:m, C0:C0 + T]

            def rows_out(b, steps):
                for kind, g, i, h in steps:
                    key, what, br = (kind, g, i, h), kind[:2], kind[2]
                    heads = HG if br == "a" else 1
                    n = g + (NG if br == "f" else 0)
                    if what == "s2":
                        if h == 0 and n * NT + i >= 2:
                            act.wait_ge(*pv_done.at(b, n * NT + i - 1))
                        act.wait_ge(*filled_at(b, key))
                        a0 = P * i
                        if br == "f":
                            a0 -= a0 % 2
                        nc.scalar.activation(pt[:, i % 2, h, a0:T], ring(key)[0:P, C0 + a0:C0 + T], ACT.Exp
                                             ).then_inc(freed, 1)
                    elif what == "pv" and i == NT - 1:
                        m = 128 if br == "a" else HD + 1
                        act.wait_ge(*pv_done.at(b, (n + 1) * NT))
                        if n >= 2:
                            act.wait_ge(*filled_at(b, ("yta" if n < NG + 2 else "ytf", (n - 2) % NG, 0, 0)))
                        nc.scalar.activation(ysb[0:m, n % 2, :], acc[0:m, C0:C0 + T], ACT.Copy
                                             ).then_inc(y_out.sem, 1)

            act.wait_ge(w_in, 32)
            act.wait_ge(scaled, 2)
            with act.Fori(0, B) as b:
                for k in range(NK):
                    act.wait_ge(*filled_at(b, ("xt", k)))
                    nc.scalar.activation(xT[:, k, :], row(("xt", k), KH), ACT.Copy).then_inc(freed, 1)
                for m in range(MI):
                    act.wait_ge(*filled_at(b, ("xe", m)))
                    nc.scalar.activation(xe[:, m, 1:1 + T], row(("xe", m)), ACT.Copy).then_inc(freed, 1)
                for m in range(MI):
                    act.wait_ge(*tap.at(b, TAPS * (m + 1)))
                    nc.scalar.activation(hT[:, m, :], cv[:, m, :], ACT.Silu,
                                         bias=Cc[:, C_CONV + 5 * m + 4:C_CONV + 5 * m + 5]).then_inc(mixed.sem, 1)
                for m in range(MI):
                    for o, n in enumerate(("xg", "zg")):
                        act.wait_ge(*filled_at(b, (n, m)))
                        if o and m >= 2:
                            act.wait_ge(*gated.at(b, m - 1))
                        nc.scalar.activation(sg[:, m % 2, :] if o else gT[:, m, :], row((n, m)), ACT.Silu
                                             ).then_inc(freed, 1)
                for t in range(NT // 2):
                    act.wait_ge(*filled_at(b, ("y", t)))
                    nc.scalar.activation(y[:, 2 * t:2 * t + 2, :],
                                         ring(("y", t))[0:P, :].rearrange("p (o c) -> p o c", o=2)[:, :, 0:D],
                                         ACT.Copy).then_inc(freed, 1)
                for k in range(NK):
                    act.wait_ge(*filled_at(b, ("nt", k)))
                    nc.scalar.activation(nT[:, k, :], row(("nt", k), KH), ACT.Copy).then_inc(freed, 1)
                for n in range(2 * NK):
                    act.wait_ge(*filled_at(b, ("qk", n)))
                    if n < NK:
                        nc.scalar.activation(f[:, n, :], row(("qk", n), KH), ACT.Identity,
                                             bias=qb4[:, n:n + 1], scale=DH ** -0.5).then_inc(freed, 1)
                    else:
                        nc.scalar.activation(f[:, n, :], row(("qk", n), KH), ACT.Identity,
                                             bias=Cc[0:KH, C_QK + n:C_QK + n + 1]).then_inc(freed, 1)
                rows_out(b, ATTN)
                for k in range(NK):
                    act.wait_ge(*filled_at(b, ("ot", k)))
                    nc.scalar.activation(yT[:, k, :], row(("ot", k), KH), ACT.Copy).then_inc(freed, 1)
                for k in range(NK):
                    act.wait_ge(*filled_at(b, ("n2", k)))
                    nc.scalar.activation(nT[:, k, :], row(("n2", k), KH), ACT.Copy).then_inc(freed, 1)
                act.wait_ge(*filled_at(b, ("fq", 0)))
                nc.scalar.activation(f0[:, 1:T], row(("fq", 0))[:, 0:T - 1], ACT.Identity,
                                     bias=Cc[:, C_FQK:C_FQK + 1]).then_inc(freed, 1)
                for n in range(1, 2 * E):
                    act.wait_ge(*filled_at(b, ("fq", n)))
                    if n < E:
                        nc.scalar.activation(ff[:, n, :], row(("fq", n)), ACT.Identity,
                                             bias=fb8[:, n:n + 1], scale=HD ** -0.5).then_inc(freed, 1)
                    else:
                        nc.scalar.activation(ff[:, n, :], row(("fq", n)), ACT.Identity,
                                             bias=Cc[:, C_FQK + n:C_FQK + n + 1]).then_inc(freed, 1)
                for n in range(1, 2 * E):
                    act.wait_ge(*emptied_at(b, ("fq", n)))
                    nc.scalar.activation((qa if n < E else ka)[:, n % E, :], ff[:, n, :], ACT.Copy
                                         ).then_inc(fsplit_a.sem, 1)
                act.wait_ge(*fconv.at(b, 3))
                nc.scalar.activation(ff[:, 0, :], qc[:, :], ACT.Identity, bias=fb8[:, E:E + 1],
                                     scale=HD ** -0.5).then_inc(fsplit_a.sem, 1)
                act.wait_ge(*fsplit_a.at(b, 2 * E))
                nc.scalar.activation(qa[:, 0, :], ff[:, 0, :], ACT.Copy).then_inc(fsplit_a.sem, 1)
                act.wait_ge(*vg_ok.at(b, NT // 2))
                nc.scalar.activation(gt[:, 1], gt[:, 0], ACT.Relu).then_inc(relu.sem, 1)
                act.wait_ge(*gate_v.at(b, 4))
                nc.scalar.activation(z[:, 1], z[:, 11], ACT.Exp).then_inc(gate_a.sem, 1)
                act.wait_ge(*gate_v.at(b, 7))
                nc.scalar.activation(z[:, 3], z[:, 2], ACT.Exp).then_inc(gate_a.sem, 1)
                rows_out(b, FFN)
                for k in range(NK):
                    act.wait_ge(*filled_at(b, ("o2", k)))
                    nc.scalar.activation(yT[:, k, :], row(("o2", k), KH), ACT.Copy).then_inc(freed, 1)

        @block.vector
        def _(dve):
            freed = emptied["dve"].sem

            def pair(key, w):
                return ring(key)[0:P, :].rearrange("p (o c) -> p o c", o=2)[:, :, 0:w]

            def tiles(ap):
                return ap.unsqueeze(1).to_broadcast([P, NT, ap.shape[-1]])

            def moments(b, n, src):
                for t in range(NT):
                    nc.vector.bn_stats(stats[:, n, t, :], src[:, t, :]).then_inc(stat.sem, 1)
                dve.wait_ge(*stat.at(b, NSTAT * n + NT))
                nc.vector.memset(begun[:, n:n + 1], 0.0).then_inc(stat.sem, 1)
                for t in range(NT):
                    nc.vector.bn_aggr(mv[:, n, t, :], stats[:, n, t:t + 1, :]).then_inc(stat.sem, 1)

            def normalise(n, dst, src, t):
                return nc.vector.tensor_scalar(dst[:, t, :], src[:, t, :], mv[:, n, t, 0:1], rs[:, n, t:t + 1],
                                               ALU.subtract, ALU.mult)

            def maxima(b, steps):
                for kind, g, i, h in steps:
                    key, what, br = (kind, g, i, h), kind[:2], kind[2]
                    n = g + (NG if br == "f" else 0)
                    if what == "s1":
                        dve.wait_ge(*filled_at(b, key))
                        z0 = P * (i + 1)
                        if br == "a":
                            nc.vector.tensor_reduce(mx[:, g % 2, i, h:h + 1], ring(key)[0:P, C0:C0 + z0], AX.X, ALU.max
                                                    ).then_inc(freed, 1)
                        else:
                            z0 += z0 % 2
                            nc.vector.tensor_reduce(mfx[:, g % 2, i:i + 1], ring(key)[0:P, C0:C0 + z0], AX.X, ALU.max
                                                    ).then_inc(freed, 1)
                        if i == NT - 1 and (br == "f" or h == HG - 1):
                            dve.wait_ge(*emptied_at(b, key))
                            (split_max if br == "a" else split_max_f)(b, g)
                    elif what == "mt":
                        dve.wait_ge(*filled_at(b, key))
                        if br == "a":
                            if g:
                                dve.wait_ge(*mrow_w[g - 1].at(b, 16))
                            nc.vector.tensor_copy(mrow[:, :], ring(key)[0:3 * HG, C0:C0 + T]).then_inc(freed, 1)
                        else:
                            nc.vector.tensor_copy(qb[HD:KH, g, :], ring(key)[HD:KH, C0:C0 + T]).then_inc(freed, 1)
                    elif what == "yt":
                        dve.wait_ge(*filled_at(b, key))
                        d = ring(key)
                        banks = [d[0:P, 512 * o:512 * o + 384].rearrange("p (t h c) -> p t h c", t=3, c=VS)
                                 for o in range(2)]
                        if br == "a":
                            for o in range(2):
                                last = nc.vector.reciprocal(rl[:, 3 * o:3 * o + 3, :], banks[o][:, :, :, DH])
                            last.then_inc(rl_ok.sem, 1)
                            dve.wait_ge(*rl_ok.at(b, g + 1))
                            for o in range(2):
                                last = nc.vector.tensor_tensor(
                                    yn[:, 3 * o:3 * o + 3, D // NG * g:D // NG * (g + 1)].rearrange(
                                        "p t (h c) -> p t h c", c=DH),
                                    banks[o][:, :, :, 0:DH],
                                    rl[:, 3 * o:3 * o + 3, :].unsqueeze(3).to_broadcast([P, 3, HG, DH]), ALU.mult)
                            last.then_inc(freed, 1)
                        else:
                            banks = [d[0:P, 512 * o:512 * o + 384].rearrange("p (t c) -> p t c", t=3)
                                     for o in range(2)]
                            for o in range(2):
                                last = nc.vector.reciprocal(wl[:, 0, 3 * o:3 * o + 3], banks[o][:, :, HD])
                            last.then_inc(rl_ok.sem, 1)
                            dve.wait_ge(*rl_ok.at(b, NG + 2 * g + 1))
                            nc.vector.tensor_tensor(wl[:, 1, :], wl[:, 0, :], z[:, 10, :, g], ALU.mult
                                                    ).then_inc(rl_ok.sem, 1)
                            dve.wait_ge(*rl_ok.at(b, NG + 2 * g + 2))
                            for o in range(2):
                                last = nc.vector.tensor_tensor(
                                    yn[:, 3 * o:3 * o + 3, HD * g:HD * (g + 1)], banks[o][:, :, 0:HD],
                                    wl[:, 1, 3 * o:3 * o + 3].unsqueeze(2).to_broadcast([P, 3, HD]), ALU.mult)
                            last.then_inc(freed, 1)

            def split_max(b, g):
                def step(k, ins):
                    ins.then_inc(msplit.sem, 1)
                    if k < 6:
                        dve.wait_ge(*msplit.at(b, 6 * g + k))
                m = mx[:, g % 2]
                if g:
                    dve.wait_ge(*filled_at(b, ("mta", g - 1, 0, 0)))
                step(1, nc.vector.tensor_scalar(mb[:, 0], m, -1.0, None, ALU.mult))
                step(2, nc.vector.scalar_tensor_tensor(mr[:, 0], m, -1.0, mb[:, 0], ALU.mult, ALU.subtract))
                step(3, nc.vector.tensor_copy(mb[:, 1], mr[:, 0]))
                nc.vector.tensor_copy(m3[:, :, 0, :], mb[:, 0])
                step(4, nc.vector.tensor_copy(m3[:, :, 1, :], mb[:, 1]))
                step(5, nc.vector.tensor_tensor(mr[:, 1], mr[:, 0], mb[:, 1], ALU.subtract))
                step(6, nc.vector.tensor_copy(m3[:, :, 2, :], mr[:, 1]))

            def split_max_f(b, e):
                def step(k, ins):
                    ins.then_inc(mfsplit.sem, 1)
                    if k < 4:
                        dve.wait_ge(*mfsplit.at(b, 4 * e + k))
                m = mfx[:, e % 2]
                if e:
                    dve.wait_ge(*filled_at(b, ("mtf", e - 1, 0, 0)))
                step(1, nc.vector.tensor_scalar(mfr[:, 0], m, -1.0, None, ALU.mult))
                step(2, nc.vector.scalar_tensor_tensor(mfr[:, 1], m, -1.0, mfr[:, 0], ALU.mult, ALU.subtract))
                step(3, nc.vector.tensor_copy(mf[:, :, HD], mfr[:, 0]))
                step(4, nc.vector.tensor_copy(mf[:, :, HD + 1], mfr[:, 1]))

            def gate(b):
                def step(k, ins, wait=True):
                    ins.then_inc(gate_v.sem, 1)
                    if wait:
                        dve.wait_ge(*gate_v.at(b, k))
                def over(ap):
                    return ap.unsqueeze(2).to_broadcast([P, NT, E])
                dve.wait_ge(*gate_p.at(b, E))
                step(1, nc.vector.tensor_reduce(z[:, 0].rearrange("p t e -> p e t"), gm[:, :, :, :], AX.X, ALU.add))
                step(2, nc.vector.tensor_tensor(z[:, 7], z[:, 0], tiles(R[:, R_BG2:R_BG2 + E]), ALU.add))
                step(3, nc.vector.tensor_reduce(zs[:, 0], z[:, 7], AX.X, ALU.max))
                step(4, nc.vector.tensor_tensor(z[:, 11], z[:, 7], over(zs[:, 0]), ALU.subtract))
                dve.wait_ge(*gate_a.at(b, 1))
                step(5, nc.vector.tensor_reduce(zs[:, 1], z[:, 1], AX.X, ALU.add))
                step(6, nc.vector.reciprocal(zs[:, 2], zs[:, 1]))
                step(7, nc.vector.tensor_tensor(z[:, 2], z[:, 1], over(zs[:, 2]), ALU.mult))
                p = [z[:, 2, :, e] for e in range(E)]
                c = [zs[:, 3 + n] for n in range(5)]
                nc.vector.tensor_tensor(c[0], p[0], p[1], ALU.is_lt)
                nc.vector.tensor_tensor(c[1], p[0], p[2], ALU.is_lt)
                nc.vector.tensor_tensor(c[2], p[1], p[0], ALU.is_le)
                nc.vector.tensor_tensor(c[3], p[1], p[2], ALU.is_lt)
                step(8, nc.vector.tensor_tensor(c[4], p[2], p[0], ALU.is_le))
                nc.vector.tensor_tensor(z[:, 4, :, 0], c[0], c[1], ALU.mult)
                nc.vector.tensor_tensor(z[:, 4, :, 1], c[2], c[3], ALU.mult)
                step(9, nc.vector.tensor_tensor(z[:, 5, :, 0], p[2], p[1], ALU.is_le))
                step(10, nc.vector.tensor_tensor(z[:, 4, :, 2], c[4], z[:, 5, :, 0], ALU.mult))
                step(11, nc.vector.tensor_scalar(z[:, 6], z[:, 4], -1.0, 1.0, ALU.mult, ALU.add))
                dve.wait_ge(*gate_a.at(b, 2))
                step(12, nc.vector.tensor_tensor(z[:, 8], z[:, 3], z[:, 6], ALU.mult))
                step(13, nc.vector.tensor_reduce(zs[:, 0], z[:, 8], AX.X, ALU.add))
                step(14, nc.vector.reciprocal(zs[:, 1], zs[:, 0]))
                step(15, nc.vector.tensor_tensor(z[:, 10], z[:, 8], over(zs[:, 1]), ALU.mult))
                step(16, nc.vector.tensor_copy(z[:, 9, :, 0], zs[:, 0]))

            nc.vector.memset(wl[:, 0, :], 0.0).then_inc(emptied["act"].sem, RING)
            nc.vector.memset(wl[:, 1, :], 0.0).then_inc(emptied["dve"].sem, RING)
            nc.vector.memset(begun[:, :], 0.0).then_inc(stored.sem, 32)
            nc.vector.memset(xe[:, :, :], 0.0).then_inc(zeroed, 1)
            nc.vector.memset(f0[:, :], 0.0).then_inc(zeroed, 1)
            nc.vector.memset(va_[:, :, :, :], 0.0).then_inc(zeroed, 1)
            dve.wait_ge(zeroed, 3)
            nc.vector.memset(va_[:, :, :, DH:DH + 1], 1.0).then_inc(zeroed, 1)
            nc.vector.memset(v2[:, :, :, HD:HD + 1], 1.0).then_inc(zeroed, 1)
            nc.vector.memset(mf[:, :, :], 0.0).then_inc(zeroed, 1)
            dve.wait_ge(w_in, 32)
            nc.vector.tensor_scalar(qb4[:, :], Cc[0:KH, C_QK:C_QK + NK], DH ** -0.5, None, ALU.mult).then_inc(scaled, 1)
            nc.vector.tensor_scalar(fb8[:, :], Cc[:, C_FB:C_FB + E + 1], HD ** -0.5, None, ALU.mult).then_inc(scaled, 1)
            dve.wait_ge(w_all, 48)
            dve.wait_ge(zeroed, 6)
            with dve.Fori(0, B) as b:
                for m in range(MI):
                    dve.wait_ge(*emptied_at(b, ("xe", m)))
                    w = C_CONV + 5 * m
                    nc.vector.tensor_scalar(cv[:, m, :], xe[:, m, 0:T], Cc[:, w:w + 1], None, ALU.mult
                                            ).then_inc(tap.sem, 1)
                    for k in range(1, TAPS):
                        dve.wait_ge(*tap.at(b, TAPS * m + k))
                        nc.vector.scalar_tensor_tensor(cv[:, m, :], xe[:, m, k:k + T], Cc[:, w + k:w + k + 1],
                                                       cv[:, m, :], ALU.mult, ALU.add).then_inc(tap.sem, 1)
                for m in range(MI):
                    dve.wait_ge(*emptied_at(b, ("zg", m)))
                    nc.vector.tensor_tensor(gT[:, m, :], gT[:, m, :], sg[:, m % 2, :], ALU.mult
                                            ).then_inc(gated.sem, 1)
                dve.wait_ge(*emptied_at(b, ("y", NT // 2 - 1)))
                moments(b, 0, y)
                dve.wait_ge(*var_c.at(b, 4))
                for t in range(NT):
                    last = normalise(0, t1, y, t)
                last.then_inc(normed.sem, 1)
                dve.wait_ge(*normed.at(b, 1))
                nc.vector.tensor_tensor(y[:, :, :], t1[:, :, :], tiles(R[:, R_GAMMA:R_GAMMA + D]), ALU.mult
                                        ).then_inc(norm_t.sem, 1)
                dve.wait_ge(*norm_t.at(b, 1))
                nc.vector.tensor_tensor(h0[:, :, :], y[:, :, :], tiles(R[:, R_BETA:R_BETA + D]), ALU.add
                                        ).then_inc(h0_ok.sem, 1)
                dve.wait_ge(*h0_ok.at(b, 1))
                moments(b, 1, h0)
                dve.wait_ge(*var_c.at(b, 6))
                for t in range(NT):
                    last = normalise(1, hn, h0, t)
                last.then_inc(normed.sem, 1)
                for n in range(2 * NK):
                    dve.wait_ge(*emptied_at(b, ("qk", n)))
                    nc.vector.tensor_copy(parts[:, n, 0, :], f[:, n, :]).then_inc(split.sem, 1)
                    dve.wait_ge(*split.at(b, 3 * n + 1))
                    nc.vector.tensor_tensor(fr[:, n % 2, :], f[:, n, :], parts[:, n, 0, :], ALU.subtract
                                            ).then_inc(split_s.sem, 1)
                    dve.wait_ge(*split_s.at(b, n + 1))
                    nc.vector.tensor_copy(parts[:, n, 1, :], fr[:, n % 2, :]).then_inc(split.sem, 1)
                    dve.wait_ge(*split.at(b, 3 * n + 2))
                    nc.vector.tensor_tensor(parts[:, n, 2, :], fr[:, n % 2, :], parts[:, n, 1, :], ALU.subtract
                                            ).then_inc(split.sem, 1)
                for t in range(NT // 2):
                    dve.wait_ge(*filled_at(b, ("v", t)))
                    for o in range(2):
                        last = nc.vector.tensor_tensor(
                            va_[:, 2 * t + o, :, 0:DH],
                            ring(("v", t))[0:P, 512 * o:512 * o + D].rearrange("p (h c) -> p h c", c=DH),
                            R[:, R_BV:R_BV + D].rearrange("p (h c) -> p h c", c=DH), ALU.add)
                    last.then_inc(freed, 1)
                maxima(b, ATTN)
                dve.wait_ge(*h0b_ok.at(b, 1))
                dve.wait_ge(*stored.at(b, 0))
                for t in range(NT // 2):
                    dve.wait_ge(*filled_at(b, ("p", t)))
                    nc.vector.tensor_tensor(h1[:, 2 * t:2 * t + 2, :], pair(("p", t), D), h0[:, 2 * t:2 * t + 2, :],
                                            ALU.add).then_inc(freed, 1)
                dve.wait_ge(*emptied_at(b, ("p", NT // 2 - 1)))
                moments(b, 2, h1)
                dve.wait_ge(*var_c.at(b, 7))
                for t in range(NT):
                    last = normalise(2, hn, h1, t)
                last.then_inc(normed.sem, 1)
                dve.wait_ge(*emptied_at(b, ("fq", 0)))
                nc.vector.tensor_scalar(qc[:, :], f0[:, 0:T], Cc[:, C_FC:C_FC + 1], None, ALU.mult
                                        ).then_inc(fconv.sem, 1)
                for k in (1, 2):
                    dve.wait_ge(*fconv.at(b, k))
                    nc.vector.scalar_tensor_tensor(qc[:, :], f0[:, k:k + T], Cc[:, C_FC + k:C_FC + k + 1],
                                                   qc[:, :], ALU.mult, ALU.add).then_inc(fconv.sem, 1)
                for n in list(range(1, 2 * E)) + [0]:
                    e = n % E
                    dve.wait_ge(*fsplit_a.at(b, n if n else 2 * E + 1))
                    if n < E:
                        nc.vector.tensor_copy(qb[0:HD, e, :], ff[0:HD, n, :]).then_inc(fsplit_v.sem, 1)
                        nc.vector.tensor_tensor(qa[HD:128, e, :], ff[HD:128, n, :], qa[HD:128, e, :],
                                                ALU.subtract).then_inc(fsplit_v.sem, 1)
                    else:
                        nc.vector.tensor_tensor(kb[0:HD, e, :], ff[0:HD, n, :], ka[0:HD, e, :],
                                                ALU.subtract).then_inc(fsplit_v.sem, 1)
                for t in range(NT // 2):
                    dve.wait_ge(*filled_at(b, ("vg", t)))
                    nc.vector.tensor_tensor(gt[:, 0, 2 * t:2 * t + 2, :],
                                            pair(("vg", t), D + GH)[:, :, D:D + GH],
                                            R[:, R_BG1:R_BG1 + GH].unsqueeze(1).to_broadcast([P, 2, GH]), ALU.add
                                            ).then_inc(vg_ok.sem, 1)
                    for o in range(2):
                        last = nc.vector.tensor_tensor(
                            v2[:, 2 * t + o, :, 0:HD],
                            ring(("vg", t))[0:P, 512 * o:512 * o + D].rearrange("p (h c) -> p h c", c=HD),
                            R[:, R_BV2:R_BV2 + D].rearrange("p (h c) -> p h c", c=HD), ALU.add)
                    last.then_inc(freed, 1)
                gate(b)
                maxima(b, FFN)
                dve.wait_ge(*h0b_ok.at(b, 2))
                for t in range(NT // 2):
                    dve.wait_ge(*filled_at(b, ("p2", t)))
                    nc.vector.tensor_tensor(h1[:, 2 * t:2 * t + 2, :], pair(("p2", t), D), h1[:, 2 * t:2 * t + 2, :],
                                            ALU.add).then_inc(freed, 1)

        @block.gpsimd
        def _(pool):
            def select(dst, base, step, channel, fill, op=ALU.is_ge):
                nc.gpsimd.affine_select(out=dst, in_=dst, compare_op=op, fill=fill, base=base,
                                        pattern=[[step, dst.shape[-1]]], channel_multiplier=channel
                                        ).then_inc(consts, 1)

            for t in (idf, idb, mask_q, mask_k):
                nc.gpsimd.memset(t[:, :], 0.0).then_inc(made, 1)
            for n, v in enumerate(CONSTS):
                nc.gpsimd.memset(expo[:, n, :], v).then_inc(made, 1)
            n = 4 + len(CONSTS)
            pool.wait_ge(made, n)
            nc.gpsimd.memset(kb[HD:KH, :, :].bitcast(F32), 0.0).then_inc(made, 1)
            pool.wait_ge(made, n + 1)
            nc.gpsimd.memset(ks[STACK:STACK + 3, :, :], 1.0).then_inc(made, 1)
            pool.wait_ge(made, n + 2)
            nc.gpsimd.memset(kb[HD:HD + 2, :, :].bitcast(F32), 1.0).then_inc(made, 1)
            pool.wait_ge(made, n + 3)
            select(idf[:, :], 0, -1, 1, 1.0, ALU.not_equal)
            select(idb[:, :], 0, -1, 1, 1.0, ALU.not_equal)
            select(mask_q[:, :], 0, -1, 1, NEG)
            select(mask_k[:, :], -1, 1, -1, NEG)
            pool.wait_ge(w_all, 48)

            def tiles(ap):
                return ap.unsqueeze(1).to_broadcast([P, NT, ap.shape[-1]])

            with pool.Fori(0, B) as b:
                pool.wait_ge(*stat.at(b, NSTAT))
                nc.gpsimd.tensor_tensor(va[:, 0, :], mv[:, 0, :, 1], expo[:, 3, :], ALU.mult
                                        ).then_inc(var_c.sem, 1)
                pool.wait_ge(*var_c.at(b, 1))
                nc.gpsimd.tensor_tensor(sd[:, :], va[:, 0, :], expo[:, 1, :], ALU.pow).then_inc(var_c.sem, 1)
                pool.wait_ge(*var_c.at(b, 2))
                nc.gpsimd.tensor_tensor(sde[:, :], sd[:, :], expo[:, 4, :], ALU.add).then_inc(var_c.sem, 1)
                pool.wait_ge(*var_c.at(b, 3))
                nc.gpsimd.tensor_tensor(rs[:, 0, :], sde[:, :], expo[:, 2, :], ALU.pow).then_inc(var_c.sem, 1)
                for n, done in ((1, 4), (2, 6)):
                    pool.wait_ge(*stat.at(b, NSTAT * (n + 1)))
                    if n == 1:
                        nc.gpsimd.tensor_tensor(va[:, 1, :], mv[:, 1, :, 1], expo[:, 5, :], ALU.add
                                                ).then_inc(var_c.sem, 1)
                        pool.wait_ge(*var_c.at(b, 5))
                        nc.gpsimd.tensor_tensor(rs[:, 1, :], va[:, 1, :], expo[:, 0, :], ALU.pow
                                                ).then_inc(var_c.sem, 1)
                        pool.wait_ge(*normed.at(b, 2))
                        nc.gpsimd.tensor_tensor(h0[:, :, :], h0[:, :, :], tiles(R[:, R_BPROJ:R_BPROJ + D]), ALU.add
                                                ).then_inc(h0b_ok.sem, 1)
                    else:
                        nc.gpsimd.tensor_tensor(va[:, 2, :], mv[:, 2, :, 1], expo[:, 5, :], ALU.add
                                                ).then_inc(var_s.sem, 1)
                        pool.wait_ge(*var_s.at(b, 1))
                        nc.gpsimd.tensor_tensor(rs[:, 2, :], va[:, 2, :], expo[:, 0, :], ALU.pow
                                                ).then_inc(var_c.sem, 1)
                        pool.wait_ge(*normed.at(b, 3))
                        nc.gpsimd.tensor_tensor(h1[:, :, :], h1[:, :, :], tiles(R[:, R_BP:R_BP + D]), ALU.add
                                                ).then_inc(h0b_ok.sem, 1)
                pool.wait_ge(*relu.at(b, 1))
                for e in range(E):
                    nc.gpsimd.tensor_tensor(gm[:, e], gt[:, 1], tiles(R[:, R_WG2 + GH * e:R_WG2 + GH * (e + 1)]),
                                            ALU.mult).then_inc(gate_p.sem, 1)


def kernel(x, **w):
    import numpy as np
    import concourse.bacc as bacc
    from concourse.bass_utils import run_bass_kernel_spmd

    w = {k[3:]: np.asarray(v) for k, v in w.items()}
    x = np.ascontiguousarray(x)

    def contract(mats, n, p):
        a = np.concatenate(mats, axis=1)
        return np.ascontiguousarray(a.reshape(n, p, -1).transpose(1, 0, 2))

    wqk, bqk = w["ffn_Wqk"], w["ffn_bqk"]
    both = [wqk[:, HD * n:HD * (n + 1)] for n in range(2 * E) for _ in range(2)]
    w96 = contract([w["tok_W_in"].T, w["attn_w_attn"].T, w["attn_w_proj"].T, *both,
                    *w["ffn_Wv"], w["ffn_Wg1"], w["ffn_Wp"]], NK, KH)
    w128 = contract([w["tok_W_x"].T, w["tok_W_z"].T, w["tok_W_out"].T], MI, 128)
    cols = np.zeros((128, COLS), np.float32)
    conv = np.concatenate([w["tok_conv_w"][:, 0, :], w["tok_conv_b"][:, None]], axis=1)
    cols[:, C_CONV:C_QK] = conv.reshape(MI, 128, TAPS + 1).transpose(1, 0, 2).reshape(128, -1)
    cols[:KH, C_QK:C_FQK] = w["attn_b_attn"][:2 * D].reshape(2 * NK, KH).T
    for half in (slice(0, HD), slice(HD, 128)):
        cols[half, C_FQK:C_FB] = bqk.reshape(2 * E, HD).T
        cols[half, C_FB:C_FB + E] = bqk[:D].reshape(E, HD).T
        cols[half, C_FB + E] = w["ffn_conv_b"]
        cols[half, C_FC:COLS] = w["ffn_conv_w"][:, 0, :]
    row = np.concatenate([w["tok_gamma"], w["tok_beta"], w["attn_b_attn"][2 * D:], w["attn_b_proj"],
                          w["ffn_bv"].reshape(-1), w["ffn_bg1"], w["ffn_bp"],
                          w["ffn_Wg2"].T.reshape(-1), w["ffn_bg2"]])
    rows = np.ascontiguousarray(np.broadcast_to(row, (P, ROWS)))

    nc = bacc.Bacc("TRN2", target_bir_lowering=False, num_devices=1)
    arrays = {"x_dram": x, "w96_dram": w96, "w128_dram": w128, "cols_dram": cols, "rows_dram": rows}
    aps = [nc.dram_tensor(n, a.shape, mybir.dt.from_np(a.dtype), kind="ExternalInput").ap()
           for n, a in arrays.items()]
    out = nc.dram_tensor("out_dram", (B, T - 1, D), F32, kind="ExternalOutput").ap()
    audio_tower(nc, *aps, out)
    r = run_bass_kernel_spmd(nc, [arrays], core_ids=[0])
    return r.results[0]["out_dram"]
```

```python
from contextlib import ExitStack

import concourse.bass as bass
from concourse import mybir

F32 = mybir.dt.float32
F32R = mybir.dt.float32r
BF16 = mybir.dt.bfloat16
ACT = mybir.ActivationFunctionType
ALU = mybir.AluOpType
AX = mybir.AxisListType

B, T, D = 4, 750, 192
DI = 2 * D
TAPS = 4
P, NT = 125, 6
KH, NK = 96, 2
MI = DI // 128
H, DH = 12, 16
HG, NG = 4, 3
E, HD, GH = 3, 64, 32
VS = 32
SPLIT = 500
C0 = 512 - SPLIT
RING = 3
NEG = -1.0e30
QPARTS = (0, 0, 0, 1, 1, 2)
KPARTS = (0, 1, 2, 0, 1, 0)
STACK = DH * len(QPARTS)
MPARTS = 2
LEAD = 6
HOLD = 6
TURN = 3


def cuts(a, z):
    return [(s, e) for s, e in ((a, min(z, SPLIT)), (max(a, SPLIT), z)) if s < e]


def foreground():
    s1, s2 = [], []
    for st, g in GROUPS:
        heads = HG if st == "A" else 1
        for i in range(NT):
            for h in range(heads):
                s1.append((EARLIEST[st, g](i * heads + h), (st, "s1", g, i, h)))
                s2.append([(st, "s2", g, i, h)])
                if h == heads // 2 and i:
                    s2[-1].append((st, "pv", g, i - 1))
        s2[-1] += [(st, "pv", g, NT - 1), (st, "yt", g)]
    out, waiting = [], []

    def take(unit):
        out.append(unit)
        if unit[1] in ("s1", "s2"):
            for w in waiting:
                w[0] -= 1
            if unit[1] == "s1" and unit[3:] == (NT - 1, HG - 1 if unit[0] == "A" else 0):
                waiting.append([TURN, unit])
        while waiting and waiting[0][0] <= 0:
            st, _, g = waiting.pop(0)[1][:3]
            out.extend([(st, "mt", g), (st, "md", g)])
    for n, group in enumerate(s2):
        while s1 and s1[0][0] <= n:
            take(s1.pop(0)[1])
        for unit in group:
            take(unit)
    return out


GROUPS = [("A", 0), ("A", 1), ("F", 0), ("F", 1), ("F", 2), ("A", 2)]
SLOT = (0, 1, 1)
A1_AT, F_AT, A2_AT = HG * NT, 2 * HG * NT, 2 * HG * NT + E * NT
EARLIEST = {("A", 0): lambda k: 0, ("A", 1): lambda k: max(0, k - LEAD),
            ("F", 0): lambda k: A1_AT + k, ("F", 1): lambda k: A1_AT + 6 + k, ("F", 2): lambda k: A1_AT + 12 + k,
            ("A", 2): lambda k: F_AT + HOLD + k * (E * NT - HOLD - 3) // (HG * NT)}


def background():
    f = [(0, ("F", "mo")), (1, ("F", "rs")), (6, ("F", "no")), (1, ("F", "bo"))]
    f += [(5, ("F", "n2", 0)), (0, ("F", "n2", 1))]
    for n in range(2 * E):
        f += [(3 if n == 0 else 1, ("F", "fq", n))]
        if n == 0:
            f += [(0, ("F", "cv"))]
        else:
            f += [(1, ("F", "hi", n)), (0, ("F", "lo", n))]
        if n == E:
            f += [(0, ("F", "cq")), (1, ("F", "hi", 0)), (0, ("F", "lo", 0))]
    f += [(1, ("F", "vg", t)) for t in range(NT // 2)]
    f += [(1, ("F", "ga")), (1, ("F", "gp")), (3, ("F", "g1")), (1, ("F", "e1")), (2, ("F", "g2")),
          (1, ("F", "e2")), (2, ("F", "g3"))]
    m = [(0, ("M", "xt", 0)), (1, ("M", "xt", 1)), (0, ("M", "pad"))]
    m += [(2 if k == 0 else 1, ("M", "xe", k)) for k in range(MI)]
    for k in range(MI):
        m += [(1, ("M", "cv", k))]
        if k:
            m += [(1, ("M", "th", k - 1)), (1, ("M", "h", k - 1))]
    m += [(1, ("M", "th", MI - 1)), (1, ("M", "h", MI - 1))]
    for k in range(MI):
        m += [(2, ("M", "xg", k)), (2, ("M", "zg", k)), (0, ("M", "g", k))]
    m += [(4 if t == 0 else 1, ("M", "y", t)) for t in range(NT // 2)]
    m += [(1, ("M", "m0")), (0, ("M", "r0")), (8, ("M", "n0")), (0, ("M", "ro")), (5, ("M", "m1")), (0, ("M", "r1")),
          (5, ("M", "n1")), (3, ("M", "nt", 0)), (0, ("M", "nt", 1))]
    for n in range(2 * NK):
        m += [(2 if n == 0 else 1, ("M", "qk", n)), (1, ("M", "sp", n)), (0, ("M", "pw", n))]
    m += [(2, ("M", "ld", 0))]
    return f, m


F_SPAN = (12, 80)
M_SPAN = (81, 226)
O_FROM = 12


def whole_pass():
    fg = foreground()
    places = []
    for bg, (a, z) in zip(background(), (F_SPAN, M_SPAN)):
        total = sum(w for w, _ in bg)
        c = 0
        for w, key in bg:
            c += w
            places.append((a + (z - a) * c / total, key))
    f_done = fg.index(("F", "yt", E - 1)) + O_FROM
    places += [(f_done + 2, ("F", "o2", k)) for k in range(NK)]
    places += [(f_done + 5 + 2 * t, ("F", "p2", t)) for t in range(NT // 2)] + [(f_done + 10, ("F", "st"))]
    places.sort(key=lambda x: x[0])
    out = [("M", "x"), ("A", "b0")]
    for n, key in enumerate(fg):
        while places and places[0][0] <= n:
            out.append(places.pop(0)[1])
        out.append(key)
        if key == ("A", "s2", 1, NT - 1, HG - 1):
            out.append(("A", "ld", 2))
    out += [k for _, k in places]
    out += [("M", "ld", 1)] + [("M", "v", t) for t in range(NT // 2)]
    out += [("A", "ot", k) for k in range(NK)] + [("A", "p", t) for t in range(NT // 2)]
    at = {k: n for n, k in enumerate(out)}
    assert max(at["F", "lo", 2 * E - 1], at["F", "vg", NT // 2 - 1]) < at["M", "xt", 0]
    assert at["A", "md", NG - 1] < at["M", "pw", 0] and at["A", "pv", NG - 1, NT - 1] < at["M", "v", 0]
    assert at["A", "s2", 0, NT - 1, HG - 1] < at["M", "ld", 0] and at["A", "s1", 2, 0, 0] > at["A", "ld", 2]
    assert at["F", "g3"] < at["F", "yt", 0] and at["F", "lo", 2 * E - 1] < at["F", "s1", 0, 0, 0]
    return out


MID = whole_pass()
PROLOGUE = [k for k in MID if k[0] == "M"]
FIRST = [k for k in MID if k[0] != "F"]
LAST = [k for k in MID if k[0] != "M"]
EPILOGUE = [k for k in MID if k[0] == "F"]

EMPTIER = {("M", n): "act" for n in ("xt", "xe", "y", "nt", "qk")}
EMPTIER |= {("M", n): "dve" for n in ("xg", "zg", "v")}
EMPTIER |= {("A", n): "dve" for n in ("s1", "mt", "yt", "p")}
EMPTIER |= {("A", n): "act" for n in ("s2", "ot")}
EMPTIER |= {("F", n): "dve" for n in ("vg", "s1", "mt", "yt", "p2")}
EMPTIER |= {("F", n): "act" for n in ("n2", "fq", "s2", "o2")}


def in_ring(k):
    return k[:2] in EMPTIER


UNITS = {st: [k for k in MID if k[0] == st and in_ring(k)] for st in "MAF"}
FILL_AT = {k: n + 1 for ks in UNITS.values() for n, k in enumerate(ks)}
EMPTY_AT, EMPTY_PER = {}, {}
for _st in "MAF":
    for _e in ("act", "dve"):
        _ks = [k for k in UNITS[_st] if EMPTIER[k[:2]] == _e]
        EMPTY_AT |= {k: n + 1 for n, k in enumerate(_ks)}
        EMPTY_PER[_st, _e] = len(_ks)


LO_ORDER = [k[2] for k in MID if k[:2] == ("F", "lo")]
LO_AT = {n: sum(2 if m < E else 1 for m in LO_ORDER[:c + 1]) for c, n in enumerate(LO_ORDER)}
HI_AT = {k: c + 1 for c, k in enumerate(k for k in MID if k[:2] in (("F", "hi"), ("F", "cq")))}


class Tally:

    def __init__(self, sem, per, start=0):
        self.sem, self.per, self.start = sem, per, start

    def at(self, b, k):
        i, off = b
        return self.sem, i * self.per + (off * self.per + self.start + k)


class Pass:

    def __init__(self, order, i):
        self.order = order
        self.first = order is PROLOGUE
        self.b = {"M": (i, 2), "A": (i, 1), "F": (i, 0)}
        self.stages = {k[0] for k in order}
        self.groups = [g for g in GROUPS if g[0] in self.stages]
        self.products = [k for k in order if k[1] == "pv"]
        units = [k for k in order if in_ring(k)]
        self.slot = {k: n % RING for n, k in enumerate(units)}
        self.old = {k: units[n - RING] for n, k in enumerate(units) if n >= RING}


O_IN = 0
O_QK = O_IN + DI
O_V = O_QK + 2 * D
O_PROJ = O_V + D
O_FQK = O_PROJ + D
O_VG = O_FQK + 2 * E * 128
O_WP = O_VG + D + GH
W96 = O_WP + D
O_X = 0
O_Z = O_X + DI
O_OUT = O_Z + DI
W128 = O_OUT + D
C_CONV = 0
C_QK = C_CONV + MI * (TAPS + 1)
C_FQK = C_QK + 2 * NK
C_FB = C_FQK + 2 * E
C_FC = C_FB + E + 1
COLS = C_FC + 3
R_GAMMA = 0
R_BETA = R_GAMMA + D
R_BV = R_BETA + D
R_BPROJ = R_BV + D
R_BV2 = R_BPROJ + D
R_BG1 = R_BV2 + D
R_BP = R_BG1 + GH
R_WG2 = R_BP + D
R_BG2 = R_WG2 + E * GH
ROWS = R_BG2 + E
N_CONSTS = 4
CONSTS = (-0.5, 0.5, -1.0, D / (D - 1.0), 1e-6, 1e-5)
NSTAT = 2 * NT + 1


def audio_tower(nc, x, w96, w128, cols, rows, out):
    with ExitStack() as ctx:
        def sb(name, shape, dt=F32):
            return ctx.enter_context(nc.sbuf_tensor(name, shape, dt))

        def sem(name):
            return ctx.enter_context(nc.semaphore(name))

        def tally(name, per, start=0):
            return Tally(sem(name), per, start)

        W = sb("W", [KH, NK, W96])
        W3 = sb("W3", [128, MI, W128])
        Cc = sb("Cc", [128, COLS])
        R = sb("R", [P, ROWS])
        idf = sb("idf", [128, 128])
        idb = sb("idb", [128, 128], BF16)
        mask_q = sb("mask_q", [P, P + 1], BF16)
        mask_k = sb("mask_k", [P, P + 1], BF16)
        expo = sb("expo", [P, len(CONSTS), NT])
        qb4 = sb("qb4", [KH, NK])
        fb8 = sb("fb8", [128, E + 1])
        xin = sb("xin", [P, NT, D])
        stats = sb("stats", [P, 3, NT, 6])
        mv = sb("mv", [P, 3, NT, 2])
        begun = sb("begun", [P, 3])
        va = sb("va", [P, 3, NT])
        sd = sb("sd", [P, NT])
        sde = sb("sde", [P, NT])
        rs = sb("rs", [P, 3, NT])
        h0b = sb("h0b", [P, NT, D])
        h1 = sb("h1", [P, NT, D])
        qs = sb("qs", [STACK + MPARTS, 2, HG, T], BF16)
        ks = sb("ks", [STACK + MPARTS, 2, HG, T], BF16)
        va_ = sb("vaug", [P, NT, H, VS])
        m3 = sb("m3", [P, 2, KH])
        mb = sb("mb", [P, HG * NT], BF16)
        mrow = sb("mrow", [MPARTS * HG * NT, P], BF16)
        yna = sb("yna", [P, NT, D])
        pt = sb("pt", [P, 2, HG, T])
        ysb = sb("ysb", [128, 2, T])
        rl = sb("rl", [P, NT, HG])
        yT = sb("yT", [KH, NK, T])
        qa = sb("qa", [128, E, T], F32R)
        qb = sb("qb", [KH, E, T], F32R)
        ka = sb("ka", [128, E, T], F32R)
        kb = sb("kb", [KH, E, T], F32R)
        v2 = sb("v2", [P, NT, E, HD + 1])
        gt = sb("gt", [P, 2, NT, GH])
        gm = sb("gm", [P, E, NT, GH])
        z = sb("z", [P, 12, NT, E])
        zs = sb("zs", [P, 8, NT])
        mf = sb("mf", [P, 2, KH])
        mfr = sb("mfr", [P, NT], F32R)
        mfrow = sb("mfrow", [2 * NT, P], F32R)
        wl = sb("wl", [P, 2, NT])
        ynf = sb("ynf", [P, NT, D])
        def over(tensors):
            with ExitStack() as stage:
                return [stage.enter_context(nc.sbuf_tensor(n, s, dt)) for n, s, dt in tensors]
        hn2, nT2, f0, qc, ff = over([("hn2", [P, NT, D], F32), ("nT2", [KH, NK, T], F32),
                                     ("f0", [128, T + 2], F32),
                                     ("qc", [128, T], F32), ("ff", [128, E, T], F32)])
        xe, cv, sg, tg = over([("xe", [128, MI, T + TAPS - 1], F32),
                               ("cv", [128, MI, T], F32), ("sg", [128, 2, T], F32), ("tg", [128, 2, T], F32)])
        gT, _, _, xT = over([("gT", [128, MI, T + TAPS - 1], F32), ("space1", [128, MI, T], F32),
                             ("space2", [128, 2, T], F32), ("xT", [KH, NK, T], F32)])
        _, y, t1, hn = over([("space3", [128, MI, T + TAPS - 1], F32), ("y", [P, NT, D], F32),
                             ("t1", [P, NT, D], F32), ("hn", [P, NT, D], F32)])
        nT, f, fr, parts, h0 = over([("nT", [KH, NK, T], F32), ("f", [KH, 2, T], F32), ("fr", [KH, T], F32),
                                     ("parts", [KH, 2, 3, T], BF16), ("h0", [P, NT, D], F32)])
        stackd = nc.dram_tensor("stackd", [2, 3, NK, KH, T], BF16, kind="Internal").ap()
        rowsd = nc.dram_tensor("rowsd", [NG, MPARTS * HG * NT, P], BF16, kind="Internal").ap()
        rowsf = nc.dram_tensor("rowsf", [E, 2 * NT, P], F32, kind="Internal").ap()

        ps = [ctx.enter_context(nc.psum_tensor(f"ps{n}", [128, 1024], F32)) for n in range(RING)]
        acc = ctx.enter_context(nc.psum_tensor("acc", [128, 1024], F32))

        w_in = sem("w_in")
        w_all = sem("w_all")
        consts = sem("consts")
        scaled = sem("scaled")
        made = sem("made")
        zeroed = sem("zeroed")
        filled = {st: tally(f"filled_{st}", len(UNITS[st])) for st in "MAF"}
        emptied = {se: tally("emptied_%s_%s" % se, n) for se, n in EMPTY_PER.items()}
        x_in = tally("x_in", 16)
        padded = tally("padded", 1)
        tap = tally("tap", MI * TAPS)
        tanhs = tally("tanhs", 3 * MI)
        mixed = tally("mixed", MI)
        gated = tally("gated", MI)
        stat = {n: tally(f"stat{n}", NSTAT) for n in range(3)}
        var = {n: tally(f"var{n}", k) for n, k in enumerate((4, 2, 2))}
        normed = {n: tally(f"normed{n}", 1) for n in range(3)}
        affine = tally("affine", 2)
        split = tally("split", 4 * 2 * NK)
        stack_w = [tally(f"stack_w{n}", 16) for n in range(2 * NK)]
        stack_r = [tally(f"stack_r{g}", 16 * 2 * len(QPARTS)) for g in range(NG)]
        h0b_ok = tally("h0b_ok", 1)
        msplit = tally("msplit", 2 * NG)
        mrow_w = [tally(f"mrow_w{g}", 16) for g in range(NG)]
        mrows = [tally(f"mrows{g}", 16) for g in range(NG)]
        rl_a = tally("rl_a", NG)
        pv_done = {"A": tally("pv_done_A", NG * NT), "F": tally("pv_done_F", E * NT)}
        y_out = {"A": tally("y_out_A", NG), "F": tally("y_out_F", E)}
        h1b_ok = tally("h1b_ok", 1)
        padded_f = tally("padded_f", 1)
        fconv = tally("fconv", 3)
        hi = tally("hi", len(HI_AT))
        lo = tally("lo", 3 * E)
        vg_ok = tally("vg_ok", NT // 2)
        gate_p = tally("gate_p", E)
        relu = tally("relu", 1)
        gate_v = tally("gate_v", 16)
        gate_a = tally("gate_a", 2)
        mfsplit = tally("mfsplit", 2 * E)
        mfrow_w = [tally(f"mfrow_w{e}", 16) for e in range(E)]
        mfrows = [tally(f"mfrows{e}", 16) for e in range(E)]
        rl_f = tally("rl_f", 2 * E)
        stored = tally("stored", 32, 32)

        block = ctx.enter_context(nc.Block())

        def ring(p, key):
            return ps[p.slot[key]]

        def filled_at(p, key):
            return filled[key[0]].at(p.b[key[0]], FILL_AT[key])

        def emptied_at(p, key):
            return emptied[key[0], EMPTIER[key[:2]]].at(p.b[key[0]], EMPTY_AT[key])

        def free_at(p, key):
            return emptied_at(p, p.old[key])

        def one(ap, b):
            i, off = b
            return ap[i + off:i + off + 1] if isinstance(i, int) else ap[off:][bass.ds(i, 1)]

        def passes(eng, run):
            run(Pass(PROLOGUE, -2), None)
            run(Pass(FIRST, -1), Pass(PROLOGUE, -2))
            with eng.Fori(0, B - 2) as i:
                run(Pass(MID, i), Pass(MID, i - 1))
            run(Pass(LAST, B - 2), Pass(MID, B - 3))
            run(Pass(EPILOGUE, B - 1), Pass(LAST, B - 2))

        M_END = ("M", "v", NT // 2 - 1)
        A_END = ("A", "p", NT // 2 - 1)
        F_END = ("F", "p2", NT // 2 - 1)

        @block.sync
        def _(sp):
            sp.dma_start(W[:, :, 0:DI], w96[:, :, 0:DI]).then_inc(w_in, 16)
            sp.dma_start(Cc[:, :], cols).then_inc(w_in, 16)

            def run(p, before):
                for key in p.order:
                    st, what = key[:2]
                    b = p.b[st]
                    if key == ("M", "x"):
                        if before:
                            sp.wait_ge(*filled_at(before, ("M", "xt", NK - 1)))
                        if "F" in p.stages:
                            sp.wait_ge(*stored.at(p.b["F"], 0))
                        sp.dma_start(xin[:, :, :], one(x, b).rearrange("o (n p) d -> p (o n) d", p=P)
                                     ).then_inc(x_in.sem, 16)
                    elif what == "pw":
                        n = key[2]
                        sp.wait_ge(*split.at(b, 4 * (n + 1)))
                        sp.dma_start(stackd[n // NK, :, n % NK].rearrange("a p t -> p a t"), parts[:, n % 2, :, :]
                                     ).then_inc(stack_w[n].sem, 16)
                    elif what == "ld":
                        g = key[2]
                        if st == "M":
                            if "A" in p.stages:
                                sp.wait_ge(*filled_at(p, ("A", "s2", (0, NG - 1)[g], NT - 1, HG - 1)))
                            if g == 0:
                                for n in range(2 * NK):
                                    sp.wait_ge(*stack_w[n].at(b, 16))
                        else:
                            sp.wait_ge(*filled_at(p, ("A", "s2", 1, NT - 1, HG - 1)))
                        for side, (dst, order) in enumerate(((qs, QPARTS), (ks, KPARTS))):
                            for r, part in enumerate(order):
                                sp.dma_start(dst[r * DH:(r + 1) * DH, SLOT[g], :, :],
                                             stackd[side, part].rearrange("k (h i) t -> i (k h) t", i=DH)[
                                                 :, HG * g:HG * (g + 1), :]).then_inc(stack_r[g].sem, 16)
                    elif what == "md":
                        g = key[2]
                        sp.wait_ge(*emptied_at(p, (st, "mt", g)))
                        if st == "A":
                            sp.dma_start(rowsd[g], mrow[:, :]).then_inc(mrow_w[g].sem, 16)
                            sp.wait_ge(*mrow_w[g].at(b, 16))
                            sp.dma_start(qs[STACK:STACK + MPARTS, SLOT[g], :, :],
                                         rowsd[g].rearrange("(a h t) c -> a h (t c)", a=MPARTS, h=HG)
                                         ).then_inc(mrows[g].sem, 16)
                        else:
                            sp.dma_start(rowsf[g], mfrow[:, :].bitcast(F32)).then_inc(mfrow_w[g].sem, 16)
                            sp.wait_ge(*mfrow_w[g].at(b, 16))
                            sp.dma_start(qb[HD:HD + 2, g, :].bitcast(F32), rowsf[g].rearrange("(a t) c -> a (t c)", a=2)
                                         ).then_inc(mfrows[g].sem, 16)
                    elif what == "st":
                        sp.wait_ge(*emptied_at(p, F_END))
                        sp.dma_start(one(out, b)[:, 0:P * (NT - 1), :].rearrange("o (n p) d -> p (o n) d", p=P),
                                     xin[:, 0:NT - 1, :]).then_inc(stored.sem, 16)
                        sp.dma_start(one(out, b)[:, P * (NT - 1):T - 1, :].rearrange("o (n p) d -> p (o n) d", p=P - 1),
                                     xin[0:P - 1, NT - 1:NT, :]).then_inc(stored.sem, 16)
                    if p.first and key == ("M", "x"):
                        sp.dma_start(W3[:, :, :], w128).then_inc(w_all, 16)
                        sp.dma_start(R[:, :], rows).then_inc(w_all, 16)
                        sp.dma_start(W[:, :, DI:W96], w96[:, :, DI:W96]).then_inc(w_all, 16)

            passes(sp, run)
            sp.wait_ge(stored.sem, 32 * (B + 1))

        @block.tensor
        def _(pe):
            def turn(p, key, src):
                d = ring(p, key)
                for i in range(NT):
                    c = C0 + P * i
                    mm = nc.tensor.transpose(d[0:KH, c:c + P], src[:, i, :], idf[0:P, 0:P])
                return mm

            def by_feature(p, key, w, src, m):
                d = ring(p, key)
                n = len(w)
                for s, e in cuts(0, T):
                    for k in range(n):
                        mm = nc.tensor.matmul(d[0:m, C0 + s:C0 + e], w[k], src[k][:, s:e],
                                              start=(k == 0), stop=(k == n - 1))
                return mm

            def by_token(p, key, src, w, width):
                d = ring(p, key)
                n = len(w)
                for o in range(2):
                    i = 2 * key[2] + o
                    for k in range(n):
                        mm = nc.tensor.matmul(d[0:P, 512 * o:512 * o + width], src[k][:, P * i:P * (i + 1)], w[k],
                                              start=(k == 0), stop=(k == n - 1))
                return mm

            def maxima_scores(d, st, g, i, h):
                z0 = P * (i + 1)
                if st == "F":
                    z0 += z0 % 2
                for s, e in cuts(0, z0):
                    diag = e == z0
                    if st == "A":
                        nc.tensor.matmul(d[0:P, C0 + s:C0 + e], qs[0:STACK, SLOT[g], h, P * i:P * (i + 1)],
                                         ks[0:STACK, SLOT[g], h, s:e], start=True, stop=not diag)
                    else:
                        nc.tensor.matmul(d[0:P, C0 + s:C0 + e], qa[:, g, P * i:P * (i + 1)],
                                         ka[:, g, s:e], start=True, stop=not diag)
                return nc.tensor.matmul(d[0:P, C0 + P * i:C0 + z0], idb[0:P, 0:P],
                                        mask_q[:, 0:z0 - P * i], start=False, stop=True)

            def scores(d, st, g, i, h):
                a0 = P * i
                if st == "F":
                    a0 -= a0 % 2
                for s, e in cuts(a0, T):
                    diag = s == a0
                    dst = d[0:P, C0 + s:C0 + e]
                    if st == "A":
                        mm = nc.tensor.matmul(dst, ks[:, SLOT[g], h, P * i:P * (i + 1)], qs[:, SLOT[g], h, s:e],
                                              start=True, stop=not diag)
                    else:
                        nc.tensor.matmul(dst, ka[:, g, P * i:P * (i + 1)], qa[:, g, s:e],
                                         start=True, stop=False)
                        mm = nc.tensor.matmul(dst, kb[:, g, P * i:P * (i + 1)], qb[:, g, s:e],
                                              start=False, stop=not diag)
                    if diag:
                        mm = nc.tensor.matmul(d[0:P, C0 + a0:C0 + P * (i + 1)], idb[0:P, 0:P],
                                              mask_k[:, 1 - (P * i - a0):P + 1], start=False, stop=True)
                return mm

            def times_values(st, g, i):
                for s, e in cuts(P * i, T):
                    for h in range(HG if st == "A" else 1):
                        if st == "A":
                            w, m0, m1 = va_[:, i, HG * g + h, :], VS * h, VS * (h + 1)
                        else:
                            w, m0, m1 = v2[:, i, g, :], 0, HD + 1
                        mm = nc.tensor.matmul(acc[m0:m1, C0 + s:C0 + e], w, pt[:, i % 2, h, s:e],
                                              start=(i == 0), stop=(P * (i + 1) == e))
                return mm

            def result_turn(d, st, g):
                m = 128 if st == "A" else HD + 1
                for t in range(NT):
                    c = 512 * (t // 3) + 128 * (t % 3)
                    mm = nc.tensor.transpose(d[0:P, c:c + m], ysb[0:m, GROUPS.index((st, g)) % 2, P * t:P * (t + 1)],
                                             idf[0:m, 0:m])
                return mm

            def wk(o, n):
                return [W[:, k, o:o + n] for k in range(NK)]

            def tiles_of(t, n=NK):
                return [t[:, k, :] for k in range(n)]

            def run(p, before):
                if before:
                    pe.wait_ge(*emptied_at(before, M_END if "A" not in before.stages else A_END))
                for key in p.order:
                    st, what = key[:2]
                    b = p.b[st]
                    n = key[2] if len(key) > 2 else None
                    if in_ring(key) and key in p.old:
                        pe.wait_ge(*free_at(p, key))
                    if what == "xt":
                        pe.wait_ge(*x_in.at(b, 16))
                        mm = turn(p, key, xin[:, :, KH * n:KH * (n + 1)])
                    elif what == "xe":
                        pe.wait_ge(*emptied_at(p, ("M", "xt", NK - 1)))
                        mm = by_feature(p, key, wk(O_IN + 128 * n, 128), tiles_of(xT), 128)
                    elif what in ("xg", "zg"):
                        if p.first:
                            pe.wait_ge(w_all, 48)
                        pe.wait_ge(*mixed.at(b, MI))
                        o = 128 * n + (O_X if what == "xg" else O_Z)
                        mm = by_feature(p, key, [W3[:, k, o:o + 128] for k in range(MI)], tiles_of(cv, MI), 128)
                    elif what == "y":
                        pe.wait_ge(*gated.at(b, MI))
                        mm = by_token(p, key, [gT[:, k, 0:T] for k in range(MI)], [W3[:, k, O_OUT:O_OUT + D] for k in range(MI)], D)
                    elif what == "nt":
                        pe.wait_ge(*normed[1].at(b, 1))
                        mm = turn(p, key, hn[:, :, KH * n:KH * (n + 1)])
                    elif what == "qk":
                        pe.wait_ge(*emptied_at(p, ("M", "nt", NK - 1)))
                        mm = by_feature(p, key, wk(O_QK + KH * n, KH), tiles_of(nT), KH)
                    elif what == "v":
                        mm = by_token(p, key, tiles_of(nT), wk(O_V, D), D)
                    elif what == "s1":
                        if key[3:] == (0, 0):
                            if st == "A":
                                pe.wait_ge(*stack_r[n].at(b, stack_r[n].per))
                            else:
                                pe.wait_ge(*hi.at(b, max(HI_AT[k] for k in HI_AT if k[-1] in (n, n + E))))
                                pe.wait_ge(*lo.at(b, max(LO_AT[n], LO_AT[n + E])))
                        mm = maxima_scores(ring(p, key), *(key[:1] + key[2:]))
                    elif what == "mt":
                        if st == "A":
                            pe.wait_ge(*msplit.at(b, 2 * (n + 1)))
                            mm = nc.tensor.transpose(ring(p, key)[0:KH, C0:C0 + P], m3[:, n % 2, :], idf[0:P, 0:P])
                        else:
                            pe.wait_ge(*mfsplit.at(b, 2 * (n + 1)))
                            mm = nc.tensor.transpose(ring(p, key)[0:KH, C0:C0 + P], mf[:, n % 2, :], idf[0:P, 0:P])
                    elif what == "s2":
                        if key[3:] == (0, 0):
                            if st == "A":
                                pe.wait_ge(*mrows[n].at(b, 16))
                            else:
                                pe.wait_ge(*mfrows[n].at(b, 16))
                        mm = scores(ring(p, key), *(key[:1] + key[2:]))
                    elif what == "pv":
                        if key[3] == 0:
                            at = p.groups.index((st, n))
                            if at:
                                other, g = p.groups[at - 1]
                                pe.wait_ge(*y_out[other].at(p.b[other], g + 1))
                            if st == "A" and n == 0:
                                pe.wait_ge(*emptied[("M", "dve")].at(b, EMPTY_AT["M", "v", NT // 2 - 1]))
                            if st == "F" and n == 0:
                                pe.wait_ge(*emptied_at(p, ("F", "vg", NT // 2 - 1)))
                        pe.wait_ge(*emptied_at(p, (st, "s2", n, key[3], HG - 1 if st == "A" else 0)))
                        times_values(st, n, key[3]).then_inc(pv_done[st].sem, 1)
                    elif what == "yt":
                        pe.wait_ge(*y_out[st].at(b, n + 1))
                        mm = result_turn(ring(p, key), st, n)
                    elif what == "ot":
                        pe.wait_ge(*emptied_at(p, ("A", "yt", NG - 1)))
                        mm = turn(p, key, yna[:, :, KH * n:KH * (n + 1)])
                    elif what == "p":
                        pe.wait_ge(*emptied_at(p, ("A", "ot", NK - 1)))
                        mm = by_token(p, key, tiles_of(yT), wk(O_PROJ, D), D)
                    elif what == "n2":
                        pe.wait_ge(*normed[2].at(b, 1))
                        mm = turn(p, key, hn2[:, :, KH * n:KH * (n + 1)])
                    elif what == "fq":
                        pe.wait_ge(*emptied_at(p, ("F", "n2", NK - 1)))
                        mm = by_feature(p, key, wk(O_FQK + 128 * n, 128), tiles_of(nT2), 128)
                    elif what == "vg":
                        mm = by_token(p, key, tiles_of(nT2), wk(O_VG, D + GH), D + GH)
                    elif what == "o2":
                        pe.wait_ge(*emptied_at(p, ("F", "yt", E - 1)))
                        mm = turn(p, key, ynf[:, :, KH * n:KH * (n + 1)])
                    elif what == "p2":
                        pe.wait_ge(*emptied_at(p, ("F", "o2", NK - 1)))
                        mm = by_token(p, key, tiles_of(yT), wk(O_WP, D), D)
                    if in_ring(key):
                        mm.then_inc(filled[st].sem, 1)

            pe.wait_ge(consts, N_CONSTS)
            pe.wait_ge(zeroed, 6)
            pe.wait_ge(w_in, 32)
            passes(pe, run)

        @block.scalar
        def _(act):
            def run(p, before):
                def row(key, m=128):
                    return ring(p, key)[0:m, C0:C0 + T]

                for key in p.order:
                    st, what = key[:2]
                    b = p.b[st]
                    n = key[2] if len(key) > 2 else None
                    if in_ring(key) and EMPTIER[key[:2]] == "act":
                        act.wait_ge(*filled_at(p, key))
                    if what == "xt":
                        if n == 0:
                            if before:
                                for k in range(2 * NK):
                                    act.wait_ge(*stack_w[k].at(p.b["A"], 16))
                                act.wait_ge(*h0b_ok.at(p.b["A"], 1))
                            if "F" in p.stages:
                                act.wait_ge(*lo.at(p.b["F"], lo.per))
                        ins = nc.scalar.activation(xT[:, n, :], row(key, KH), ACT.Copy)
                    elif what == "xe":
                        ins = nc.scalar.activation(xe[:, n, 1:1 + T], row(key), ACT.Copy)
                    elif what == "th":
                        act.wait_ge(*tap.at(b, TAPS * (n + 1)))
                        if n >= 2:
                            act.wait_ge(*mixed.at(b, n - 1))
                        nc.scalar.activation(tg[:, n % 2, :], cv[:, n, :], ACT.Tanh, scale=0.5
                                             ).then_inc(tanhs.sem, 1)
                    elif what in ("xg", "zg"):
                        act.wait_ge(*filled_at(p, key))
                        if n:
                            act.wait_ge(*emptied_at(p, ("M", what, n - 1)))
                        elif what == "xg":
                            act.wait_ge(*mixed.at(b, MI))
                        nc.scalar.activation(tg[:, what == "zg", :], row(key), ACT.Tanh, scale=0.25
                                             ).then_inc(tanhs.sem, 1)
                    elif what == "y":
                        ins = nc.scalar.activation(y[:, 2 * n:2 * n + 2, :],
                                                   ring(p, key)[0:P, :].rearrange("p (o c) -> p o c", o=2)[:, :, 0:D],
                                                   ACT.Copy, scale=1 / 16)
                    elif what == "nt":
                        ins = nc.scalar.activation(nT[:, n, :], row(key, KH), ACT.Copy)
                    elif what == "qk":
                        if n >= 2:
                            act.wait_ge(*split.at(b, 4 * (n - 1)))
                        if n < NK:
                            ins = nc.scalar.activation(f[:, n % 2, :], row(key, KH), ACT.Identity,
                                                       bias=qb4[:, n:n + 1], scale=DH ** -0.5)
                        else:
                            ins = nc.scalar.activation(f[:, n % 2, :], row(key, KH), ACT.Identity,
                                                       bias=Cc[0:KH, C_QK + n:C_QK + n + 1])
                    elif what == "s2":
                        i, h = key[3:]
                        if h == 0:
                            at = p.products.index((st, "pv", n, i)) - 2
                            if at >= 0:
                                other, _, g, j = p.products[at]
                                act.wait_ge(*pv_done[other].at(p.b[other], g * NT + j + 1))
                        a0 = P * i
                        if st == "F":
                            a0 -= a0 % 2
                        ins = nc.scalar.activation(pt[:, i % 2, h, a0:T], ring(p, key)[0:P, C0 + a0:C0 + T], ACT.Exp)
                    elif what == "pv" and key[3] == NT - 1:
                        m = 128 if st == "A" else HD + 1
                        at = GROUPS.index((st, n))
                        act.wait_ge(*pv_done[st].at(b, (n + 1) * NT))
                        for other, g in [o for o in GROUPS[:at] if o in p.groups and (GROUPS.index(o) - at) % 2 == 0][-1:]:
                            act.wait_ge(*filled_at(p, (other, "yt", g)))
                        nc.scalar.activation(ysb[0:m, at % 2, :], acc[0:m, C0:C0 + T], ACT.Copy
                                             ).then_inc(y_out[st].sem, 1)
                    elif what in ("ot", "o2"):
                        if what == "ot" and "F" in p.stages:
                            act.wait_ge(*filled_at(p, F_END))
                        ins = nc.scalar.activation(yT[:, n, :], row(key, KH), ACT.Copy)
                    elif what == "n2":
                        ins = nc.scalar.activation(nT2[:, n, :], row(key, KH), ACT.Copy)
                    elif what == "fq":
                        if n == 0:
                            if "A" in p.stages:
                                for k in range(2 * NK):
                                    act.wait_ge(*stack_w[k].at(p.b["A"], 16))
                                act.wait_ge(*h0b_ok.at(p.b["A"], 1))
                            ins = nc.scalar.activation(f0[:, 1:T], row(key)[:, 0:T - 1], ACT.Identity,
                                                       bias=Cc[:, C_FQK:C_FQK + 1])
                        else:
                            if n > E:
                                act.wait_ge(*lo.at(b, LO_AT[n - E]))
                            if n < E:
                                ins = nc.scalar.activation(ff[:, n % E, :], row(key), ACT.Identity,
                                                           bias=fb8[:, n:n + 1], scale=HD ** -0.5)
                            else:
                                ins = nc.scalar.activation(ff[:, n % E, :], row(key), ACT.Identity,
                                                           bias=Cc[:, C_FQK + n:C_FQK + n + 1])
                    elif what == "hi":
                        if n:
                            act.wait_ge(*emptied_at(p, ("F", "fq", n)))
                        else:
                            act.wait_ge(*hi.at(b, HI_AT["F", "cq"]))
                        nc.scalar.activation((qa if n < E else ka)[:, n % E, :], ff[:, n % E, :], ACT.Copy
                                             ).then_inc(hi.sem, 1)
                    elif what == "cq":
                        act.wait_ge(*fconv.at(b, 3))
                        act.wait_ge(*lo.at(b, LO_AT[E]))
                        nc.scalar.activation(ff[:, 0, :], qc[:, :], ACT.Identity, bias=fb8[:, E:E + 1],
                                             scale=HD ** -0.5).then_inc(hi.sem, 1)
                    elif what == "ga":
                        act.wait_ge(*vg_ok.at(b, NT // 2))
                        nc.scalar.activation(gt[:, 1], gt[:, 0], ACT.Relu).then_inc(relu.sem, 1)
                    elif what == "e1":
                        act.wait_ge(*gate_v.at(b, 4))
                        nc.scalar.activation(z[:, 1], z[:, 11], ACT.Exp).then_inc(gate_a.sem, 1)
                    elif what == "e2":
                        act.wait_ge(*gate_v.at(b, 7))
                        nc.scalar.activation(z[:, 3], z[:, 2], ACT.Exp).then_inc(gate_a.sem, 1)
                    if in_ring(key) and EMPTIER[key[:2]] == "act":
                        ins.then_inc(emptied[st, "act"].sem, 1)

            act.wait_ge(w_in, 32)
            act.wait_ge(scaled, 2)
            passes(act, run)

        @block.vector
        def _(dve):
            def tiles(ap):
                return ap.unsqueeze(1).to_broadcast([P, NT, ap.shape[-1]])

            def moments(b, n, src):
                for t in range(NT):
                    nc.vector.bn_stats(stats[:, n, t, :], src[:, t, :]).then_inc(stat[n].sem, 1)
                dve.wait_ge(*stat[n].at(b, NT))
                nc.vector.memset(begun[:, n:n + 1], 0.0).then_inc(stat[n].sem, 1)
                for t in range(NT):
                    nc.vector.bn_aggr(mv[:, n, t, :], stats[:, n, t:t + 1, :]).then_inc(stat[n].sem, 1)

            def normalise(n, dst, src):
                for t in range(NT):
                    last = nc.vector.tensor_scalar(dst[:, t, :], src[:, t, :], mv[:, n, t, 0:1], rs[:, n, t:t + 1],
                                                   ALU.subtract, ALU.mult)
                last.then_inc(normed[n].sem, 1)

            def gate(b, part):
                def step(k, ins):
                    ins.then_inc(gate_v.sem, 1)
                    if k not in (4, 7, 16):
                        dve.wait_ge(*gate_v.at(b, k))
                def over(ap):
                    return ap.unsqueeze(2).to_broadcast([P, NT, E])
                if part == "g1":
                    dve.wait_ge(*gate_p.at(b, E))
                    step(1, nc.vector.tensor_reduce(z[:, 0].rearrange("p t e -> p e t"), gm[:, :, :, :], AX.X, ALU.add))
                    step(2, nc.vector.tensor_tensor(z[:, 7], z[:, 0], tiles(R[:, R_BG2:R_BG2 + E]), ALU.add))
                    step(3, nc.vector.tensor_reduce(zs[:, 0], z[:, 7], AX.X, ALU.max))
                    step(4, nc.vector.tensor_tensor(z[:, 11], z[:, 7], over(zs[:, 0]), ALU.subtract))
                elif part == "g2":
                    dve.wait_ge(*gate_a.at(b, 1))
                    step(5, nc.vector.tensor_reduce(zs[:, 1], z[:, 1], AX.X, ALU.add))
                    step(6, nc.vector.reciprocal(zs[:, 2], zs[:, 1]))
                    step(7, nc.vector.tensor_tensor(z[:, 2], z[:, 1], over(zs[:, 2]), ALU.mult))
                else:
                    dve.wait_ge(*gate_v.at(b, 7))
                    q = [z[:, 2, :, e] for e in range(E)]
                    c = [zs[:, 3 + n] for n in range(5)]
                    nc.vector.tensor_tensor(c[0], q[0], q[1], ALU.is_lt)
                    nc.vector.tensor_tensor(c[1], q[0], q[2], ALU.is_lt)
                    nc.vector.tensor_tensor(c[2], q[1], q[0], ALU.is_le)
                    nc.vector.tensor_tensor(c[3], q[1], q[2], ALU.is_lt)
                    step(8, nc.vector.tensor_tensor(c[4], q[2], q[0], ALU.is_le))
                    nc.vector.tensor_tensor(z[:, 4, :, 0], c[0], c[1], ALU.mult)
                    nc.vector.tensor_tensor(z[:, 4, :, 1], c[2], c[3], ALU.mult)
                    step(9, nc.vector.tensor_tensor(z[:, 5, :, 0], q[2], q[1], ALU.is_le))
                    step(10, nc.vector.tensor_tensor(z[:, 4, :, 2], c[4], z[:, 5, :, 0], ALU.mult))
                    step(11, nc.vector.tensor_scalar(z[:, 6], z[:, 4], -1.0, 1.0, ALU.mult, ALU.add))
                    dve.wait_ge(*gate_a.at(b, 2))
                    step(12, nc.vector.tensor_tensor(z[:, 8], z[:, 3], z[:, 6], ALU.mult))
                    step(13, nc.vector.tensor_reduce(zs[:, 0], z[:, 8], AX.X, ALU.add))
                    step(14, nc.vector.reciprocal(zs[:, 1], zs[:, 0]))
                    step(15, nc.vector.tensor_tensor(z[:, 10], z[:, 8], over(zs[:, 1]), ALU.mult))
                    step(16, nc.vector.tensor_copy(z[:, 9, :, 0], zs[:, 0]))

            def run(p, before):
                def pair(key, w):
                    return ring(p, key)[0:P, :].rearrange("p (o c) -> p o c", o=2)[:, :, 0:w]

                for key in p.order:
                    st, what = key[:2]
                    b = p.b[st]
                    n = key[2] if len(key) > 2 else None
                    if in_ring(key) and EMPTIER[key[:2]] == "dve":
                        dve.wait_ge(*filled_at(p, key))
                    if what == "pad":
                        dve.wait_ge(*emptied_at(p, ("M", "xt", NK - 1)))
                        nc.vector.memset(xe[:, :, 0:1], 0.0)
                        nc.vector.memset(xe[:, :, T + 1:T + TAPS - 1], 0.0).then_inc(padded.sem, 1)
                    elif st == "M" and what == "cv":
                        dve.wait_ge(*emptied_at(p, ("M", "xe", n)))
                        dve.wait_ge(*padded.at(b, 1))
                        w = C_CONV + (TAPS + 1) * n
                        nc.vector.tensor_scalar(cv[:, n, :], xe[:, n, 0:T], Cc[:, w:w + 1],
                                                Cc[:, w + TAPS:w + TAPS + 1], ALU.mult, ALU.add).then_inc(tap.sem, 1)
                        for k in range(1, TAPS):
                            dve.wait_ge(*tap.at(b, TAPS * n + k))
                            nc.vector.scalar_tensor_tensor(cv[:, n, :], xe[:, n, k:k + T], Cc[:, w + k:w + k + 1],
                                                           cv[:, n, :], ALU.mult, ALU.add).then_inc(tap.sem, 1)
                    elif what == "h":
                        dve.wait_ge(*tanhs.at(b, n + 1))
                        nc.vector.scalar_tensor_tensor(cv[:, n, :], tg[:, n % 2, :], 1.0, cv[:, n, :],
                                                       ALU.add, ALU.mult).then_inc(mixed.sem, 1)
                    elif what in ("xg", "zg"):
                        o = what == "zg"
                        dve.wait_ge(*tanhs.at(b, MI + 2 * n + o + 1))
                        if o and n >= 2:
                            dve.wait_ge(*gated.at(b, n - 1))
                        ins = nc.vector.scalar_tensor_tensor(sg[:, n % 2, :] if o else gT[:, n, 0:T], tg[:, o, :], 1.0,
                                                             ring(p, key)[:, C0:C0 + T], ALU.add, ALU.mult)
                    elif what == "m0":
                        dve.wait_ge(*emptied_at(p, ("M", "y", NT // 2 - 1)))
                        moments(b, 0, y)
                    elif what == "n0":
                        dve.wait_ge(*var[0].at(b, 4))
                        normalise(0, t1, y)
                    elif what == "m1":
                        dve.wait_ge(*affine.at(b, 2))
                        moments(b, 1, h0)
                    elif what == "n1":
                        dve.wait_ge(*var[1].at(b, 2))
                        normalise(1, hn, h0)
                    elif what == "sp":
                        dve.wait_ge(*emptied_at(p, ("M", "qk", n)))
                        if n >= 2:
                            dve.wait_ge(*stack_w[n - 2].at(b, 16))
                        if n:
                            dve.wait_ge(*split.at(b, 4 * n))
                        nc.vector.tensor_copy(parts[:, n % 2, 0, :], f[:, n % 2, :]).then_inc(split.sem, 1)
                        dve.wait_ge(*split.at(b, 4 * n + 1))
                        nc.vector.tensor_tensor(fr[:, :], f[:, n % 2, :], parts[:, n % 2, 0, :], ALU.subtract
                                                ).then_inc(split.sem, 1)
                        dve.wait_ge(*split.at(b, 4 * n + 2))
                        nc.vector.tensor_copy(parts[:, n % 2, 1, :], fr[:, :]).then_inc(split.sem, 1)
                        dve.wait_ge(*split.at(b, 4 * n + 3))
                        nc.vector.tensor_tensor(parts[:, n % 2, 2, :], fr[:, :], parts[:, n % 2, 1, :], ALU.subtract
                                                ).then_inc(split.sem, 1)
                    elif what == "v":
                        if n == 0 and "A" in p.stages:
                            dve.wait_ge(*pv_done["A"].at(p.b["A"], NG * NT))
                        for o in range(2):
                            ins = nc.vector.tensor_tensor(
                                va_[:, 2 * n + o, :, 0:DH],
                                ring(p, key)[0:P, 512 * o:512 * o + D].rearrange("p (h c) -> p h c", c=DH),
                                R[:, R_BV:R_BV + D].rearrange("p (h c) -> p h c", c=DH), ALU.add)
                    elif what == "s1":
                        i, h = key[3:]
                        z0 = P * (i + 1)
                        z0 += z0 % 2 if st == "F" else 0
                        c = NT * h + i
                        dst = (m3 if st == "A" else mf)[:, n % 2, c:c + 1]
                        ins = nc.vector.tensor_reduce(dst, ring(p, key)[0:P, C0:C0 + z0], AX.X, ALU.max)
                    elif what == "mt":
                        if st == "A":
                            if n:
                                dve.wait_ge(*mrow_w[n - 1].at(b, 16))
                            ins = nc.vector.tensor_copy(mrow[:, :], ring(p, key)[0:MPARTS * HG * NT, C0:C0 + P])
                        else:
                            if n:
                                dve.wait_ge(*mfrow_w[n - 1].at(b, 16))
                            ins = nc.vector.tensor_copy(mfrow[:, :], ring(p, key)[0:2 * NT, C0:C0 + P])
                    elif what == "yt" and st == "A":
                        d = ring(p, key)
                        banks = [d[0:P, 512 * o:512 * o + 384].rearrange("p (t h c) -> p t h c", t=3, c=VS)
                                 for o in range(2)]
                        for o in range(2):
                            last = nc.vector.reciprocal(rl[:, 3 * o:3 * o + 3, :], banks[o][:, :, :, DH])
                        last.then_inc(rl_a.sem, 1)
                        dve.wait_ge(*rl_a.at(b, n + 1))
                        for o in range(2):
                            ins = nc.vector.tensor_tensor(
                                yna[:, 3 * o:3 * o + 3, D // NG * n:D // NG * (n + 1)].rearrange(
                                    "p t (h c) -> p t h c", c=DH),
                                banks[o][:, :, :, 0:DH],
                                rl[:, 3 * o:3 * o + 3, :].unsqueeze(3).to_broadcast([P, 3, HG, DH]), ALU.mult)
                    elif what == "yt":
                        d = ring(p, key)
                        banks = [d[0:P, 512 * o:512 * o + 384].rearrange("p (t c) -> p t c", t=3) for o in range(2)]
                        for o in range(2):
                            last = nc.vector.reciprocal(wl[:, 0, 3 * o:3 * o + 3], banks[o][:, :, HD])
                        last.then_inc(rl_f.sem, 1)
                        dve.wait_ge(*rl_f.at(b, 2 * n + 1))
                        nc.vector.tensor_tensor(wl[:, 1, :], wl[:, 0, :], z[:, 10, :, n], ALU.mult
                                                ).then_inc(rl_f.sem, 1)
                        dve.wait_ge(*rl_f.at(b, 2 * n + 2))
                        for o in range(2):
                            ins = nc.vector.tensor_tensor(
                                ynf[:, 3 * o:3 * o + 3, HD * n:HD * (n + 1)], banks[o][:, :, 0:HD],
                                wl[:, 1, 3 * o:3 * o + 3].unsqueeze(2).to_broadcast([P, 3, HD]), ALU.mult)
                    elif what == "p":
                        if n == 0:
                            dve.wait_ge(*h0b_ok.at(b, 1))
                            if "F" in p.stages:
                                dve.wait_ge(*emptied_at(p, F_END))
                        ins = nc.vector.tensor_tensor(h1[:, 2 * n:2 * n + 2, :], pair(key, D), h0b[:, 2 * n:2 * n + 2, :],
                                                      ALU.add)
                    elif what == "mo":
                        dve.wait_ge(*emptied[("A", "dve")].at(b, EMPTY_AT[A_END]))
                        moments(b, 2, h1)
                    elif what == "no":
                        nc.vector.memset(f0[:, 0:1], 0.0)
                        nc.vector.memset(f0[:, T:T + 2], 0.0).then_inc(padded_f.sem, 1)
                        dve.wait_ge(*var[2].at(b, 2))
                        normalise(2, hn2, h1)
                    elif what == "cv":
                        dve.wait_ge(*emptied_at(p, ("F", "fq", 0)))
                        dve.wait_ge(*padded_f.at(b, 1))
                        nc.vector.tensor_scalar(qc[:, :], f0[:, 0:T], Cc[:, C_FC:C_FC + 1], None, ALU.mult
                                                ).then_inc(fconv.sem, 1)
                        for k in (1, 2):
                            dve.wait_ge(*fconv.at(b, k))
                            nc.vector.scalar_tensor_tensor(qc[:, :], f0[:, k:k + T], Cc[:, C_FC + k:C_FC + k + 1],
                                                           qc[:, :], ALU.mult, ALU.add).then_inc(fconv.sem, 1)
                    elif what == "lo":
                        e = n % E
                        dve.wait_ge(*hi.at(b, HI_AT["F", "hi", n]))
                        if n < E:
                            nc.vector.tensor_copy(qb[0:HD, e, :], ff[0:HD, e, :]).then_inc(lo.sem, 1)
                            nc.vector.tensor_tensor(qa[HD:128, e, :], ff[HD:128, e, :], qa[HD:128, e, :],
                                                    ALU.subtract).then_inc(lo.sem, 1)
                        else:
                            nc.vector.tensor_tensor(kb[0:HD, e, :], ff[0:HD, e, :], ka[0:HD, e, :],
                                                    ALU.subtract).then_inc(lo.sem, 1)
                    elif what == "vg":
                        nc.vector.tensor_tensor(gt[:, 0, 2 * n:2 * n + 2, :], pair(key, D + GH)[:, :, D:D + GH],
                                                R[:, R_BG1:R_BG1 + GH].unsqueeze(1).to_broadcast([P, 2, GH]), ALU.add
                                                ).then_inc(vg_ok.sem, 1)
                        for o in range(2):
                            ins = nc.vector.tensor_tensor(
                                v2[:, 2 * n + o, :, 0:HD],
                                ring(p, key)[0:P, 512 * o:512 * o + D].rearrange("p (h c) -> p h c", c=HD),
                                R[:, R_BV2:R_BV2 + D].rearrange("p (h c) -> p h c", c=HD), ALU.add)
                    elif what in ("g1", "g2", "g3"):
                        gate(b, what)
                    elif what == "p2":
                        if n == 0:
                            dve.wait_ge(*h1b_ok.at(b, 1))
                            if "M" in p.stages:
                                dve.wait_ge(*filled_at(p, ("M", "xt", NK - 1)))
                            else:
                                dve.wait_ge(*stored.at(b, 0))
                        ins = nc.vector.tensor_tensor(xin[:, 2 * n:2 * n + 2, :], pair(key, D), h1[:, 2 * n:2 * n + 2, :],
                                                      ALU.add)
                    if in_ring(key) and EMPTIER[key[:2]] == "dve":
                        ins.then_inc(emptied[st, "dve"].sem, 1)
                    if key == ("A", "s1", n, NT - 1, HG - 1):
                        dve.wait_ge(*emptied_at(p, key))
                        c = HG * NT
                        nc.vector.tensor_copy(mb[:, :], m3[:, n % 2, 0:c]).then_inc(msplit.sem, 1)
                        dve.wait_ge(*msplit.at(b, 2 * n + 1))
                        nc.vector.tensor_tensor(m3[:, n % 2, c:2 * c], m3[:, n % 2, 0:c], mb[:, :], ALU.subtract
                                                ).then_inc(msplit.sem, 1)
                    elif key == ("F", "s1", n, NT - 1, 0):
                        dve.wait_ge(*emptied_at(p, key))
                        nc.vector.tensor_copy(mfr[:, :], mf[:, n % 2, 0:NT]).then_inc(mfsplit.sem, 1)
                        dve.wait_ge(*mfsplit.at(b, 2 * n + 1))
                        nc.vector.tensor_tensor(mf[:, n % 2, NT:2 * NT], mf[:, n % 2, 0:NT], mfr[:, :], ALU.subtract
                                                ).then_inc(mfsplit.sem, 1)

            nc.vector.memset(begun[:, :], 0.0).then_inc(stored.sem, 32)
            nc.vector.memset(m3[:, :, :], 0.0).then_inc(zeroed, 1)
            nc.vector.memset(mf[:, :, :], 0.0).then_inc(zeroed, 1)
            nc.vector.memset(va_[:, :, :, :], 0.0).then_inc(zeroed, 1)
            nc.vector.memset(qb[HD:KH, :, :].bitcast(F32), 0.0).then_inc(zeroed, 1)
            dve.wait_ge(zeroed, 4)
            nc.vector.memset(va_[:, :, :, DH:DH + 1], 1.0).then_inc(zeroed, 1)
            nc.vector.memset(v2[:, :, :, HD:HD + 1], 1.0).then_inc(zeroed, 1)
            dve.wait_ge(w_in, 32)
            nc.vector.tensor_scalar(qb4[:, :], Cc[0:KH, C_QK:C_QK + NK], DH ** -0.5, None, ALU.mult).then_inc(scaled, 1)
            nc.vector.tensor_scalar(fb8[:, :], Cc[:, C_FB:C_FB + E + 1], HD ** -0.5, None, ALU.mult).then_inc(scaled, 1)
            dve.wait_ge(w_all, 48)
            dve.wait_ge(zeroed, 6)
            passes(dve, run)

        @block.gpsimd
        def _(pool):
            def select(dst, base, step, channel, fill, op=ALU.is_ge):
                nc.gpsimd.affine_select(out=dst, in_=dst, compare_op=op, fill=fill, base=base,
                                        pattern=[[step, dst.shape[-1]]], channel_multiplier=channel
                                        ).then_inc(consts, 1)

            def tiles(ap):
                return ap.unsqueeze(1).to_broadcast([P, NT, ap.shape[-1]])

            def run(p, before):
                for key in p.order:
                    st, what = key[:2]
                    b = p.b[st]
                    if what == "b0":
                        if "A" in before.stages:
                            pool.wait_ge(*emptied_at(before, A_END))
                        pool.wait_ge(*affine.at(b, 2))
                        nc.gpsimd.tensor_tensor(h0b[:, :, :], h0[:, :, :], tiles(R[:, R_BPROJ:R_BPROJ + D]), ALU.add
                                                ).then_inc(h0b_ok.sem, 1)
                    elif what == "g":
                        n = key[2]
                        pool.wait_ge(*emptied_at(p, ("M", "zg", n)))
                        nc.gpsimd.tensor_tensor(gT[:, n, 0:T], gT[:, n, 0:T], sg[:, n % 2, :], ALU.mult
                                                ).then_inc(gated.sem, 1)
                    elif what == "r0":
                        pool.wait_ge(*stat[0].at(b, NSTAT))
                        nc.gpsimd.tensor_tensor(va[:, 0, :], mv[:, 0, :, 1], expo[:, 3, :], ALU.mult
                                                ).then_inc(var[0].sem, 1)
                        pool.wait_ge(*var[0].at(b, 1))
                        nc.gpsimd.tensor_tensor(sd[:, :], va[:, 0, :], expo[:, 1, :], ALU.pow).then_inc(var[0].sem, 1)
                        pool.wait_ge(*var[0].at(b, 2))
                        nc.gpsimd.tensor_tensor(sde[:, :], sd[:, :], expo[:, 4, :], ALU.add).then_inc(var[0].sem, 1)
                        pool.wait_ge(*var[0].at(b, 3))
                        nc.gpsimd.tensor_tensor(rs[:, 0, :], sde[:, :], expo[:, 2, :], ALU.pow).then_inc(var[0].sem, 1)
                    elif what in ("r1", "rs"):
                        n = 1 if what == "r1" else 2
                        pool.wait_ge(*stat[n].at(b, NSTAT))
                        nc.gpsimd.tensor_tensor(va[:, n, :], mv[:, n, :, 1], expo[:, 5, :], ALU.add
                                                ).then_inc(var[n].sem, 1)
                        pool.wait_ge(*var[n].at(b, 1))
                        nc.gpsimd.tensor_tensor(rs[:, n, :], va[:, n, :], expo[:, 0, :], ALU.pow
                                                ).then_inc(var[n].sem, 1)
                    elif what == "ro":
                        if p.first:
                            pool.wait_ge(w_all, 48)
                        pool.wait_ge(*normed[0].at(b, 1))
                        nc.gpsimd.tensor_tensor(y[:, :, :], t1[:, :, :], tiles(R[:, R_GAMMA:R_GAMMA + D]), ALU.mult
                                                ).then_inc(affine.sem, 1)
                        pool.wait_ge(*affine.at(b, 1))
                        if "A" in p.stages:
                            pool.wait_ge(*h0b_ok.at(p.b["A"], 1))
                        nc.gpsimd.tensor_tensor(h0[:, :, :], y[:, :, :], tiles(R[:, R_BETA:R_BETA + D]), ALU.add
                                                ).then_inc(affine.sem, 1)
                    elif what == "bo":
                        pool.wait_ge(*normed[2].at(b, 1))
                        nc.gpsimd.tensor_tensor(h1[:, :, :], h1[:, :, :], tiles(R[:, R_BP:R_BP + D]), ALU.add
                                                ).then_inc(h1b_ok.sem, 1)
                    elif what == "gp":
                        pool.wait_ge(*relu.at(b, 1))
                        for e in range(E):
                            nc.gpsimd.tensor_tensor(gm[:, e], gt[:, 1], tiles(R[:, R_WG2 + GH * e:R_WG2 + GH * (e + 1)]),
                                                    ALU.mult).then_inc(gate_p.sem, 1)

            for t in (idf, idb, mask_q, mask_k):
                nc.gpsimd.memset(t[:, :], 0.0).then_inc(made, 1)
            for n, v in enumerate(CONSTS):
                nc.gpsimd.memset(expo[:, n, :], v).then_inc(made, 1)
            n = 4 + len(CONSTS)
            pool.wait_ge(made, n)
            nc.gpsimd.memset(kb[HD:KH, :, :].bitcast(F32), 0.0).then_inc(made, 1)
            pool.wait_ge(made, n + 1)
            nc.gpsimd.memset(ks[STACK:STACK + MPARTS, :, :, :], -1.0).then_inc(made, 1)
            pool.wait_ge(made, n + 2)
            nc.gpsimd.memset(kb[HD:HD + 2, :, :].bitcast(F32), -1.0).then_inc(made, 1)
            pool.wait_ge(made, n + 3)
            select(idf[:, :], 0, -1, 1, 1.0, ALU.not_equal)
            select(idb[:, :], 0, -1, 1, 1.0, ALU.not_equal)
            select(mask_q[:, :], 0, -1, 1, NEG)
            select(mask_k[:, :], -1, 1, -1, NEG)
            passes(pool, run)


def kernel(x, **w):
    import numpy as np
    import concourse.bacc as bacc
    from concourse.bass_utils import run_bass_kernel_spmd

    w = {k[3:]: np.asarray(v) for k, v in w.items()}
    x = np.ascontiguousarray(x)

    def contract(mats, n, p):
        a = np.concatenate(mats, axis=1)
        return np.ascontiguousarray(a.reshape(n, p, -1).transpose(1, 0, 2))

    wqk, bqk = w["ffn_Wqk"], w["ffn_bqk"]
    both = [wqk[:, HD * n:HD * (n + 1)] for n in range(2 * E) for _ in range(2)]
    w96 = contract([w["tok_W_in"].T, w["attn_w_attn"].T, w["attn_w_proj"].T, *both,
                    *w["ffn_Wv"], w["ffn_Wg1"], w["ffn_Wp"]], NK, KH)
    w128 = contract([w["tok_W_x"].T, w["tok_W_z"].T, w["tok_W_out"].T], MI, 128)
    cols = np.zeros((128, COLS), np.float32)
    conv = np.concatenate([w["tok_conv_w"][:, 0, :], w["tok_conv_b"][:, None]], axis=1)
    cols[:, C_CONV:C_QK] = conv.reshape(MI, 128, TAPS + 1).transpose(1, 0, 2).reshape(128, -1)
    cols[:KH, C_QK:C_FQK] = w["attn_b_attn"][:2 * D].reshape(2 * NK, KH).T
    for half in (slice(0, HD), slice(HD, 128)):
        cols[half, C_FQK:C_FB] = bqk.reshape(2 * E, HD).T
        cols[half, C_FB:C_FB + E] = bqk[:D].reshape(E, HD).T
        cols[half, C_FB + E] = w["ffn_conv_b"]
        cols[half, C_FC:COLS] = w["ffn_conv_w"][:, 0, :]
    row = np.concatenate([w["tok_gamma"], w["tok_beta"], w["attn_b_attn"][2 * D:], w["attn_b_proj"],
                          w["ffn_bv"].reshape(-1), w["ffn_bg1"], w["ffn_bp"],
                          w["ffn_Wg2"].T.reshape(-1), w["ffn_bg2"]])
    rows = np.ascontiguousarray(np.broadcast_to(row, (P, ROWS)))

    nc = bacc.Bacc("TRN2", target_bir_lowering=False, num_devices=1)
    arrays = {"x_dram": x, "w96_dram": w96, "w128_dram": w128, "cols_dram": cols, "rows_dram": rows}
    aps = [nc.dram_tensor(n, a.shape, mybir.dt.from_np(a.dtype), kind="ExternalInput").ap()
           for n, a in arrays.items()]
    out = nc.dram_tensor("out_dram", (B, T - 1, D), F32, kind="ExternalOutput").ap()
    audio_tower(nc, *aps, out)
    r = run_bass_kernel_spmd(nc, [arrays], core_ids=[0])
    return r.results[0]["out_dram"]
```

```python
from contextlib import ExitStack

import concourse.bass as bass
from concourse import mybir

F32 = mybir.dt.float32
F32R = mybir.dt.float32r
BF16 = mybir.dt.bfloat16
ACT = mybir.ActivationFunctionType
ALU = mybir.AluOpType
AX = mybir.AxisListType

B, T, D = 4, 750, 192
DI = 2 * D
TAPS = 4
P, NT = 125, 6
KH, NK = 96, 2
MI = DI // 128
H, DH = 12, 16
HG, NG = 4, 3
E, HD, GH = 3, 64, 32
VS = 32
SPLIT = 500
C0 = 512 - SPLIT
RING = 3
NEG = -1.0e30
QPARTS = (0, 0, 0, 1, 1, 2)
KPARTS = (0, 1, 2, 0, 1, 0)
STACK = DH * len(QPARTS)
QRUNS = ((0, 3, 0, True), (3, 2, 1, True), (5, 1, 2, True))
KRUNS = ((0, 3, 0, False), (3, 2, 0, False), (5, 1, 0, False))
QK_ORDER = (0, NK, 1, NK + 1)
HT = H // NK
MPARTS = 2
LAG, END_LAG, TURN_LAG = 0, 1, 1
F_LEAD = 2
HOLD = 2
AHEAD = 5
M_HOLD = 4
TURN = 3


def cuts(a, z):
    return [(s, e) for s, e in ((a, min(z, SPLIT)), (max(a, SPLIT), z)) if s < e]


HEADS = {"s1": tuple(1024 // max(256, 1 << (P * (i + 1) - 1).bit_length()) for i in range(NT)),
         "s2": tuple(1024 // max(256, 1 << (P * (NT - i) - 1).bit_length()) for i in range(NT))}


def steps(st, kind, g):
    if st == "F":
        return [(st, kind, g, i, 0) for i in range(NT)]
    return [(st, kind, g, i, h) for i in range(NT) for h in range(0, HG, HEADS[kind][i])]


def heads_in_tiles(g):
    out = []
    for h in range(HG * g, HG * (g + 1)):
        if out and h // HT == out[-1][0]:
            out[-1][2] += 1
        else:
            out.append([h // HT, h % HT, 1, h - HG * g])
    return out


A_STEPS = len(steps("A", "s1", 0))


def foreground():
    s1, s2 = [], []
    for st, g in GROUPS[1:] + [("M", 0)]:
        s1 += [(EARLIEST[st, g](k), key) for k, key in enumerate(steps(st, "s1", g))]
    for st, g in GROUPS:
        s2 += steps(st, "s2", g)
    out, waiting = [], []

    def take(unit):
        out.append(unit)
        st, kind, g, i, h = unit
        for w in waiting:
            w[0] -= 1
        if unit == steps(st, "s1", g)[-1]:
            waiting.append([TURN, [(st, "mt", g), (st, "md", g)]])
        if kind == "s2":
            if i and (st == "F" or h == 0):
                waiting.append([LAG if i < NT - 2 else 0, [(st, "pv", g, i - 1)]])
            if unit == steps(st, "s2", g)[-1]:
                waiting.append([END_LAG, [(st, "pv", g, i)]])
                waiting.append([END_LAG + TURN_LAG, [(st, "yt", g)]])
        for w in [w for w in waiting if w[0] <= 0]:
            out.extend(w[1])
            waiting.remove(w)
    for n, unit in enumerate(s2):
        while s1 and s1[0][0] <= n:
            take(s1.pop(0)[1])
        take(unit)
    for _, unit in s1:
        take(unit)
    return out + [u for w in waiting for u in w[1]]


GROUPS = [("A", 0), ("A", 1), ("F", 0), ("F", 1), ("F", 2), ("A", 2)]
SLOT = (0, 1, 1)
A1_AT, F_AT, A2_AT = A_STEPS, 2 * A_STEPS, 2 * A_STEPS + E * NT
EARLIEST = {("A", 1): lambda k: HOLD + k * (A_STEPS - HOLD - AHEAD) // A_STEPS,
            ("F", 0): lambda k: A1_AT - F_LEAD + k, ("F", 1): lambda k: A1_AT - F_LEAD + 6 + k,
            ("F", 2): lambda k: A1_AT - F_LEAD + 12 + k,
            ("A", 2): lambda k: F_AT + HOLD + k * (E * NT - HOLD - AHEAD) // A_STEPS,
            ("M", 0): lambda k: A2_AT + M_HOLD + k * (A_STEPS - M_HOLD) // A_STEPS}


def background():
    f = [(0, ("F", "mo")), (1, ("F", "rs")), (6, ("F", "no")), (1, ("F", "bo"))]
    f += [(5, ("F", "n2", 0)), (0, ("F", "n2", 1))]
    for n in range(E):
        f += [(3 if n == 0 else 1, ("F", "fq", n))]
        if n == 0:
            f += [(0.4, ("F", "cv", k)) for k in range(3)]
        else:
            f += [(3, ("F", "hi", n))] + [(0.4, ("F", "lo", n, k)) for k in range(3)]
    f += [(2, ("F", "hi", 0))] + [(0.4, ("F", "lo", 0, k)) for k in range(3)]
    f += [(1, ("F", "vg", t)) for t in range(NT // 2)]
    f += [(2, ("F", "ga")), (1, ("F", "gp")), (3, ("F", "g1")), (1, ("F", "e1")), (2, ("F", "g2")),
          (1, ("F", "e2")), (2, ("F", "g3"))]
    m = [(0, ("M", "xt", 0)), (1, ("M", "xt", 1)), (0, ("M", "pad"))]
    m += [(2 if k == 0 else 1, ("M", "xe", k)) for k in range(MI)]
    for k in range(MI):
        m += [(0.5, ("M", "cv", k, tap)) for tap in range(TAPS)]
        if k:
            m += [(1, ("M", "th", k - 1)), (1, ("M", "h", k - 1))]
    m += [(1, ("M", "th", MI - 1)), (1, ("M", "h", MI - 1))]
    for k in range(MI):
        m += [(2, ("M", "xg", k)), (0.4, ("M", "zg", k)), (0, ("M", "g", k))]
    m += [(4 if t == 0 else 1, ("M", "y", t)) for t in range(NT // 2)]
    m += [(0.4, ("M", "m0")), (0, ("M", "r0")), (4, ("M", "n0")), (1, ("M", "m1")), (0, ("M", "r1")),
          (5, ("M", "n1")), (3, ("M", "nt", 0)), (0, ("M", "nt", 1))]
    late = []
    for n in range(2 * NK):
        to = m if n < 2 else late
        to += [(2 if n == 0 else 1, ("M", "qk", n)), *((0.4, ("M", "sp", n, k)) for k in range(4)), (0, ("M", "pw", n))]
    m += [(2, ("M", "ld", 0))]
    return f, m, late


F_FROM, F_TO = 1, 38
M_FROM = 2
LD_AHEAD = 8
O_FROM = 4


def order_of(stages, f_to):
    fg = [k for k in foreground() if k[0] in stages]
    places = []
    to = fg.index(("M", "s1", 0, 0, 0)) - LD_AHEAD if "M" in stages else 0
    for bg, a, z in zip(background(), (F_FROM, f_to + 1, to), (f_to, to, to + LD_AHEAD - 0.5)):
        total = sum(w for w, _ in bg)
        c = 0
        for w, key in bg:
            c += w
            if key[0] in stages:
                places.append((a + (z - a) * c / total, key))
    if "F" in stages:
        f_done = fg.index(("F", "yt", E - 1)) + O_FROM
        places += [(f_done + 2, ("F", "o2", k)) for k in range(NK)]
        places += [(f_done + 5 + 2 * t, ("F", "p2", t)) for t in range(NT // 2)] + [(f_done + 10, ("F", "st"))]
    places.sort(key=lambda x: x[0])
    out = [("M", "x"), ("A", "b0")]
    for n, key in enumerate(fg):
        while places and places[0][0] <= n:
            out.append(places.pop(0)[1])
        out.append(key)
        if key == steps("A", "s2", 1)[-1]:
            out.append(("A", "ld", 2))
    out += [k for _, k in places]
    out += [("M", "ld", 1)] + [("M", "v", t) for t in range(NT // 2)]
    out += [("A", "ot", k) for k in range(NK)] + [("A", "p", t) for t in range(NT // 2)]
    return [k for k in out if k[0] in stages]


def checked(order):
    at = {k: n for n, k in enumerate(order)}
    assert at["A", "pv", NG - 1, NT - 1] < at["M", "v", 0]
    assert max(at[steps("A", "s2", 0)[-1]], at["M", "pw", 1]) < at["M", "ld", 0] < at["M", "s1", 0, 0, 0]
    assert at["A", "mt", NG - 1] < at["M", "s1", 0, 0, 0] and at["A", "s1", 2, 0, 0] > at["A", "ld", 2]
    if order is MID:
        assert max(at["F", "lo", 0, 2], at["F", "vg", NT // 2 - 1]) < at["M", "xt", 0]
        assert at["F", "g3"] < at["F", "yt", 0] and at["F", "lo", 0, 2] < at["F", "s1", 0, 0, 0]
    for st in "MAF":
        assert [k for k in order if k[0] == st] in ([], [k for k in MID if k[0] == st])


MID = order_of("MAF", F_TO)
PROLOGUE = [k for k in MID if k[0] == "M"]
FIRST = order_of("MA", M_FROM)
LAST = [k for k in MID if k[0] != "M"]
EPILOGUE = [k for k in MID if k[0] == "F"]
checked(MID)
checked(FIRST)

EMPTIER = {("M", n): "dve" for n in ("s1", "mt")}
EMPTIER |= {("M", n): "act" for n in ("xt", "xe", "y", "nt", "qk")}
EMPTIER |= {("M", n): "dve" for n in ("xg", "zg", "v")}
EMPTIER |= {("A", n): "dve" for n in ("s1", "mt", "yt", "p")}
EMPTIER |= {("A", n): "act" for n in ("s2", "ot")}
EMPTIER |= {("F", n): "dve" for n in ("vg", "s1", "mt", "yt", "p2")}
EMPTIER |= {("F", n): "act" for n in ("n2", "fq", "s2", "o2")}


def in_ring(k):
    return k[:2] in EMPTIER


UNITS = {st: [k for k in MID if k[0] == st and in_ring(k)] for st in "MAF"}
FILL_AT = {k: n + 1 for ks in UNITS.values() for n, k in enumerate(ks)}
EMPTY_AT, EMPTY_PER = {}, {}
for _st in "MAF":
    for _e in ("act", "dve"):
        _ks = [k for k in UNITS[_st] if EMPTIER[k[:2]] == _e]
        EMPTY_AT |= {k: n + 1 for n, k in enumerate(_ks)}
        EMPTY_PER[_st, _e] = len(_ks)


SPLIT_AT = {n: c + 1 for c, n in enumerate(k[2] for k in MID if k[:2] == ("F", "hi"))}


class Tally:

    def __init__(self, sem, per, start=0):
        self.sem, self.per, self.start = sem, per, start

    def at(self, b, k):
        i, off = b
        return self.sem, i * self.per + (off * self.per + self.start + k)


class Pass:

    def __init__(self, order, i):
        self.order = order
        self.first = order is PROLOGUE
        self.b = {"M": (i, 2), "A": (i, 1), "F": (i, 0)}
        self.stages = {k[0] for k in order}
        self.groups = [g for g in GROUPS if g[0] in self.stages]
        self.products = [k for k in order if k[1] == "pv"]
        units = [k for k in order if in_ring(k)]
        self.slot = {k: n % RING for n, k in enumerate(units)}
        self.old = {k: units[n - RING] for n, k in enumerate(units) if n >= RING}


O_IN = 0
O_QK = O_IN + DI
O_V = O_QK + 2 * D
O_PROJ = O_V + D
O_FQK = O_PROJ + D
O_VG = O_FQK + 2 * D
O_WP = O_VG + D + GH
W96 = O_WP + D
O_X = 0
O_Z = O_X + DI
O_OUT = O_Z + DI
W128 = O_OUT + D
C_CONV = 0
C_QK = C_CONV + MI * (TAPS + 1)
C_FQK = C_QK + 2 * NK
C_FC = C_FQK + E
COLS = C_FC + 4
R_GAMMA = 0
R_BETA = R_GAMMA + D
R_BV = R_BETA + D
R_BPROJ = R_BV + D
R_BV2 = R_BPROJ + D
R_BG1 = R_BV2 + D
R_BP = R_BG1 + GH
R_WG2 = R_BP + D
R_BG2 = R_WG2 + E * GH
ROWS = R_BG2 + E
CONSTS = (-0.5, 0.5, -1.0, D / (D - 1.0), 1e-6, 1e-5)
N_CONSTS, N_MADE = 5, 4 + len(CONSTS)
NSTAT = 2 * NT + 1


def audio_tower(nc, x, w96, w128, cols, rows, out):
    with ExitStack() as ctx:
        def sb(name, shape, dt=F32):
            return ctx.enter_context(nc.sbuf_tensor(name, shape, dt))

        def sem(name):
            return ctx.enter_context(nc.semaphore(name))

        def tally(name, per, start=0):
            return Tally(sem(name), per, start)

        W = sb("W", [KH, NK, W96])
        W3 = sb("W3", [128, MI, W128])
        Cc = sb("Cc", [128, COLS])
        R = sb("R", [P, ROWS])
        idf = sb("idf", [128, 128])
        idb = sb("idb", [128, 128], BF16)
        mask_q = sb("mask_q", [P, P + 1], BF16)
        mask_k = sb("mask_k", [P, P + 1], BF16)
        expo = sb("expo", [P, len(CONSTS), NT])
        xin = sb("xin", [P, NT, D])
        stats = sb("stats", [P, 3, NT, 6])
        mv = sb("mv", [P, 3, NT, 2])
        begun = sb("begun", [P, 3])
        va = sb("va", [P, 3, NT])
        sd = sb("sd", [P, NT])
        sde = sb("sde", [P, NT])
        rs = sb("rs", [P, 3, NT])
        h0b = sb("h0b", [P, NT, D])
        h1 = sb("h1", [P, NT, D])
        qs = sb("qs", [STACK + MPARTS, 2, HG, T], BF16)
        ks = sb("ks", [STACK + MPARTS, 2, HG, T], BF16)
        va_ = sb("vaug", [P, NT, H, VS])
        m3 = sb("m3", [P, 2, KH])
        mb = sb("mb", [P, HG * NT], BF16)
        mrow = sb("mrow", [MPARTS * HG * NT, P], BF16)
        yna = sb("yna", [P, NT, D])
        pt = sb("pt", [P, 2, HG, T])
        ysb = sb("ysb", [128, 2, T])
        rl = sb("rl", [P, NT, HG])
        yT = sb("yT", [KH, NK, T])
        qa = sb("qa", [128, E, T], F32R)
        qb = sb("qb", [KH, E, T], F32R)
        ka = sb("ka", [128, E, T], F32R)
        kb = sb("kb", [KH, E, T], F32R)
        v2 = sb("v2", [P, NT, E, HD + 1])
        gt = sb("gt", [P, 2, NT, GH])
        gm = sb("gm", [P, E, NT, GH])
        z = sb("z", [P, 12, NT, E])
        zs = sb("zs", [P, 8, NT])
        mf = sb("mf", [P, 2, KH])
        mfr = sb("mfr", [P, NT], F32R)
        mfrow = sb("mfrow", [2 * NT, P], F32R)
        wl = sb("wl", [P, 2, NT])
        ynf = sb("ynf", [P, NT, D])
        def over(tensors):
            with ExitStack() as stage:
                return [stage.enter_context(nc.sbuf_tensor(n, s, dt)) for n, s, dt in tensors]
        hn2, nT2, f0, ff = over([("hn2", [P, NT, D], F32), ("nT2", [KH, NK, T], F32),
                                     ("f0", [HD, T + 2], F32),
                                     ("ff", [128, E, T], F32)])
        xe, cv, sg, tg = over([("xe", [128, MI, T + TAPS - 1], F32),
                               ("cv", [128, MI, T], F32), ("sg", [128, 2, T], F32), ("tg", [128, 2, T], F32)])
        gT, _, _, xT = over([("gT", [128, MI, T + TAPS - 1], F32), ("space1", [128, MI, T], F32),
                             ("space2", [128, 2, T], F32), ("xT", [KH, NK, T], F32)])
        _, y, t1, hn = over([("space3", [128, MI, T + TAPS - 1], F32), ("y", [P, NT, D], F32),
                             ("t1", [P, NT, D], F32), ("hn", [P, NT, D], F32)])
        nT, f, fr, parts, h0 = over([("nT", [KH, NK, T], F32), ("f", [KH, 2, T], F32), ("fr", [KH, T], F32),
                                     ("parts", [KH, 2, 3, T], BF16), ("h0", [P, NT, D], F32)])
        stackd = nc.dram_tensor("stackd", [B, 2 * NK, len(QPARTS), KH, T], BF16, kind="Internal").ap()
        rowsd = nc.dram_tensor("rowsd", [NG, MPARTS * HG * NT, P], BF16, kind="Internal").ap()
        rowsf = nc.dram_tensor("rowsf", [E, 2 * NT, P], F32, kind="Internal").ap()

        ps = [ctx.enter_context(nc.psum_tensor(f"ps{n}", [128, 1024], F32)) for n in range(RING)]
        acc = ctx.enter_context(nc.psum_tensor("acc", [128, 1024], F32))

        w_in = sem("w_in")
        w_all = sem("w_all")
        consts = sem("consts")
        made = sem("made")
        zeroed = sem("zeroed")
        filled = {st: tally(f"filled_{st}", len(UNITS[st])) for st in "MAF"}
        emptied = {se: tally("emptied_%s_%s" % se, n) for se, n in EMPTY_PER.items()}
        x_in = tally("x_in", 16)
        padded = tally("padded", 1)
        tap = tally("tap", MI * TAPS)
        tanhs = tally("tanhs", 3 * MI)
        mixed = tally("mixed", MI)
        gated = tally("gated", MI)
        stat = {n: tally(f"stat{n}", NSTAT) for n in range(3)}
        var = {n: tally(f"var{n}", k) for n, k in enumerate((4, 2, 2))}
        normed = {n: tally(f"normed{n}", 1) for n in (1, 2)}
        affine = tally("affine", 2)
        split = tally("split", 4 * 2 * NK)
        stack_w = [tally(f"stack_w{n}", 48) for n in range(2 * NK)]
        stack_r = [tally(f"stack_r{g}", 16 * 2 * len(heads_in_tiles(g))) for g in range(NG)]
        h0b_ok = tally("h0b_ok", 1)
        msplit = tally("msplit", 2 * NG)
        mrow_w = [tally(f"mrow_w{g}", 16) for g in range(NG)]
        mrows = [tally(f"mrows{g}", 16) for g in range(NG)]
        rl_a = tally("rl_a", NG)
        pv_done = {"A": tally("pv_done_A", NG * NT), "F": tally("pv_done_F", E * NT)}
        y_out = {"A": tally("y_out_A", NG), "F": tally("y_out_F", E)}
        h1b_ok = tally("h1b_ok", 1)
        padded_f = tally("padded_f", 1)
        fconv = tally("fconv", 3)
        hi = tally("hi", E)
        lo = tally("lo", E)
        vg_ok = tally("vg_ok", NT // 2)
        gate_p = tally("gate_p", E)
        relu = tally("relu", 1)
        gate_v = tally("gate_v", 16)
        gate_a = tally("gate_a", 2)
        mfsplit = tally("mfsplit", 2 * E)
        mfrow_w = [tally(f"mfrow_w{e}", 16) for e in range(E)]
        mfrows = [tally(f"mfrows{e}", 16) for e in range(E)]
        rl_f = tally("rl_f", 2 * E)
        stored = tally("stored", 32, 32)

        block = ctx.enter_context(nc.Block())

        def ring(p, key):
            return ps[p.slot[key]]

        def filled_at(p, key):
            return filled[key[0]].at(p.b[key[0]], FILL_AT[key])

        def emptied_at(p, key):
            return emptied[key[0], EMPTIER[key[:2]]].at(p.b[key[0]], EMPTY_AT[key])

        def free_at(p, key):
            return emptied_at(p, p.old[key])

        def one(ap, b):
            i, off = b
            return ap[i + off:i + off + 1] if isinstance(i, int) else ap[off:][bass.ds(i, 1)]

        def passes(eng, run):
            run(Pass(PROLOGUE, -2), None)
            run(Pass(FIRST, -1), Pass(PROLOGUE, -2))
            with eng.Fori(0, B - 2) as i:
                run(Pass(MID, i), Pass(MID, i - 1))
            run(Pass(LAST, B - 2), Pass(MID, B - 3))
            run(Pass(EPILOGUE, B - 1), Pass(LAST, B - 2))

        M_END = ("M", "v", NT // 2 - 1)
        A_END = ("A", "p", NT // 2 - 1)
        F_END = ("F", "p2", NT // 2 - 1)

        @block.sync
        def _(sp):
            def run(p, before):
                for key in p.order:
                    st, what = key[:2]
                    b = p.b[st]
                    if key == ("M", "x"):
                        if before:
                            sp.wait_ge(*filled_at(before, ("M", "xt", NK - 1)))
                        if "F" in p.stages:
                            sp.wait_ge(*stored.at(p.b["F"], 0))
                        sp.dma_start(xin[:, :, :], one(x, b).rearrange("o (n p) d -> p (o n) d", p=P)
                                     ).then_inc(x_in.sem, 16)
                    elif what == "pw":
                        n = key[2]
                        tile = QK_ORDER[n]
                        sp.wait_ge(*split.at(b, 4 * (n + 1)))
                        for r, count, part, spread in QRUNS if tile < NK else KRUNS:
                            src = parts[:, n % 2, part:part + 1, :].to_broadcast([KH, count, T]) if spread \
                                else parts[:, n % 2, part:part + count, :]
                            sp.dma_start(one(stackd, b)[:, tile, r:r + count].rearrange("o r p t -> p (o r) t"), src
                                         ).then_inc(stack_w[n].sem, 16)
                    elif what == "ld":
                        g = key[2]
                        if "A" in p.stages:
                            sp.wait_ge(*filled_at(p, steps("A", "s2", {"M0": 0, "A2": 1, "M1": NG - 1}[f"{st}{g}"])[-1]))
                        if st == "M":
                            for n in ((0, 1), (2, 3))[g]:
                                sp.wait_ge(*stack_w[n].at(b, 48))
                        for side, dst in enumerate((qs, ks)):
                            for tile, h, count, to in heads_in_tiles(g):
                                sp.dma_start(dst[0:STACK, SLOT[g], to:to + count, :],
                                             one(stackd, b)[:, side * NK + tile].rearrange(
                                                 "o r (i h) t -> (o r i) h t", h=HT)[:, h:h + count, :]
                                             ).then_inc(stack_r[g].sem, 16)
                    elif what == "md":
                        g = key[2]
                        sp.wait_ge(*emptied_at(p, (st, "mt", g)))
                        if st != "F":
                            sp.dma_start(rowsd[g], mrow[:, :]).then_inc(mrow_w[g].sem, 16)
                            sp.wait_ge(*mrow_w[g].at(b, 16))
                            sp.dma_start(qs[STACK:STACK + MPARTS, SLOT[g], :, :],
                                         rowsd[g].rearrange("(a h t) c -> a h (t c)", a=MPARTS, h=HG)
                                         ).then_inc(mrows[g].sem, 16)
                        else:
                            sp.dma_start(rowsf[g], mfrow[:, :].bitcast(F32)).then_inc(mfrow_w[g].sem, 16)
                            sp.wait_ge(*mfrow_w[g].at(b, 16))
                            sp.dma_start(qb[HD:HD + 2, g, :].bitcast(F32), rowsf[g].rearrange("(a t) c -> a (t c)", a=2)
                                         ).then_inc(mfrows[g].sem, 16)
                    elif what == "st":
                        sp.wait_ge(*emptied_at(p, F_END))
                        sp.dma_start(one(out, b)[:, 0:P * (NT - 1), :].rearrange("o (n p) d -> p (o n) d", p=P),
                                     xin[:, 0:NT - 1, :]).then_inc(stored.sem, 16)
                        sp.dma_start(one(out, b)[:, P * (NT - 1):T - 1, :].rearrange("o (n p) d -> p (o n) d", p=P - 1),
                                     xin[0:P - 1, NT - 1:NT, :]).then_inc(stored.sem, 16)
                    if p.first and key == ("M", "x"):
                        sp.dma_start(W[:, :, 0:DI], w96[:, :, 0:DI]).then_inc(w_in, 16)
                        sp.dma_start(Cc[:, :], cols).then_inc(w_in, 16)
                        sp.dma_start(W3[:, :, :], w128).then_inc(w_all, 16)
                        sp.dma_start(R[:, :], rows).then_inc(w_all, 16)
                        sp.dma_start(W[:, :, DI:W96], w96[:, :, DI:W96]).then_inc(w_all, 16)

            passes(sp, run)
            sp.wait_ge(stored.sem, 32 * (B + 1))

        @block.tensor
        def _(pe):
            def turn(p, key, src):
                d = ring(p, key)
                for i in range(NT):
                    c = C0 + P * i
                    mm = nc.tensor.transpose(d[0:KH, c:c + P], src[:, i, :], idf[0:P, 0:P])
                return mm

            def by_feature(p, key, w, src, m):
                d = ring(p, key)
                n = len(w)
                for s, e in cuts(0, T):
                    for k in range(n):
                        mm = nc.tensor.matmul(d[0:m, C0 + s:C0 + e], w[k], src[k][:, s:e],
                                              start=(k == 0), stop=(k == n - 1))
                return mm

            def by_token(p, key, src, w, width):
                d = ring(p, key)
                n = len(w)
                for o in range(2):
                    i = 2 * key[2] + o
                    for k in range(n):
                        mm = nc.tensor.matmul(d[0:P, 512 * o:512 * o + width], src[k][:, P * i:P * (i + 1)], w[k],
                                              start=(k == 0), stop=(k == n - 1))
                return mm

            def maxima_scores(d, st, g, i, h):
                z0 = P * (i + 1)
                if st == "F":
                    z0 += z0 % 2
                    for s, e in cuts(0, z0):
                        nc.tensor.matmul(d[0:P, C0 + s:C0 + e], qa[:, g, P * i:P * (i + 1)],
                                         ka[:, g, s:e], start=True, stop=e != z0)
                    return nc.tensor.matmul(d[0:P, C0 + P * i:C0 + z0], idb[0:P, 0:P],
                                            mask_q[:, 0:z0 - P * i], start=False, stop=True)
                heads = HEADS["s1"][i]
                for k in range(heads):
                    c = C0 if heads == 1 else 1024 // heads * k
                    for s, e in cuts(0, z0):
                        nc.tensor.matmul(d[0:P, c + s:c + e], qs[0:STACK, SLOT[g], h + k, P * i:P * (i + 1)],
                                         ks[0:STACK, SLOT[g], h + k, s:e], start=True, stop=e != z0)
                    mm = nc.tensor.matmul(d[0:P, c + P * i:c + z0], idb[0:P, 0:P], mask_q[:, 0:P],
                                          start=False, stop=True)
                return mm

            def scores(d, st, g, i, h):
                a0 = P * i
                if st == "F":
                    a0 -= a0 % 2
                heads = 1 if st == "F" else HEADS["s2"][i]
                for k in range(heads):
                    c = C0 if heads == 1 else 1024 // heads * k - a0
                    for s, e in cuts(a0, T) if heads == 1 else [(a0, T)]:
                        diag = s == a0
                        dst = d[0:P, c + s:c + e]
                        if st == "F":
                            nc.tensor.matmul(dst, ka[:, g, P * i:P * (i + 1)], qa[:, g, s:e], start=True, stop=False)
                            mm = nc.tensor.matmul(dst, kb[:, g, P * i:P * (i + 1)], qb[:, g, s:e],
                                                  start=False, stop=not diag)
                        else:
                            mm = nc.tensor.matmul(dst, ks[:, SLOT[g], h + k, P * i:P * (i + 1)],
                                                  qs[:, SLOT[g], h + k, s:e], start=True, stop=not diag)
                        if diag:
                            mm = nc.tensor.matmul(d[0:P, c + a0:c + P * (i + 1)], idb[0:P, 0:P],
                                                  mask_k[:, 1 - (P * i - a0):P + 1], start=False, stop=True)
                return mm

            def times_values(st, g, i):
                for s, e in cuts(P * i, T):
                    for h in range(HG if st == "A" else 1):
                        if st == "A":
                            w, m0, m1 = va_[:, i, HG * g + h, :], VS * h, VS * (h + 1)
                        else:
                            w, m0, m1 = v2[:, i, g, :], 0, HD + 1
                        mm = nc.tensor.matmul(acc[m0:m1, C0 + s:C0 + e], w, pt[:, i % 2, h, s:e],
                                              start=(i == 0), stop=(P * (i + 1) == e))
                return mm

            def result_turn(d, st, g):
                m = 128 if st == "A" else HD + 1
                for t in range(NT):
                    c = 512 * (t // 3) + 128 * (t % 3)
                    mm = nc.tensor.transpose(d[0:P, c:c + m], ysb[0:m, GROUPS.index((st, g)) % 2, P * t:P * (t + 1)],
                                             idf[0:m, 0:m])
                return mm

            def wk(o, n):
                return [W[:, k, o:o + n] for k in range(NK)]

            def tiles_of(t, n=NK):
                return [t[:, k, :] for k in range(n)]

            def run(p, before):
                if before:
                    pe.wait_ge(*emptied_at(before, M_END if "A" not in before.stages else A_END))
                for key in p.order:
                    st, what = key[:2]
                    b = p.b[st]
                    n = key[2] if len(key) > 2 else None
                    if in_ring(key) and key in p.old:
                        pe.wait_ge(*free_at(p, key))
                    if what == "xt":
                        pe.wait_ge(*x_in.at(b, 16))
                        mm = turn(p, key, xin[:, :, KH * n:KH * (n + 1)])
                    elif what == "xe":
                        if p.first:
                            pe.wait_ge(w_in, 32)
                        pe.wait_ge(*emptied_at(p, ("M", "xt", NK - 1)))
                        mm = by_feature(p, key, wk(O_IN + 128 * n, 128), tiles_of(xT), 128)
                    elif what in ("xg", "zg"):
                        if p.first:
                            pe.wait_ge(w_all, 48)
                        pe.wait_ge(*mixed.at(b, MI))
                        o = 128 * n + (O_X if what == "xg" else O_Z)
                        mm = by_feature(p, key, [W3[:, k, o:o + 128] for k in range(MI)], tiles_of(cv, MI), 128)
                    elif what == "y":
                        pe.wait_ge(*gated.at(b, MI))
                        mm = by_token(p, key, [gT[:, k, 0:T] for k in range(MI)],
                                      [W3[:, k, O_OUT:O_OUT + D] for k in range(MI)], D)
                    elif what == "nt":
                        pe.wait_ge(*normed[1].at(b, 1))
                        mm = turn(p, key, hn[:, :, KH * n:KH * (n + 1)])
                    elif what == "qk":
                        pe.wait_ge(*emptied_at(p, ("M", "nt", NK - 1)))
                        mm = by_feature(p, key, wk(O_QK + KH * QK_ORDER[n], KH), tiles_of(nT), KH)
                    elif what == "v":
                        mm = by_token(p, key, tiles_of(nT), wk(O_V, D), D)
                    elif what == "s1":
                        if key[3:] == (0, 0):
                            if p.first:
                                pe.wait_ge(consts, N_CONSTS)
                                pe.wait_ge(made, N_MADE)
                                pe.wait_ge(zeroed, 8)
                            if st != "F":
                                pe.wait_ge(*stack_r[n].at(b, stack_r[n].per))
                            else:
                                pe.wait_ge(*lo.at(b, SPLIT_AT[n]))
                        mm = maxima_scores(ring(p, key), *(key[:1] + key[2:]))
                    elif what == "mt":
                        if st != "F":
                            pe.wait_ge(*msplit.at(b, 2 * (n + 1)))
                            mm = nc.tensor.transpose(ring(p, key)[0:KH, C0:C0 + P], m3[:, n % 2, :], idf[0:P, 0:P])
                        else:
                            pe.wait_ge(*mfsplit.at(b, 2 * (n + 1)))
                            mm = nc.tensor.transpose(ring(p, key)[0:KH, C0:C0 + P], mf[:, n % 2, :], idf[0:P, 0:P])
                    elif what == "s2":
                        if key[3:] == (0, 0):
                            if st == "A":
                                pe.wait_ge(*mrows[n].at(b, 16))
                            else:
                                pe.wait_ge(*mfrows[n].at(b, 16))
                        mm = scores(ring(p, key), *(key[:1] + key[2:]))
                    elif what == "pv":
                        if key[3] == 0:
                            at = p.groups.index((st, n))
                            if at:
                                other, g = p.groups[at - 1]
                                pe.wait_ge(*y_out[other].at(p.b[other], g + 1))
                            if st == "A" and n == 0:
                                pe.wait_ge(*emptied[("M", "dve")].at(b, EMPTY_AT["M", "v", NT // 2 - 1]))
                            if st == "F" and n == 0:
                                pe.wait_ge(*emptied_at(p, ("F", "vg", NT // 2 - 1)))
                        pe.wait_ge(*emptied_at(p, [k for k in steps(st, "s2", n) if k[3] == key[3]][-1]))
                        times_values(st, n, key[3]).then_inc(pv_done[st].sem, 1)
                    elif what == "yt":
                        pe.wait_ge(*y_out[st].at(b, n + 1))
                        mm = result_turn(ring(p, key), st, n)
                    elif what == "ot":
                        pe.wait_ge(*emptied_at(p, ("A", "yt", NG - 1)))
                        mm = turn(p, key, yna[:, :, KH * n:KH * (n + 1)])
                    elif what == "p":
                        pe.wait_ge(*emptied_at(p, ("A", "ot", NK - 1)))
                        mm = by_token(p, key, tiles_of(yT), wk(O_PROJ, D), D)
                    elif what == "n2":
                        pe.wait_ge(*normed[2].at(b, 1))
                        mm = turn(p, key, hn2[:, :, KH * n:KH * (n + 1)])
                    elif what == "fq":
                        pe.wait_ge(*emptied_at(p, ("F", "n2", NK - 1)))
                        mm = by_feature(p, key, wk(O_FQK + 128 * n, 128), tiles_of(nT2), 128)
                    elif what == "vg":
                        mm = by_token(p, key, tiles_of(nT2), wk(O_VG, D + GH), D + GH)
                    elif what == "o2":
                        pe.wait_ge(*emptied_at(p, ("F", "yt", E - 1)))
                        mm = turn(p, key, ynf[:, :, KH * n:KH * (n + 1)])
                    elif what == "p2":
                        pe.wait_ge(*emptied_at(p, ("F", "o2", NK - 1)))
                        mm = by_token(p, key, tiles_of(yT), wk(O_WP, D), D)
                    if in_ring(key):
                        mm.then_inc(filled[st].sem, 1)

            pe.wait_ge(consts, 1)
            passes(pe, run)

        @block.scalar
        def _(act):
            def run(p, before):
                def row(key, m=128):
                    return ring(p, key)[0:m, C0:C0 + T]

                for key in p.order:
                    st, what = key[:2]
                    b = p.b[st]
                    n = key[2] if len(key) > 2 else None
                    if in_ring(key) and EMPTIER[key[:2]] == "act":
                        act.wait_ge(*filled_at(p, key))
                    if what == "xt":
                        if n == 0:
                            if before:
                                for k in range(2 * NK):
                                    act.wait_ge(*stack_w[k].at(p.b["A"], 48))
                                act.wait_ge(*h0b_ok.at(p.b["A"], 1))
                            if "F" in p.stages:
                                act.wait_ge(*lo.at(p.b["F"], lo.per))
                        ins = nc.scalar.activation(xT[:, n, :], row(key, KH), ACT.Copy)
                    elif what == "xe":
                        ins = nc.scalar.activation(xe[:, n, 1:1 + T], row(key), ACT.Copy)
                    elif what == "th":
                        act.wait_ge(*tap.at(b, TAPS * (n + 1)))
                        if n >= 2:
                            act.wait_ge(*mixed.at(b, n - 1))
                        nc.scalar.activation(tg[:, n % 2, :], cv[:, n, :], ACT.Tanh, scale=0.5
                                             ).then_inc(tanhs.sem, 1)
                    elif what in ("xg", "zg"):
                        act.wait_ge(*filled_at(p, key))
                        if n:
                            act.wait_ge(*emptied_at(p, ("M", what, n - 1)))
                        elif what == "xg":
                            act.wait_ge(*mixed.at(b, MI))
                        nc.scalar.activation(tg[:, what == "zg", :], row(key), ACT.Tanh, scale=0.25
                                             ).then_inc(tanhs.sem, 1)
                    elif what == "y":
                        ins = nc.scalar.activation(y[:, 2 * n:2 * n + 2, :],
                                                   ring(p, key)[0:P, :].rearrange("p (o c) -> p o c", o=2)[:, :, 0:D],
                                                   ACT.Copy, scale=1 / 16)
                    elif what == "nt":
                        ins = nc.scalar.activation(nT[:, n, :], row(key, KH), ACT.Copy)
                    elif what == "qk":
                        if n >= 2:
                            act.wait_ge(*split.at(b, 4 * (n - 1)))
                        c = C_QK + QK_ORDER[n]
                        ins = nc.scalar.activation(f[:, n % 2, :], row(key, KH), ACT.Identity, bias=Cc[0:KH, c:c + 1])
                    elif what == "s2":
                        i, h = key[3:]
                        if h == 0:
                            at = p.products.index((st, "pv", n, i)) - 2
                            if at >= 0:
                                other, _, g, j = p.products[at]
                                act.wait_ge(*pv_done[other].at(p.b[other], g * NT + j + 1))
                        if st == "F" or HEADS[what][i] == 1:
                            a0 = P * i - (P * i) % 2 if st == "F" else P * i
                            ins = nc.scalar.activation(pt[:, i % 2, h, a0:T], ring(p, key)[0:P, C0 + a0:C0 + T],
                                                       ACT.Exp, scale=HD ** -0.5 if st == "F" else DH ** -0.5)
                        else:
                            heads = HEADS[what][i]
                            ins = nc.scalar.activation(
                                pt[:, i % 2, h:h + heads, P * i:T],
                                ring(p, key)[0:P, :].rearrange("p (h c) -> p h c", h=heads)[:, :, 0:T - P * i], ACT.Exp,
                                scale=DH ** -0.5)
                    elif what == "pv" and key[3] == NT - 1:
                        m = 128 if st == "A" else HD + 1
                        at = GROUPS.index((st, n))
                        act.wait_ge(*pv_done[st].at(b, (n + 1) * NT))
                        same_half = [o for o in p.groups if GROUPS.index(o) < at and (GROUPS.index(o) - at) % 2 == 0]
                        for other, g in same_half[-1:]:
                            act.wait_ge(*filled_at(p, (other, "yt", g)))
                        nc.scalar.activation(ysb[0:m, at % 2, :], acc[0:m, C0:C0 + T], ACT.Copy
                                             ).then_inc(y_out[st].sem, 1)
                    elif what in ("ot", "o2"):
                        if what == "ot" and "F" in p.stages:
                            act.wait_ge(*filled_at(p, F_END))
                        ins = nc.scalar.activation(yT[:, n, :], row(key, KH), ACT.Copy)
                    elif what == "n2":
                        ins = nc.scalar.activation(nT2[:, n, :], row(key, KH), ACT.Copy)
                    elif what == "fq":
                        if n == 0:
                            if "A" in p.stages:
                                for k in range(2 * NK):
                                    act.wait_ge(*stack_w[k].at(p.b["A"], 48))
                                act.wait_ge(*h0b_ok.at(p.b["A"], 1))
                            nc.scalar.activation(f0[:, 1:T], row(key, HD)[:, 0:T - 1], ACT.Identity,
                                                 bias=Cc[0:HD, C_FQK:C_FQK + 1])
                            ins = nc.scalar.activation(ff[HD:128, 0, :], ring(p, key)[HD:128, C0:C0 + T], ACT.Identity,
                                                       bias=Cc[HD:128, C_FQK:C_FQK + 1])
                        else:
                            ins = nc.scalar.activation(ff[:, n, :], row(key), ACT.Identity,
                                                       bias=Cc[:, C_FQK + n:C_FQK + n + 1])
                    elif what == "hi":
                        act.wait_ge(*emptied_at(p, ("F", "fq", n)))
                        if n == 0:
                            act.wait_ge(*fconv.at(b, 3))
                        nc.scalar.activation(qa[0:HD, n, :], ff[0:HD, n, :], ACT.Copy)
                        nc.scalar.activation(ka[0:HD, n, :], ff[HD:128, n, :], ACT.Copy)
                        nc.scalar.activation(ka[HD:128, n, :], ff[HD:128, n, :], ACT.Copy).then_inc(hi.sem, 1)
                    elif what == "ga":
                        act.wait_ge(*vg_ok.at(b, NT // 2))
                        nc.scalar.activation(gt[:, 1], gt[:, 0], ACT.Relu).then_inc(relu.sem, 1)
                    elif what == "e1":
                        act.wait_ge(*gate_v.at(b, 4))
                        nc.scalar.activation(z[:, 1], z[:, 11], ACT.Exp).then_inc(gate_a.sem, 1)
                    elif what == "e2":
                        act.wait_ge(*gate_v.at(b, 7))
                        nc.scalar.activation(z[:, 3], z[:, 2], ACT.Exp).then_inc(gate_a.sem, 1)
                    if in_ring(key) and EMPTIER[key[:2]] == "act":
                        ins.then_inc(emptied[st, "act"].sem, 1)

            act.wait_ge(w_in, 32)
            passes(act, run)

        @block.vector
        def _(dve):
            def tiles(ap):
                return ap.unsqueeze(1).to_broadcast([P, NT, ap.shape[-1]])

            def moments(b, n, src):
                for t in range(NT):
                    nc.vector.bn_stats(stats[:, n, t, :], src[:, t, :]).then_inc(stat[n].sem, 1)
                dve.wait_ge(*stat[n].at(b, NT))
                nc.vector.memset(begun[:, n:n + 1], 0.0).then_inc(stat[n].sem, 1)
                for t in range(NT):
                    nc.vector.bn_aggr(mv[:, n, t, :], stats[:, n, t:t + 1, :]).then_inc(stat[n].sem, 1)

            def normalise(n, dst, src):
                for t in range(NT):
                    last = nc.vector.tensor_scalar(dst[:, t, :], src[:, t, :], mv[:, n, t, 0:1], rs[:, n, t:t + 1],
                                                   ALU.subtract, ALU.mult)
                last.then_inc(normed[n].sem, 1)

            def gate(b, part):
                def step(k, ins):
                    ins.then_inc(gate_v.sem, 1)
                    if k not in (4, 7, 16):
                        dve.wait_ge(*gate_v.at(b, k))
                def over(ap):
                    return ap.unsqueeze(2).to_broadcast([P, NT, E])
                if part == "g1":
                    dve.wait_ge(*gate_p.at(b, E))
                    step(1, nc.vector.tensor_reduce(z[:, 0].rearrange("p t e -> p e t"), gm[:, :, :, :], AX.X, ALU.add))
                    step(2, nc.vector.tensor_tensor(z[:, 7], z[:, 0], tiles(R[:, R_BG2:R_BG2 + E]), ALU.add))
                    step(3, nc.vector.tensor_reduce(zs[:, 0], z[:, 7], AX.X, ALU.max))
                    step(4, nc.vector.tensor_tensor(z[:, 11], z[:, 7], over(zs[:, 0]), ALU.subtract))
                elif part == "g2":
                    dve.wait_ge(*gate_a.at(b, 1))
                    step(5, nc.vector.tensor_reduce(zs[:, 1], z[:, 1], AX.X, ALU.add))
                    step(6, nc.vector.reciprocal(zs[:, 2], zs[:, 1]))
                    step(7, nc.vector.tensor_tensor(z[:, 2], z[:, 1], over(zs[:, 2]), ALU.mult))
                else:
                    dve.wait_ge(*gate_v.at(b, 7))
                    q = [z[:, 2, :, e] for e in range(E)]
                    c = [zs[:, 3 + n] for n in range(5)]
                    nc.vector.tensor_tensor(c[0], q[0], q[1], ALU.is_lt)
                    nc.vector.tensor_tensor(c[1], q[0], q[2], ALU.is_lt)
                    nc.vector.tensor_tensor(c[2], q[1], q[0], ALU.is_le)
                    nc.vector.tensor_tensor(c[3], q[1], q[2], ALU.is_lt)
                    step(8, nc.vector.tensor_tensor(c[4], q[2], q[0], ALU.is_le))
                    nc.vector.tensor_tensor(z[:, 4, :, 0], c[0], c[1], ALU.mult)
                    nc.vector.tensor_tensor(z[:, 4, :, 1], c[2], c[3], ALU.mult)
                    step(9, nc.vector.tensor_tensor(z[:, 5, :, 0], q[2], q[1], ALU.is_le))
                    step(10, nc.vector.tensor_tensor(z[:, 4, :, 2], c[4], z[:, 5, :, 0], ALU.mult))
                    step(11, nc.vector.tensor_scalar(z[:, 6], z[:, 4], -1.0, 1.0, ALU.mult, ALU.add))
                    dve.wait_ge(*gate_a.at(b, 2))
                    step(12, nc.vector.tensor_tensor(z[:, 8], z[:, 3], z[:, 6], ALU.mult))
                    step(13, nc.vector.tensor_reduce(zs[:, 0], z[:, 8], AX.X, ALU.add))
                    step(14, nc.vector.reciprocal(zs[:, 1], zs[:, 0]))
                    step(15, nc.vector.tensor_tensor(z[:, 10], z[:, 8], over(zs[:, 1]), ALU.mult))
                    step(16, nc.vector.tensor_copy(z[:, 9, :, 0], zs[:, 0]))

            def constant_parts(k):
                if k == 0:
                    nc.vector.memset(m3[:, :, :], 0.0).then_inc(zeroed, 1)
                    nc.vector.memset(mf[:, :, :], 0.0).then_inc(zeroed, 1)
                elif k == 1:
                    nc.vector.memset(va_[:, :, :, :], 0.0).then_inc(zeroed, 1)
                elif k == 2:
                    nc.vector.memset(qb[HD:KH, :, :].bitcast(F32), 0.0).then_inc(zeroed, 1)
                elif k == 3:
                    nc.vector.memset(kb[HD:KH, :, :].bitcast(F32), 0.0).then_inc(zeroed, 1)
                elif k == 5:
                    dve.wait_ge(zeroed, 5)
                    nc.vector.memset(kb[HD:HD + 2, :, :].bitcast(F32), -1.0).then_inc(zeroed, 1)
                    nc.vector.memset(va_[:, :, :, DH:DH + 1], 1.0).then_inc(zeroed, 1)
                    nc.vector.memset(v2[:, :, :, HD:HD + 1], 1.0).then_inc(zeroed, 1)

            def run(p, before):
                def pair(key, w):
                    return ring(p, key)[0:P, :].rearrange("p (o c) -> p o c", o=2)[:, :, 0:w]

                for key in p.order:
                    st, what = key[:2]
                    b = p.b[st]
                    n = key[2] if len(key) > 2 else None
                    if p.first and what in ("xg", "zg"):
                        constant_parts(2 * n + (what == "zg"))
                    if in_ring(key) and EMPTIER[key[:2]] == "dve":
                        dve.wait_ge(*filled_at(p, key))
                    if what == "pad":
                        dve.wait_ge(*emptied_at(p, ("M", "xt", NK - 1)))
                        nc.vector.memset(xe[:, :, 0:1], 0.0)
                        nc.vector.memset(xe[:, :, T + 1:T + TAPS - 1], 0.0).then_inc(padded.sem, 1)
                    elif st == "M" and what == "cv":
                        if key[3] == 0:
                            dve.wait_ge(*emptied_at(p, ("M", "xe", n)))
                        dve.wait_ge(*padded.at(b, 1))
                        k = key[3]
                        w = C_CONV + (TAPS + 1) * n
                        if k == 0:
                            nc.vector.tensor_scalar(cv[:, n, :], xe[:, n, 0:T], Cc[:, w:w + 1],
                                                    Cc[:, w + TAPS:w + TAPS + 1], ALU.mult, ALU.add
                                                    ).then_inc(tap.sem, 1)
                        else:
                            dve.wait_ge(*tap.at(b, TAPS * n + k))
                            nc.vector.scalar_tensor_tensor(cv[:, n, :], xe[:, n, k:k + T], Cc[:, w + k:w + k + 1],
                                                           cv[:, n, :], ALU.mult, ALU.add).then_inc(tap.sem, 1)
                    elif what == "h":
                        dve.wait_ge(*tanhs.at(b, n + 1))
                        nc.vector.scalar_tensor_tensor(cv[:, n, :], tg[:, n % 2, :], 1.0, cv[:, n, :],
                                                       ALU.add, ALU.mult).then_inc(mixed.sem, 1)
                    elif what in ("xg", "zg"):
                        o = what == "zg"
                        dve.wait_ge(*tanhs.at(b, MI + 2 * n + o + 1))
                        if o and n >= 2:
                            dve.wait_ge(*gated.at(b, n - 1))
                        ins = nc.vector.scalar_tensor_tensor(sg[:, n % 2, :] if o else gT[:, n, 0:T], tg[:, o, :], 1.0,
                                                             ring(p, key)[:, C0:C0 + T], ALU.add, ALU.mult)
                    elif what == "m0":
                        if p.first:
                            dve.wait_ge(w_all, 48)
                            dve.wait_ge(zeroed, 8)
                        dve.wait_ge(*emptied_at(p, ("M", "y", NT // 2 - 1)))
                        moments(b, 0, y)
                    elif what == "n0":
                        dve.wait_ge(*stat[0].at(b, NSTAT))
                        for t in range(NT):
                            last = nc.vector.scalar_tensor_tensor(t1[:, t, :], y[:, t, :], mv[:, 0, t, 0:1],
                                                                  R[:, R_GAMMA:R_GAMMA + D], ALU.subtract, ALU.mult)
                        last.then_inc(affine.sem, 1)
                        dve.wait_ge(*var[0].at(b, 4))
                        dve.wait_ge(*affine.at(b, 1))
                        if "A" in p.stages:
                            dve.wait_ge(*h0b_ok.at(p.b["A"], 1))
                        for t in range(NT):
                            last = nc.vector.scalar_tensor_tensor(h0[:, t, :], t1[:, t, :], rs[:, 0, t:t + 1],
                                                                  R[:, R_BETA:R_BETA + D], ALU.mult, ALU.add)
                        last.then_inc(affine.sem, 1)
                    elif what == "m1":
                        dve.wait_ge(*affine.at(b, 2))
                        moments(b, 1, h0)
                    elif what == "n1":
                        dve.wait_ge(*var[1].at(b, 2))
                        normalise(1, hn, h0)
                    elif what == "sp":
                        k = key[3]
                        whole, part, rest = f[:, n % 2, :], parts[:, n % 2], fr[:, :]
                        if k == 0:
                            dve.wait_ge(*emptied_at(p, ("M", "qk", n)))
                            if n >= 2:
                                dve.wait_ge(*stack_w[n - 2].at(b, 48))
                            nc.vector.tensor_copy(part[:, 0, :], whole).then_inc(split.sem, 1)
                        else:
                            dve.wait_ge(*split.at(b, 4 * n + k))
                            if k == 1:
                                nc.vector.tensor_tensor(rest, whole, part[:, 0, :], ALU.subtract).then_inc(split.sem, 1)
                            elif k == 2:
                                nc.vector.tensor_copy(part[:, 1, :], rest).then_inc(split.sem, 1)
                            else:
                                nc.vector.tensor_tensor(part[:, 2, :], rest, part[:, 1, :], ALU.subtract
                                                        ).then_inc(split.sem, 1)
                    elif what == "v":
                        if n == 0 and "A" in p.stages:
                            dve.wait_ge(*pv_done["A"].at(p.b["A"], NG * NT))
                        for o in range(2):
                            ins = nc.vector.tensor_tensor(
                                va_[:, 2 * n + o, :, 0:DH],
                                ring(p, key)[0:P, 512 * o:512 * o + D].rearrange("p (h c) -> p h c", c=DH),
                                R[:, R_BV:R_BV + D].rearrange("p (h c) -> p h c", c=DH), ALU.add)
                    elif what == "s1":
                        i, h = key[3:]
                        z0 = P * (i + 1)
                        if st == "F":
                            z0 += z0 % 2
                            ins = nc.vector.tensor_reduce(mf[:, n % 2, i:i + 1], ring(p, key)[0:P, C0:C0 + z0],
                                                          AX.X, ALU.max)
                        elif HEADS[what][i] == 1:
                            c = NT * h + i
                            ins = nc.vector.tensor_reduce(m3[:, n % 2, c:c + 1], ring(p, key)[0:P, C0:C0 + z0],
                                                          AX.X, ALU.max)
                        else:
                            heads = HEADS[what][i]
                            ins = nc.vector.tensor_reduce(
                                m3[:, n % 2, 0:HG * NT].rearrange("p (h t) -> p h t", t=NT)[:, h:h + heads, i],
                                ring(p, key)[0:P, :].rearrange("p (h c) -> p h c", h=heads)[:, :, 0:z0], AX.X, ALU.max)
                    elif what == "mt":
                        if st != "F":
                            if n:
                                dve.wait_ge(*mrow_w[n - 1].at(b, 16))
                            elif "A" in p.stages:
                                dve.wait_ge(*mrow_w[NG - 1].at(p.b["A"], 16))
                            ins = nc.vector.tensor_copy(mrow[:, :], ring(p, key)[0:MPARTS * HG * NT, C0:C0 + P])
                        else:
                            if n:
                                dve.wait_ge(*mfrow_w[n - 1].at(b, 16))
                            ins = nc.vector.tensor_copy(mfrow[:, :], ring(p, key)[0:2 * NT, C0:C0 + P])
                    elif what == "yt" and st == "A":
                        d = ring(p, key)
                        banks = [d[0:P, 512 * o:512 * o + 384].rearrange("p (t h c) -> p t h c", t=3, c=VS)
                                 for o in range(2)]
                        for o in range(2):
                            last = nc.vector.reciprocal(rl[:, 3 * o:3 * o + 3, :], banks[o][:, :, :, DH])
                        last.then_inc(rl_a.sem, 1)
                        dve.wait_ge(*rl_a.at(b, n + 1))
                        for o in range(2):
                            ins = nc.vector.tensor_tensor(
                                yna[:, 3 * o:3 * o + 3, D // NG * n:D // NG * (n + 1)].rearrange(
                                    "p t (h c) -> p t h c", c=DH),
                                banks[o][:, :, :, 0:DH],
                                rl[:, 3 * o:3 * o + 3, :].unsqueeze(3).to_broadcast([P, 3, HG, DH]), ALU.mult)
                    elif what == "yt":
                        d = ring(p, key)
                        banks = [d[0:P, 512 * o:512 * o + 384].rearrange("p (t c) -> p t c", t=3) for o in range(2)]
                        for o in range(2):
                            last = nc.vector.reciprocal(wl[:, 0, 3 * o:3 * o + 3], banks[o][:, :, HD])
                        last.then_inc(rl_f.sem, 1)
                        dve.wait_ge(*rl_f.at(b, 2 * n + 1))
                        nc.vector.tensor_tensor(wl[:, 1, :], wl[:, 0, :], z[:, 10, :, n], ALU.mult
                                                ).then_inc(rl_f.sem, 1)
                        dve.wait_ge(*rl_f.at(b, 2 * n + 2))
                        for o in range(2):
                            ins = nc.vector.tensor_tensor(
                                ynf[:, 3 * o:3 * o + 3, HD * n:HD * (n + 1)], banks[o][:, :, 0:HD],
                                wl[:, 1, 3 * o:3 * o + 3].unsqueeze(2).to_broadcast([P, 3, HD]), ALU.mult)
                    elif what == "p":
                        if n == 0:
                            dve.wait_ge(*h0b_ok.at(b, 1))
                            if "F" in p.stages:
                                dve.wait_ge(*emptied_at(p, F_END))
                        ins = nc.vector.tensor_tensor(h1[:, 2 * n:2 * n + 2, :], pair(key, D), h0b[:, 2 * n:2 * n + 2, :],
                                                      ALU.add)
                    elif what == "mo":
                        dve.wait_ge(*emptied[("A", "dve")].at(b, EMPTY_AT[A_END]))
                        moments(b, 2, h1)
                    elif what == "no":
                        nc.vector.memset(f0[:, 0:1], 0.0)
                        nc.vector.memset(f0[:, T:T + 2], 0.0).then_inc(padded_f.sem, 1)
                        dve.wait_ge(*var[2].at(b, 2))
                        normalise(2, hn2, h1)
                    elif what == "cv":
                        q, w = ff[0:HD, 0, :], Cc[0:HD, C_FC:C_FC + 4]
                        if n == 0:
                            dve.wait_ge(*emptied_at(p, ("F", "fq", 0)))
                            dve.wait_ge(*padded_f.at(b, 1))
                            nc.vector.tensor_scalar(q, f0[:, 0:T], w[:, 0:1], w[:, 3:4], ALU.mult, ALU.add
                                                    ).then_inc(fconv.sem, 1)
                        else:
                            dve.wait_ge(*fconv.at(b, n))
                            nc.vector.scalar_tensor_tensor(q, f0[:, n:n + T], w[:, n:n + 1], q, ALU.mult, ALU.add
                                                           ).then_inc(fconv.sem, 1)
                    elif what == "lo":
                        if key[3] == 0:
                            dve.wait_ge(*hi.at(b, SPLIT_AT[n]))
                            nc.vector.tensor_copy(qb[0:HD, n, :], ff[0:HD, n, :])
                        elif key[3] == 1:
                            nc.vector.tensor_tensor(qa[HD:128, n, :], ff[0:HD, n, :], qa[0:HD, n, :], ALU.subtract)
                        else:
                            nc.vector.tensor_tensor(kb[0:HD, n, :], ff[HD:128, n, :], ka[HD:128, n, :], ALU.subtract
                                                    ).then_inc(lo.sem, 1)
                    elif what == "vg":
                        nc.vector.tensor_tensor(gt[:, 0, 2 * n:2 * n + 2, :], pair(key, D + GH)[:, :, D:D + GH],
                                                R[:, R_BG1:R_BG1 + GH].unsqueeze(1).to_broadcast([P, 2, GH]), ALU.add
                                                ).then_inc(vg_ok.sem, 1)
                        for o in range(2):
                            ins = nc.vector.tensor_tensor(
                                v2[:, 2 * n + o, :, 0:HD],
                                ring(p, key)[0:P, 512 * o:512 * o + D].rearrange("p (h c) -> p h c", c=HD),
                                R[:, R_BV2:R_BV2 + D].rearrange("p (h c) -> p h c", c=HD), ALU.add)
                    elif what in ("g1", "g2", "g3"):
                        gate(b, what)
                    elif what == "p2":
                        if n == 0:
                            dve.wait_ge(*h1b_ok.at(b, 1))
                            if "M" in p.stages:
                                dve.wait_ge(*filled_at(p, ("M", "xt", NK - 1)))
                            else:
                                dve.wait_ge(*stored.at(b, 0))
                        ins = nc.vector.tensor_tensor(xin[:, 2 * n:2 * n + 2, :], pair(key, D), h1[:, 2 * n:2 * n + 2, :],
                                                      ALU.add)
                    if in_ring(key) and EMPTIER[key[:2]] == "dve":
                        ins.then_inc(emptied[st, "dve"].sem, 1)
                    if what == "s1" and st != "F" and key == steps(st, "s1", n)[-1]:
                        dve.wait_ge(*emptied_at(p, key))
                        c = HG * NT
                        nc.vector.tensor_copy(mb[:, :], m3[:, n % 2, 0:c]).then_inc(msplit.sem, 1)
                        dve.wait_ge(*msplit.at(b, 2 * n + 1))
                        nc.vector.tensor_tensor(m3[:, n % 2, c:2 * c], m3[:, n % 2, 0:c], mb[:, :], ALU.subtract
                                                ).then_inc(msplit.sem, 1)
                    elif what == "s1" and st == "F" and key[3] == NT - 1:
                        dve.wait_ge(*emptied_at(p, key))
                        nc.vector.tensor_copy(mfr[:, :], mf[:, n % 2, 0:NT]).then_inc(mfsplit.sem, 1)
                        dve.wait_ge(*mfsplit.at(b, 2 * n + 1))
                        nc.vector.tensor_tensor(mf[:, n % 2, NT:2 * NT], mf[:, n % 2, 0:NT], mfr[:, :], ALU.subtract
                                                ).then_inc(mfsplit.sem, 1)

            nc.vector.memset(begun[:, :], 0.0).then_inc(stored.sem, 32)
            dve.wait_ge(w_in, 32)
            passes(dve, run)

        @block.gpsimd
        def _(pool):
            def select(dst, base, step, channel, fill, op=ALU.is_ge):
                nc.gpsimd.affine_select(out=dst, in_=dst, compare_op=op, fill=fill, base=base,
                                        pattern=[[step, dst.shape[-1]]], channel_multiplier=channel
                                        ).then_inc(consts, 1)

            def tiles(ap):
                return ap.unsqueeze(1).to_broadcast([P, NT, ap.shape[-1]])

            def run(p, before):
                for key in p.order:
                    st, what = key[:2]
                    b = p.b[st]
                    if what == "b0":
                        if "A" in before.stages:
                            pool.wait_ge(*emptied_at(before, A_END))
                        pool.wait_ge(*affine.at(b, 2))
                        nc.gpsimd.tensor_tensor(h0b[:, :, :], h0[:, :, :], tiles(R[:, R_BPROJ:R_BPROJ + D]), ALU.add
                                                ).then_inc(h0b_ok.sem, 1)
                    elif what == "g":
                        n = key[2]
                        pool.wait_ge(*emptied_at(p, ("M", "zg", n)))
                        nc.gpsimd.tensor_tensor(gT[:, n, 0:T], gT[:, n, 0:T], sg[:, n % 2, :], ALU.mult
                                                ).then_inc(gated.sem, 1)
                    elif what == "r0":
                        pool.wait_ge(*stat[0].at(b, NSTAT))
                        nc.gpsimd.tensor_tensor(va[:, 0, :], mv[:, 0, :, 1], expo[:, 3, :], ALU.mult
                                                ).then_inc(var[0].sem, 1)
                        pool.wait_ge(*var[0].at(b, 1))
                        nc.gpsimd.tensor_tensor(sd[:, :], va[:, 0, :], expo[:, 1, :], ALU.pow).then_inc(var[0].sem, 1)
                        pool.wait_ge(*var[0].at(b, 2))
                        nc.gpsimd.tensor_tensor(sde[:, :], sd[:, :], expo[:, 4, :], ALU.add).then_inc(var[0].sem, 1)
                        pool.wait_ge(*var[0].at(b, 3))
                        nc.gpsimd.tensor_tensor(rs[:, 0, :], sde[:, :], expo[:, 2, :], ALU.pow).then_inc(var[0].sem, 1)
                    elif what in ("r1", "rs"):
                        n = 1 if what == "r1" else 2
                        pool.wait_ge(*stat[n].at(b, NSTAT))
                        nc.gpsimd.tensor_tensor(va[:, n, :], mv[:, n, :, 1], expo[:, 5, :], ALU.add
                                                ).then_inc(var[n].sem, 1)
                        pool.wait_ge(*var[n].at(b, 1))
                        nc.gpsimd.tensor_tensor(rs[:, n, :], va[:, n, :], expo[:, 0, :], ALU.pow
                                                ).then_inc(var[n].sem, 1)
                    elif what == "bo":
                        pool.wait_ge(*normed[2].at(b, 1))
                        nc.gpsimd.tensor_tensor(h1[:, :, :], h1[:, :, :], tiles(R[:, R_BP:R_BP + D]), ALU.add
                                                ).then_inc(h1b_ok.sem, 1)
                    elif what == "gp":
                        pool.wait_ge(*relu.at(b, 1))
                        for e in range(E):
                            nc.gpsimd.tensor_tensor(gm[:, e], gt[:, 1], tiles(R[:, R_WG2 + GH * e:R_WG2 + GH * (e + 1)]),
                                                    ALU.mult).then_inc(gate_p.sem, 1)

            nc.gpsimd.memset(idf[:, :], 0.0).then_inc(made, 1)
            pool.wait_ge(made, 1)
            select(idf[:, :], 0, -1, 1, 1.0, ALU.not_equal)
            for t in (idb, mask_q, mask_k):
                nc.gpsimd.memset(t[:, :], 0.0).then_inc(made, 1)
            for n, v in enumerate(CONSTS):
                nc.gpsimd.memset(expo[:, n, :], v).then_inc(made, 1)
            pool.wait_ge(made, N_MADE)
            select(idb[:, :], 0, -1, 1, 1.0, ALU.not_equal)
            select(mask_q[:, :], 0, -1, 1, NEG)
            select(mask_k[:, :], -1, 1, -1, NEG)
            pool.wait_ge(consts, N_CONSTS - 1)
            nc.gpsimd.memset(ks[STACK:STACK + MPARTS, :, :, :], -1.0).then_inc(consts, 1)
            pool.wait_ge(consts, N_CONSTS)
            passes(pool, run)


def kernel(x, **w):
    import numpy as np
    import concourse.bacc as bacc
    from concourse.bass_utils import run_bass_kernel_spmd

    w = {k[3:]: np.asarray(v) for k, v in w.items()}
    x = np.ascontiguousarray(x)

    def contract(mats, n, p):
        a = np.concatenate(mats, axis=1)
        return np.ascontiguousarray(a.reshape(n, p, -1).transpose(1, 0, 2))

    wqk, bqk = w["ffn_Wqk"], w["ffn_bqk"]
    both = [wqk[:, HD * n:HD * (n + 1)] for e in range(E) for n in (e, E + e)]
    qk = np.arange(2 * D).reshape(2 * NK, HT, DH).transpose(0, 2, 1).reshape(-1)
    w96 = contract([w["tok_W_in"].T, w["attn_w_attn"][qk].T, w["attn_w_attn"][2 * D:].T, w["attn_w_proj"].T, *both,
                    *w["ffn_Wv"], w["ffn_Wg1"], w["ffn_Wp"]], NK, KH)
    w128 = contract([w["tok_W_x"].T, w["tok_W_z"].T, w["tok_W_out"].T], MI, 128)
    cols = np.zeros((128, COLS), np.float32)
    conv = np.concatenate([w["tok_conv_w"][:, 0, :], w["tok_conv_b"][:, None]], axis=1)
    cols[:, C_CONV:C_QK] = conv.reshape(MI, 128, TAPS + 1).transpose(1, 0, 2).reshape(128, -1)
    cols[:KH, C_QK:C_FQK] = w["attn_b_attn"][qk].reshape(2 * NK, KH).T
    cols[:, C_FQK:C_FC] = bqk.reshape(2, E, HD).transpose(0, 2, 1).reshape(128, E)
    cols[:HD, C_FC:C_FC + 3] = w["ffn_conv_w"][:, 0, :]
    cols[:HD, C_FC + 3] = w["ffn_conv_b"]
    row = np.concatenate([w["tok_gamma"], w["tok_beta"], w["attn_b_attn"][2 * D:], w["attn_b_proj"],
                          w["ffn_bv"].reshape(-1), w["ffn_bg1"], w["ffn_bp"],
                          w["ffn_Wg2"].T.reshape(-1), w["ffn_bg2"]])
    rows = np.ascontiguousarray(np.broadcast_to(row, (P, ROWS)))

    nc = bacc.Bacc("TRN2", target_bir_lowering=False, num_devices=1)
    arrays = {"x_dram": x, "w96_dram": w96, "w128_dram": w128, "cols_dram": cols, "rows_dram": rows}
    aps = [nc.dram_tensor(n, a.shape, mybir.dt.from_np(a.dtype), kind="ExternalInput").ap()
           for n, a in arrays.items()]
    out = nc.dram_tensor("out_dram", (B, T - 1, D), F32, kind="ExternalOutput").ap()
    audio_tower(nc, *aps, out)
    r = run_bass_kernel_spmd(nc, [arrays], core_ids=[0])
    return r.results[0]["out_dram"]
```
